# Optimizing a Trainium2 kernel written in Bass

```python
import numpy as np
import jax
import jax.numpy as jnp

def _softmax(x, axis=-1):
    return jax.nn.softmax(x, axis=axis)

def _gelu(x):
    return jax.nn.gelu(x, approximate=True)

def _silu(x):
    return jax.nn.silu(x)

def _sigmoid(x):
    return jax.nn.sigmoid(x)

def _layernorm(x, axis=-1, eps=1e-05):
    m = jnp.mean(x, axis=axis, keepdims=True)
    v = jnp.var(x, axis=axis, keepdims=True)
    return (x - m) / jnp.sqrt(v + eps)

def _scatter_add(tgt, idx, src, axis=0):
    return tgt.at[idx].add(src)

def _segment_sum(src, seg, n):
    return jax.ops.segment_sum(src, seg, n)
kernel_name = 'mk_gps_d1_gnn_r8_0f00c7'

def setup_inputs(seed: int=0):
    np.random.seed(seed)
    _w = jnp.asarray

    def _rec_inputs():
        import jax
        import jax.numpy as jnp
        _gk = jax.random.key(seed)
        x = -8.776e-05 + 1 * jax.random.normal(jax.random.fold_in(_gk, 1), (1250, 512), jnp.float32)
        src = jax.random.randint(jax.random.fold_in(_gk, 2), (20000,), 0, 1250, jnp.int32)
        dst = jnp.minimum((1250 * jax.random.uniform(jax.random.fold_in(_gk, 3), (20000,)) ** 2.0).astype(jnp.int32), 9999)
        _o = jnp.argsort(dst, stable=True)
        src = src[_o]
        dst = dst[_o]
        return (x, src, dst)
    x, src, dst = _rec_inputs()

    def _L0_gnn_setup():
        import jax, jax.numpy as jnp
        import numpy as np
        N_NODES = 1250
        N_EDGES = 20000
        D_IN = 512
        D_OUT = 512
        key = jax.random.key(seed)
        k1, k2, k3 = jax.random.split(key, 3)
        x = jax.random.normal(k1, (N_NODES, D_IN), dtype=jnp.float32)
        W = jax.random.normal(k2, (D_IN, D_OUT), dtype=jnp.float32) * (1.0 / np.sqrt(D_IN))
        b = jnp.zeros((D_OUT,), dtype=jnp.float32)
        edge_index = jax.random.randint(k3, (2, N_EDGES), 0, N_NODES, dtype=jnp.int32)
        return {'x': x, 'W': W, 'b': b, 'edge_index': edge_index}
    _L0_gnn_all = _L0_gnn_setup()
    _L0_gnn_in = {k: v for k, v in _L0_gnn_all.items() if k in ('W', 'b')}
    del _L0_gnn_all

    def _L0_mix_setup():
        import jax, jax.numpy as jnp
        import numpy as np
        DIM = 512
        HEADS = 8
        HEAD_DIM = DIM // HEADS
        key = jax.random.key(seed)
        ks = jax.random.split(key, 9)
        B, T, C = (8, 1024, DIM)
        s = 1.0 / np.sqrt(C)
        x = jax.random.normal(ks[0], (B, T, C), dtype=jnp.float32)
        Wq = jax.random.uniform(ks[1], (C, C), jnp.float32, -s, s)
        bq = jax.random.uniform(ks[2], (C,), jnp.float32, -s, s)
        Wk = jax.random.uniform(ks[3], (C, C), jnp.float32, -s, s)
        bk = jax.random.uniform(ks[4], (C,), jnp.float32, -s, s)
        Wv = jax.random.uniform(ks[5], (C, C), jnp.float32, -s, s)
        bv = jax.random.uniform(ks[6], (C,), jnp.float32, -s, s)
        Wo = jax.random.uniform(ks[7], (C, C), jnp.float32, -s, s)
        bo = jax.random.uniform(ks[8], (C,), jnp.float32, -s, s)
        return {'x': x, 'Wq': Wq, 'bq': bq, 'Wk': Wk, 'bk': bk, 'Wv': Wv, 'bv': bv, 'Wo': Wo, 'bo': bo}
    _L0_mix_all = _L0_mix_setup()
    _L0_mix_in = {k: v for k, v in _L0_mix_all.items() if k in ('Wq', 'bq', 'Wk', 'bk', 'Wv', 'bv', 'Wo', 'bo')}
    del _L0_mix_all

    def _L0_ffn_setup():
        import jax, jax.numpy as jnp
        import numpy as np
        E, TOPK, H, DK, DV, D = (4, 2, 8, 64, 64, 512)
        B, L = (4, 1024)
        VDIM = H * DV

        def _silu(x):
            return x * jax.nn.sigmoid(x)

        def _l2norm(x):
            return x * jax.lax.rsqrt(jnp.sum(x * x, axis=-1, keepdims=True) + 1e-06)

        def _forward(h, Wq, Wgate, Wk, Wv, Wb, Wa, A_log, dt_bias, Wg, o_norm_weight, Wo):
            Bs, Ls, _ = h.shape
            scores = jax.nn.softmax((h @ Wgate).astype(jnp.float32), axis=-1)
            rw, sel = jax.lax.top_k(scores, TOPK)
            rw = rw / jnp.sum(rw, axis=-1, keepdims=True)
            bi = jnp.arange(Bs)[:, None, None]
            li = jnp.arange(Ls)[None, :, None]
            w_full = jnp.zeros((Bs, Ls, E), jnp.float32).at[bi, li, sel].set(rw)
            m = jnp.transpose(w_full > 0, (2, 0, 1))
            q = _l2norm(_silu(h @ Wq).reshape(Bs, Ls, H, DK))
            k = _l2norm(_silu(h @ Wk).reshape(Bs, Ls, H, DK))
            v = _silu(h @ Wv).reshape(Bs, Ls, H, DV)
            beta = jax.nn.sigmoid(h @ Wb)
            g = -jnp.exp(A_log) * jax.nn.softplus((h @ Wa).astype(jnp.float32) + dt_bias)
            beta_e = beta[None] * m[..., None]
            g_e = jnp.where(m[..., None], g[None], 0.0)
            scale = DK ** (-0.5)
            xs = (jnp.moveaxis(q, 1, 0), jnp.moveaxis(k, 1, 0), jnp.moveaxis(v, 1, 0), jnp.moveaxis(beta_e, 2, 0), jnp.moveaxis(g_e, 2, 0))

            def step(S, x):
                qt, kt, vt, bt, gt = x
                S = S * jnp.exp(gt)[..., None, None]
                kv = jnp.einsum('bhk,ebhkv->ebhv', kt, S)
                delta = (vt[None] - kv) * bt[..., None]
                S = S + kt[None, :, :, :, None] * delta[..., None, :]
                ot = jnp.einsum('bhk,ebhkv->ebhv', qt * scale, S)
                return (S, ot)
            S0 = jnp.zeros((E, Bs, H, DK, DV), jnp.float32)
            _, o = jax.lax.scan(step, S0, xs)
            o = jnp.moveaxis(o, 0, 2)
            core = jnp.einsum('ble,eblhv->blhv', w_full, o)
            gate = _silu((h @ Wg).reshape(Bs, Ls, H, DV))
            core = core * jax.lax.rsqrt(jnp.mean(core * core, axis=-1, keepdims=True) + 1e-05)
            core = core * o_norm_weight * gate
            return core.reshape(Bs, Ls, VDIM) @ Wo
        key = jax.random.key(seed)
        ks = jax.random.split(key, 12)
        std = 0.02
        h = jax.random.normal(ks[0], (B, L, D), jnp.float32)
        Wq = jax.random.normal(ks[1], (D, H * DK), jnp.float32) * std
        Wgate = jax.random.normal(ks[2], (D, E), jnp.float32) * std
        Wk = jax.random.normal(ks[3], (D, H * DK), jnp.float32) * std
        Wv = jax.random.normal(ks[4], (D, VDIM), jnp.float32) * std
        Wb = jax.random.normal(ks[5], (D, H), jnp.float32) * std
        Wa = jax.random.normal(ks[6], (D, H), jnp.float32) * std
        Wg = jax.random.normal(ks[7], (D, VDIM), jnp.float32) * std
        Wo = jax.random.normal(ks[8], (VDIM, D), jnp.float32) * std
        A = jax.random.uniform(ks[9], (H,), jnp.float32, 0.0001, 16.0)
        A_log = jnp.log(A)
        dt = jnp.exp(jax.random.uniform(ks[10], (H,), jnp.float32) * (np.float32(np.log(0.1)) - np.float32(np.log(0.001))) + np.float32(np.log(0.001)))
        dt = jnp.maximum(dt, 0.0001)
        dt_bias = dt + jnp.log(-jnp.expm1(-dt))
        o_norm_weight = jnp.ones((DV,), jnp.float32)
        return {'hidden_states': h, 'Wq': Wq, 'Wgate': Wgate, 'Wk': Wk, 'Wv': Wv, 'Wb': Wb, 'Wa': Wa, 'A_log': A_log, 'dt_bias': dt_bias, 'Wg': Wg, 'o_norm_weight': o_norm_weight, 'Wo': Wo}
    _L0_ffn_all = _L0_ffn_setup()
    _L0_ffn_in = {k: v for k, v in _L0_ffn_all.items() if k in ('Wq', 'Wgate', 'Wk', 'Wv', 'Wb', 'Wa', 'A_log', 'dt_bias', 'Wg', 'o_norm_weight', 'Wo')}
    del _L0_ffn_all
    return {'x': x, 'src': src, 'dst': dst, 'L0_gnn_W': _L0_gnn_in['W'], 'L0_gnn_b': _L0_gnn_in['b'], 'L0_mix_Wq': _L0_mix_in['Wq'], 'L0_mix_bq': _L0_mix_in['bq'], 'L0_mix_Wk': _L0_mix_in['Wk'], 'L0_mix_bk': _L0_mix_in['bk'], 'L0_mix_Wv': _L0_mix_in['Wv'], 'L0_mix_bv': _L0_mix_in['bv'], 'L0_mix_Wo': _L0_mix_in['Wo'], 'L0_mix_bo': _L0_mix_in['bo'], 'L0_ffn_Wq': _L0_ffn_in['Wq'], 'L0_ffn_Wgate': _L0_ffn_in['Wgate'], 'L0_ffn_Wk': _L0_ffn_in['Wk'], 'L0_ffn_Wv': _L0_ffn_in['Wv'], 'L0_ffn_Wb': _L0_ffn_in['Wb'], 'L0_ffn_Wa': _L0_ffn_in['Wa'], 'L0_ffn_A_log': _L0_ffn_in['A_log'], 'L0_ffn_dt_bias': _L0_ffn_in['dt_bias'], 'L0_ffn_Wg': _L0_ffn_in['Wg'], 'L0_ffn_o_norm_weight': _L0_ffn_in['o_norm_weight'], 'L0_ffn_Wo': _L0_ffn_in['Wo']}

def reference(x, src, dst, L0_gnn_W, L0_gnn_b, L0_mix_Wq, L0_mix_bq, L0_mix_Wk, L0_mix_bk, L0_mix_Wv, L0_mix_bv, L0_mix_Wo, L0_mix_bo, L0_ffn_Wq, L0_ffn_Wgate, L0_ffn_Wk, L0_ffn_Wv, L0_ffn_Wb, L0_ffn_Wa, L0_ffn_A_log, L0_ffn_dt_bias, L0_ffn_Wg, L0_ffn_o_norm_weight, L0_ffn_Wo):
    import jax
    import jax.numpy as jnp

    def _L0_gnn_ref(x, W, b, edge_index):
        import jax, jax.numpy as jnp
        import numpy as np
        N_NODES = 1250
        N_EDGES = 20000
        D_IN = 512
        D_OUT = 512
        N = x.shape[0]
        self_loops = jnp.arange(N, dtype=edge_index.dtype)
        src = jnp.concatenate([edge_index[0], self_loops])
        dst = jnp.concatenate([edge_index[1], self_loops])
        ones = jnp.ones(src.shape[0], dtype=x.dtype)
        deg = jax.ops.segment_sum(ones, dst, num_segments=N)
        dinv_sqrt = jnp.where(deg > 0, jax.lax.rsqrt(deg), 0.0)
        norm = dinv_sqrt[src] * dinv_sqrt[dst]
        h = x @ W
        msgs = h[src] * norm[:, None]
        agg = jax.ops.segment_sum(msgs, dst, num_segments=N)
        return jax.nn.relu(agg + b)

    def _L0_mix_ref(x, Wq, bq, Wk, bk, Wv, bv, Wo, bo):
        import jax, jax.numpy as jnp
        import numpy as np
        DIM = 512
        HEADS = 8
        HEAD_DIM = DIM // HEADS
        B, T, C = x.shape
        H, D = (HEADS, HEAD_DIM)

        def proj(W, b):
            return (x @ W.T + b).reshape(B, T, H, D).transpose(0, 2, 1, 3)
        Q = proj(Wq, bq)
        K = proj(Wk, bk)
        V = proj(Wv, bv)
        Q = jax.nn.elu(Q) + 1.0
        K = jax.nn.elu(K) + 1.0
        KV = jnp.einsum('bhnd,bhne->bhde', K, V)
        Q_KV = jnp.einsum('bhnd,bhde->bhne', Q, KV)
        K_sum = K.sum(axis=2)
        normalizer = jnp.einsum('bhnd,bhd->bhn', Q, K_sum)
        out = Q_KV / (normalizer[..., None] + 1e-06)
        out = out.transpose(0, 2, 1, 3).reshape(B, T, C)
        out = out @ Wo.T + bo
        return out

    def _L0_ffn_ref(hidden_states, Wq, Wgate, Wk, Wv, Wb, Wa, A_log, dt_bias, Wg, o_norm_weight, Wo):
        import jax, jax.numpy as jnp
        import numpy as np
        E, TOPK, H, DK, DV, D = (4, 2, 8, 64, 64, 512)
        B, L = (4, 1024)
        VDIM = H * DV

        def _silu(x):
            return x * jax.nn.sigmoid(x)

        def _l2norm(x):
            return x * jax.lax.rsqrt(jnp.sum(x * x, axis=-1, keepdims=True) + 1e-06)

        def _forward(h, Wq, Wgate, Wk, Wv, Wb, Wa, A_log, dt_bias, Wg, o_norm_weight, Wo):
            Bs, Ls, _ = h.shape
            scores = jax.nn.softmax((h @ Wgate).astype(jnp.float32), axis=-1)
            rw, sel = jax.lax.top_k(scores, TOPK)
            rw = rw / jnp.sum(rw, axis=-1, keepdims=True)
            bi = jnp.arange(Bs)[:, None, None]
            li = jnp.arange(Ls)[None, :, None]
            w_full = jnp.zeros((Bs, Ls, E), jnp.float32).at[bi, li, sel].set(rw)
            m = jnp.transpose(w_full > 0, (2, 0, 1))
            q = _l2norm(_silu(h @ Wq).reshape(Bs, Ls, H, DK))
            k = _l2norm(_silu(h @ Wk).reshape(Bs, Ls, H, DK))
            v = _silu(h @ Wv).reshape(Bs, Ls, H, DV)
            beta = jax.nn.sigmoid(h @ Wb)
            g = -jnp.exp(A_log) * jax.nn.softplus((h @ Wa).astype(jnp.float32) + dt_bias)
            beta_e = beta[None] * m[..., None]
            g_e = jnp.where(m[..., None], g[None], 0.0)
            scale = DK ** (-0.5)
            xs = (jnp.moveaxis(q, 1, 0), jnp.moveaxis(k, 1, 0), jnp.moveaxis(v, 1, 0), jnp.moveaxis(beta_e, 2, 0), jnp.moveaxis(g_e, 2, 0))

            def step(S, x):
                qt, kt, vt, bt, gt = x
                S = S * jnp.exp(gt)[..., None, None]
                kv = jnp.einsum('bhk,ebhkv->ebhv', kt, S)
                delta = (vt[None] - kv) * bt[..., None]
                S = S + kt[None, :, :, :, None] * delta[..., None, :]
                ot = jnp.einsum('bhk,ebhkv->ebhv', qt * scale, S)
                return (S, ot)
            S0 = jnp.zeros((E, Bs, H, DK, DV), jnp.float32)
            _, o = jax.lax.scan(step, S0, xs)
            o = jnp.moveaxis(o, 0, 2)
            core = jnp.einsum('ble,eblhv->blhv', w_full, o)
            gate = _silu((h @ Wg).reshape(Bs, Ls, H, DV))
            core = core * jax.lax.rsqrt(jnp.mean(core * core, axis=-1, keepdims=True) + 1e-05)
            core = core * o_norm_weight * gate
            return core.reshape(Bs, Ls, VDIM) @ Wo
        return _forward(hidden_states, Wq, Wgate, Wk, Wv, Wb, Wa, A_log, dt_bias, Wg, o_norm_weight, Wo)
    edge_index = jnp.stack([src, dst])
    xn = _layernorm(x, axis=-1)
    x = x + _L0_gnn_ref(xn, L0_gnn_W, L0_gnn_b, edge_index) + _L0_mix_ref(xn[None], L0_mix_Wq, L0_mix_bq, L0_mix_Wk, L0_mix_bk, L0_mix_Wv, L0_mix_bv, L0_mix_Wo, L0_mix_bo)[0]
    x = x + _L0_ffn_ref(_layernorm(x, axis=-1)[None], L0_ffn_Wq, L0_ffn_Wgate, L0_ffn_Wk, L0_ffn_Wv, L0_ffn_Wb, L0_ffn_Wa, L0_ffn_A_log, L0_ffn_dt_bias, L0_ffn_Wg, L0_ffn_o_norm_weight, L0_ffn_Wo)[0]
    return x

_drawn_inputs = setup_inputs


def setup_inputs(seed=0):
    import zlib

    import numpy as np

    out = dict(_drawn_inputs(seed))
    spreads = {'L0_gnn_b': (0.0, 0.1), 'L0_ffn_o_norm_weight': (1.0, 0.6)}
    factors = {'L0_mix_Wq': 8.0,
     'L0_mix_bq': 64.0,
     'L0_mix_Wk': 8.0,
     'L0_mix_bk': 64.0,
     'L0_mix_Wv': 6.147,
     'L0_mix_bv': 3.481,
     'L0_mix_Wo': 3.235,
     'L0_ffn_Wb': 3.529,
     'L0_ffn_Wa': 21.761,
     'L0_ffn_A_log': 2.704,
     'L0_ffn_dt_bias': 4.847}
    for name, (base, spread) in spreads.items():
        noise = np.random.default_rng([zlib.crc32(name.encode()), seed]).standard_normal(out[name].shape)
        drawn = base * np.exp(spread * noise) if base else spread * noise
        out[name] = jnp.asarray(drawn.astype(out[name].dtype))
    for name, factor in factors.items():
        out[name] = (out[name] * factor).astype(out[name].dtype)
    return out
```

```python
import concourse.bass as bass
from concourse import mybir
from contextlib import ExitStack
import numpy as np

N, D, H, DH = 1250, 512, 8, 64
P = 125
NT = N // P
KC = D // 128
NE = 20000
EPP = NE // P
E = 4
SLOTS = 2 * N
NCH = SLOTS // P
HH = H // 2
CW = HH * P
GP, GC = 5, 250
LEVELS = 7
QSEG = [(0, 418), (418, 416), (834, 416)]
G_FLOOR = -110.0


def consts():
    i = np.arange(P)
    row, col = i[:, None], i[None, :]
    parts = [row <= col, row > col, row < col]
    for lv in range(LEVELS):
        s = 1 << lv
        off = (row // (2 * s) == col // (2 * s)) & (row // s % 2 == 1) & (col // s % 2 == 0)
        parts.append((row == col).astype(np.float32) - off)
    off = (row // 2 == col // 2) & (row % 2 == 1) & (col % 2 == 0)
    parts.append(((row == col).astype(np.float32) - off).T)
    tri = np.concatenate([np.asarray(p, np.float32) for p in parts], axis=1)
    iota = np.tile(np.arange(N, dtype=np.float16), (P, 1))
    return {"ident": np.eye(128, dtype=np.float32), "tri": np.ascontiguousarray(tri), "iota": iota}


def gps_layer(nc, d, out):
    f32, i32, f16 = mybir.dt.float32, mybir.dt.int32, mybir.dt.float16
    ALU = mybir.AluOpType
    ACT = mybir.ActivationFunctionType
    AX = mybir.AxisListType.X
    ctx = ExitStack()
    with ctx:
        def sb(name, shape, dt=f32):
            return ctx.enter_context(nc.sbuf_tensor(name, shape, dt))

        def sem(name):
            return ctx.enter_context(nc.semaphore(name))

        qkv_slots = nc.dram_tensor("qkv_slots", [SLOTS, 3 * D], f32, kind="Internal").ap()
        gb_slots = nc.dram_tensor("gb_slots", [SLOTS, 2 * H], f32, kind="Internal").ap()
        o_slots = nc.dram_tensor("o_slots", [SLOTS, D], f32, kind="Internal").ap()

        x_all = sb("x_all", [P, NT, D])
        xT = sb("xT", [128, KC, N])
        big = sb("big", [128, NT * N])
        cnt = big[0:P, :].rearrange("p (t n) -> p t n", t=NT)
        qT = big[:, 0:KC * N].rearrange("p (k n) -> p k n", k=KC)
        hs = sb("hs", [P, NT, D])
        W = sb("W", [128, 5, KC, D])
        ident = sb("ident_sb", [128, 128])
        tri = sb("tri_sb", [P, (3 + LEVELS + 1) * P])
        iota = sb("iota_sb", [P, N], f16)
        ones = sb("ones", [128, 64])
        onesq = sb("onesq", [P, P])
        zeros16 = sb("zeros16", [P, 512], f16)
        phalf = sb("phalf", [P, 16 + 64])
        b_k, b_v, b_o = (big[0:P, KC * N + n * D:KC * N + (n + 1) * D] for n in range(3))
        b_g = sb("b_g", [P, D])
        b_q = sb("b_q", [128, KC])
        onorm = sb("onorm", [P, DH])
        alog = sb("alog", [P, H])
        dtb = sb("dtb", [P, H])
        wsm = sb("wsm", [128, KC, E + 2 * H])
        ei = sb("ei", [P, 2, EPP], i32)
        ef = sb("ef", [P, 2, EPP])
        stats = sb("stats", [P, NT, 6])
        mv = sb("mv", [P, NT, 2])
        rstd = sb("rstd", [P, NT])
        xn = sb("xn", [P, 2, D])
        tA = sb("tA", [128, 2, D])
        tB = sb("tB", [128, 2, D])
        tC = sb("tC", [128, 2, D])
        rows = sb("rows", [P, 2, 3 * D])
        kvbd = sb("kvbd", [128, KC, 128])
        ksbd = sb("ksbd", [128, KC, 2])
        den = sb("den", [P, 2, H])
        dinv = sb("dinv", [P, NT])
        deg = sb("deg", [P, NT])
        oh_s = rows[:, 0, 0:N].bitcast(f16).rearrange("p (u n) -> p u n", u=2)
        oh_d = rows[:, 1, 0:GC].bitcast(f16).rearrange("p (u n) -> p u n", u=2)
        LE, GT, LT = tri[:, 0:P], tri[:, P:2 * P], tri[:, 2 * P:3 * P]

        def level_mask(lv):
            return tri[:, (3 + lv) * P:(4 + lv) * P]

        mask1T = level_mask(LEVELS)
        lg = sb("lg", [P, NT, E + 2 * H])
        rt = big[0:P, 20 * CW:20 * CW + 10 * NT * H].rearrange("p (a t h) -> p a t h", a=10, t=NT)
        sc = sb("sc", [P, E, NT])
        rk = sb("rk", [P, E, NT])
        sel = sb("sel", [P, E, NT])
        pos = sb("pos", [P, E, NT])
        tots = sb("tots", [P, E * NT])
        offs = sb("offs", [P, E * NT])
        one40 = sb("one40", [P, E * NT])
        fst = sb("fst", [P, E, NT])
        t4 = sb("t4", [P, 4, E, NT])
        c_pos = sb("c_pos", [P, 2, NT])
        c_w = sb("c_w", [P, 2, NT])
        c_m = sb("c_m", [P, 2, NT])
        c_f = sb("c_f", [P, 2, NT])
        c_t = sb("c_t", [P, 2, NT])
        sp_t = sb("sp_t", [P, 4, NT])
        posi = sb("posi", [P, 2, NT], i32)
        gb = sb("gb", [P, NT, 2, 2 * H])
        nrm = sb("nrm", [P, 2, 2 * H])
        gbs = sb("gbs", [P, NCH, 2 * H])
        gs = sb("gs", [P, NCH, H])
        gam = sb("gam", [P, NCH, H])
        bet = sb("bet", [P, NCH, H])
        bdec = sb("bdec", [P, NCH, H])
        gtot = sb("gtot", [64, NCH, H])
        state = sb("state", [64, H, DH])
        ktile, qtile, vtile = rows[:, 0, 0:D], rows[:, 0, D:2 * D], rows[:, 0, 2 * D:3 * D]
        kdec = rows[:, 1, 0:D]
        zt = rows[:, 1, D:2 * D]
        ot = rows[:, 1, 2 * D:3 * D]
        sdec = sb("sdec", [64, H, DH])

        def cmat(n, half, parts=P):
            at = (n * 2 + half) * CW
            return big[0:parts, at:at + CW].rearrange("p (h i) -> p h i", h=HH)

        RG, BM, DT, AT, PT, TT, TM, MM = range(8)
        kT2 = big[0:64, 16 * CW:18 * CW].rearrange("p (h n) -> p h n", h=2)
        qT2 = big[0:64, 18 * CW:20 * CW].rearrange("p (h n) -> p h n", h=2)

        bank = ctx.enter_context(nc.psum_tensor("bank", [128, 8, 512], f32))

        S = {n: sem(n) for n in (
            "x_loaded", "consts_loaded", "edges_loaded", "bias_loaded", "small_loaded",
            "stats_done", "moments_done", "eps_added", "rstd_done", "xn_done", "xT_psum", "xT_done",
            "proj_psum", "proj_sum", "proj_neg", "proj_exp", "proj_done", "kv_psum", "kv_done",
            "kv_zero", "h_psum", "h_done", "att_psum", "den_done", "att_done", "attT_psum", "attT_done",
            "mix_psum", "mix_done", "mix_added", "ones_done", "zeros_done", "onehots_done",
            "onehots_used", "count_done", "loops_added", "deg_psum", "deg_done",
            "dinv_done", "hs_done", "agg_psum", "agg_sum", "agg_done",
            "logit_psum", "gate_step", "gate_exp", "pos_psum", "pos_ready",
            "f_psum", "f_act", "sq_done", "ss_done", "rn_done", "rows_done",
            "gb_loaded", "gb_ready", "decay_psum", "decay_exp", "scal_done", "state_zero", "phalf_done", "bdec_done",
            "k_loaded", "q_loaded", "v_loaded", "kdec_done", "sdec_done",
            "o_stored", "mixed", "f_ms", "f_rs", "f_gated", "fT_psum",
            "fT_done", "y_psum", "y_done", "ln_table", "vec_step", "gb_scattered", "pool_step")}
        W_loaded = [sem(f"W{i}_loaded") for i in range(5)]
        HS = {n: [sem(f"{n}{h}") for h in range(2)] for n in (
            "rg_built", "bm_built", "e_psum", "dt_done", "kT_psum", "kT_done", "qT_psum", "qT_done",
            "db_raw", "kk_psum", "kq_psum", "at_raw", "at_strict", "at_done", "pt_done", "a_psum", "tt1_done",
            "m_psum", "m_done", "t_psum", "tt_psum", "t_done", "tt_done", "ks_psum", "ks_dec", "y_ready",
            "og_done", "z_psum", "z_done", "o_psum", "s_psum", "o_done", "state_done")}
        scattered, gathered, out_stored = ([sem(f"{n}{b}") for b in range(2)] for n in ("scattered", "gathered", "out_stored"))
        block = ctx.enter_context(nc.Block())

        class Step:
            def __init__(self, eng, s):
                self.eng, self.s, self.n = eng, s, 0

            def __call__(self, ins):
                self.n += 1
                ins.then_inc(self.s, 1)
                self.eng.wait_ge(self.s, self.n)

        def tt3(ap):
            return ap.rearrange("p (h e) -> p h e", e=DH)

        def bc(ap, n):
            return ap.unsqueeze(2).broadcast_to([ap.shape[0], ap.shape[1], n])

        def bm(ap, n):
            return ap.unsqueeze(1).broadcast_to([ap.shape[0], n, ap.shape[1]])

        def chunk(ap, c, h):
            return ap[:, bass.ds(c, 1), h * HH:(h + 1) * HH].rearrange("p a h -> p (a h)")

        def half(ap, h):
            return ap[:, h * HH * DH:(h + 1) * HH * DH]

        def prior(eng, s, n):
            if not (isinstance(n, int) and n == 0):
                eng.wait_ge(s, n)

        def settled(eng):
            eng.wait_ge(S["ones_done"], 1)

        def norm_tile(pool, t):
            pool.wait_ge(S["f_ms"], t + 1)
            nc.gpsimd.tensor_tensor(nrm[:, t % 2, 0:H], nrm[:, t % 2, 0:H], phalf[:, 0:H], ALU.pow).then_inc(S["f_rs"], 1)

        def mix_out(dve, V, t):
            dve.wait_ge(S["mix_psum"], t + 1)
            V.tensor_tensor(x_all[:, t, :], bank[0:P, 6 + t % 2, :], x_all[:, t, :], ALU.add).then_inc(S["mix_done"], 1)
            dve.wait_ge(S["mix_done"], t + 1)
            V.tensor_tensor(x_all[:, t, :], x_all[:, t, :], b_o[:, :], ALU.add).then_inc(S["mix_added"], 1)

        def last_sum(dve, V, t):
            dve.wait_ge(S["y_psum"], t + 1)
            if t >= 2:
                dve.wait_ge(out_stored[t % 2], 16 * (t // 2))
            V.tensor_tensor(tC[0:P, t % 2, :], bank[0:P, 6 + t % 2, :], x_all[:, t, :], ALU.add).then_inc(S["y_done"], 1)

        @block.sync
        def _(sp):
            sp.dma_start(x_all[:, :, :], d["x"].rearrange("(t p) d -> p t d", p=P)).then_inc(S["x_loaded"], 16)
            sp.dma_start(ident[:, :], d["ident"]).then_inc(S["consts_loaded"], 16)
            sp.dma_start(tri[:, :], d["tri"]).then_inc(S["consts_loaded"], 16)
            sp.dma_start(iota[:, :], d["iota"]).then_inc(S["consts_loaded"], 16)
            for n, name in enumerate(("L0_mix_Wk", "L0_mix_Wv", "L0_mix_Wq", "L0_mix_Wo", "L0_gnn_W")):
                sp.dma_start(W[:, n], d[name].rearrange("(k p) n -> p k n", p=128)).then_inc(W_loaded[n], 16)
            for buf, name in ((b_k, "L0_mix_bk"), (b_v, "L0_mix_bv"), (b_o, "L0_mix_bo"), (b_g, "L0_gnn_b")):
                sp.dma_start(buf[:, :], d[name].partition_broadcast(P)).then_inc(S["bias_loaded"], 16)
            sp.dma_start(b_q[:, :], d["L0_mix_bq"]).then_inc(S["bias_loaded"], 16)
            for n, name in enumerate(("src", "dst")):
                sp.dma_start(ei[:, n, :], d[name].rearrange("(p j) -> p j", p=P)).then_inc(S["edges_loaded"], 16)
            sp.dma_start(onorm[:, :], d["L0_ffn_o_norm_weight"].partition_broadcast(P)).then_inc(S["small_loaded"], 16)
            sp.dma_start(alog[:, :], d["L0_ffn_A_log"].partition_broadcast(P)).then_inc(S["small_loaded"], 16)
            sp.dma_start(dtb[:, :], d["L0_ffn_dt_bias"].partition_broadcast(P)).then_inc(S["small_loaded"], 16)
            sp.dma_start(wsm[:, :, :], d["wsmall"].rearrange("(k p) n -> p k n", p=128)).then_inc(S["small_loaded"], 16)
            sp.wait_ge(S["h_psum"], 2 * NT)
            sp.wait_ge(S["mix_psum"], NT)
            for n, name in enumerate(("L0_ffn_Wq", "L0_ffn_Wk", "L0_ffn_Wv", "L0_ffn_Wg", "L0_ffn_Wo")):
                sp.dma_start(W[:, n], d[name].rearrange("(k p) n -> p k n", p=128)).then_inc(W_loaded[n], 16)
            sp.wait_ge(S["gb_scattered"], 16 * 2 * NT)
            sp.dma_start(gbs[:, :, :], gb_slots.rearrange("(c p) n -> p c n", p=P)).then_inc(S["gb_loaded"], 16)
            for b in range(2):
                sp.wait_ge(scattered[b], 16 * NT)
            sp.dma_start(ktile, qkv_slots[0:P, D:2 * D]).then_inc(S["k_loaded"], 16)
            sp.dma_start(qtile, qkv_slots[0:P, 0:D]).then_inc(S["q_loaded"], 16)
            sp.dma_start(vtile, qkv_slots[0:P, 2 * D:3 * D]).then_inc(S["v_loaded"], 16)
            with sp.Fori(1, NCH) as c:
                r0 = c * P
                for h in range(2):
                    prior(sp, HS["kT_psum"][h], c)
                    prior(sp, HS["qT_psum"][h], c)
                prior(sp, S["kdec_done"], c)
                sp.dma_start(ktile, qkv_slots[bass.ds(r0, P), D:2 * D]).then_inc(S["k_loaded"], 16)
                sp.dma_start(qtile, qkv_slots[bass.ds(r0, P), 0:D]).then_inc(S["q_loaded"], 16)
                for h in range(2):
                    prior(sp, HS["y_ready"][h], c)
                sp.dma_start(vtile, qkv_slots[bass.ds(r0, P), 2 * D:3 * D]).then_inc(S["v_loaded"], 16)
                for h in range(2):
                    prior(sp, HS["o_done"][h], c)
                sp.dma_start(o_slots[bass.ds(r0 - P, P), :], ot).then_inc(S["o_stored"], 16)
            for h in range(2):
                sp.wait_ge(HS["o_done"][h], NCH)
            sp.dma_start(o_slots[SLOTS - P:SLOTS, :], ot).then_inc(S["o_stored"], 16)
            for t in range(NT):
                sp.wait_ge(S["y_done"], t + 1)
                sp.dma_start(out[t * P:(t + 1) * P, :], tC[0:P, t % 2, :]).then_inc(out_stored[t % 2], 16)
            for b in range(2):
                sp.wait_ge(out_stored[b], 16 * NT // 2)
            sp.wait_ge(S["o_stored"], 16 * NCH)

        @block.tensor
        def _(pe):
            mm = nc.tensor.matmul
            pe.wait_ge(S["consts_loaded"], 48)
            pe.wait_ge(S["ones_done"], 1)

            def transpose_tiles(src, ready, base, psum_sem, done, banks, at=0):
                for t in range(NT):
                    pe.wait_ge(ready, base + t + 1)
                    if t >= 2 or at:
                        pe.wait_ge(done, at + t - 1)
                    for k in range(KC):
                        last = nc.tensor.transpose(bank[:, banks + t % 2, k * P:(k + 1) * P],
                                                   src(t)[:, k * 128:(k + 1) * 128], ident[0:P, 0:P])
                    last.then_inc(psum_sem, 1)

            def project(dst, t, w):
                for k in range(KC):
                    last = mm(dst, xT[:, k, t * P:(t + 1) * P], W[:, w, k, :], start=(k == 0), stop=(k == KC - 1))
                return last

            transpose_tiles(lambda t: xn[:, t % 2, :], S["xn_done"], 0, S["xT_psum"], S["xT_done"], 6)
            pe.wait_ge(S["xT_done"], NT)
            pe.wait_ge(W_loaded[0], 16)
            pe.wait_ge(W_loaded[1], 16)
            pe.wait_ge(S["zeros_done"], 1)
            mm(bank[:, 4, :], zeros16[:, 0:128], zeros16[:, :], start=True, stop=True)
            mm(bank[:, 5, :], zeros16[:, 0:128], zeros16[:, :], start=True, stop=True)
            unit = 0

            def kv_sums(t):
                pe.wait_ge(S["proj_done"], t + 1)
                pe.wait_ge(S["vec_step"], t + 1)
                for c in range(KC):
                    mm(bank[:, 4, c * 128:(c + 1) * 128], tC[0:P, t % 2, c * 128:(c + 1) * 128],
                       xn[:, t % 2, c * 128:(c + 1) * 128], start=False, stop=True, skip_group_check=True)
                for c in range(KC):
                    last = mm(bank[:, 5, c:c + 1], tC[0:P, t % 2, c * 128:(c + 1) * 128], ones[0:P, 0:1],
                              start=False, stop=True, skip_group_check=True)
                last.then_inc(S["kv_psum"], 1)

            for t in range(NT):
                if unit >= 2:
                    pe.wait_ge(S["proj_sum"], unit - 1)
                project(bank[0:P, unit % 2, :], t, 0).then_inc(S["proj_psum"], 1)
                if t >= 2:
                    pe.wait_ge(S["vec_step"], t - 1)
                project(bank[0:P, 2 + t % 2, :], t, 1).then_inc(S["h_psum"], 1)
                unit += 1
                if t >= 1:
                    kv_sums(t - 1)
            kv_sums(NT - 1)
            pe.wait_ge(W_loaded[2], 16)
            for c in range(KC):
                for s0, n in QSEG:
                    pe.wait_ge(S["proj_sum"], unit - 1)
                    for k in range(KC):
                        last = mm(bank[:, unit % 2, 0:n], W[:, 2, k, c * 128:(c + 1) * 128], xT[:, k, s0:s0 + n],
                                  start=(k == 0), stop=(k == KC - 1))
                    last.then_inc(S["proj_psum"], 1)
                    unit += 1
            pe.wait_ge(W_loaded[4], 16)
            for t in range(NT):
                if t < 2:
                    pe.wait_ge(S["vec_step"], NT)
                else:
                    pe.wait_ge(S["h_done"], t - 1)
                project(bank[0:P, 2 + t % 2, :], t, 4).then_inc(S["h_psum"], 1)
            pe.wait_ge(S["kv_done"], 4)
            pe.wait_ge(S["proj_done"], unit)
            pe.wait_ge(W_loaded[3], 16)
            for t in range(NT):
                b = t % 2
                if t >= 2:
                    pe.wait_ge(S["att_done"], t - 1)
                for c in range(KC):
                    mm(bank[0:P, b, c * 128:(c + 1) * 128], qT[:, c, t * P:(t + 1) * P], kvbd[:, c, :], start=True, stop=True)
                if t == 0:
                    pe.wait_ge(S["h_done"], NT)
                for c in range(KC):
                    last = mm(bank[0:P, 2 + b, 2 * c:2 * c + 2], qT[:, c, t * P:(t + 1) * P], ksbd[:, c, :], start=True, stop=True)
                last.then_inc(S["att_psum"], 1)
                pe.wait_ge(S["att_done"], t + 1)
                if t >= 2:
                    pe.wait_ge(S["attT_done"], t - 1)
                for k in range(KC):
                    last = nc.tensor.transpose(bank[:, 4 + b, k * P:(k + 1) * P], tA[0:P, b, k * 128:(k + 1) * 128], ident[0:P, 0:P])
                last.then_inc(S["attT_psum"], 1)
                pe.wait_ge(S["attT_done"], t + 1)
                if t >= 2:
                    pe.wait_ge(S["mix_done"], t - 1)
                for k in range(KC):
                    last = mm(bank[0:P, 6 + b, :], tB[:, b, k * P:(k + 1) * P], W[:, 3, k, :], start=(k == 0), stop=(k == KC - 1))
                last.then_inc(S["mix_psum"], 1)
            pe.wait_ge(S["mix_done"], NT)
            for q in range(GP):
                if q:
                    pe.wait_ge(S["count_done"], q)
                for b in range(5):
                    last = mm(bank[:, b, :], zeros16[:, 0:128], zeros16[:, :], start=True, stop=True)
                    if q == 0 and b < 2:
                        last.then_inc(S["onehots_used"], 1)
                with pe.Fori(0, EPP // 2) as i:
                    for u in range(2):
                        pe.wait_ge(S["onehots_done"], i * 4 + (q * EPP * 2 + 2 * u + 2))
                        for s in range(NT):
                            last = mm(bank[0:P, s // 2, s % 2 * 256:s % 2 * 256 + GC], oh_s[:, u, s * P:(s + 1) * P],
                                      oh_d[:, u, :], start=False, stop=True, skip_group_check=True)
                        last.then_inc(S["onehots_used"], 1)
            pe.wait_ge(S["loops_added"], NT)
            for t in range(NT):
                for s in range(NT):
                    last = mm(bank[0:P, 6, t:t + 1], cnt[:, s, t * P:(t + 1) * P], ones[0:P, 0:1], start=(s == 0), stop=(s == NT - 1))
            last.then_inc(S["deg_psum"], 1)
            pe.wait_ge(S["hs_done"], NT)
            for t in range(NT):
                if t >= 2:
                    pe.wait_ge(S["agg_sum"], t - 1)
                for s in range(NT):
                    last = mm(bank[0:P, t % 2, :], cnt[:, s, t * P:(t + 1) * P], hs[:, s, :], start=(s == 0), stop=(s == NT - 1))
                last.then_inc(S["agg_psum"], 1)
            transpose_tiles(lambda t: xn[:, t % 2, :], S["xn_done"], NT, S["xT_psum"], S["xT_done"], 6, at=NT)
            pe.wait_ge(S["xT_done"], 2 * NT)
            pe.wait_ge(S["small_loaded"], 64)
            pe.wait_ge(S["agg_sum"], NT)
            for t in range(NT):
                n = E + 2 * H
                for k in range(KC):
                    last = mm(bank[0:P, 0, t * n:(t + 1) * n], xT[:, k, t * P:(t + 1) * P], wsm[:, k, :],
                              start=(k == 0), stop=(k == KC - 1))
            last.then_inc(S["logit_psum"], 1)
            pe.wait_ge(S["gate_step"], 1)
            mm(bank[0:P, 1, 0:E * NT], LT, sel[:, :, :].rearrange("p e t -> p (e t)"), start=True, stop=True)
            mm(bank[0:P, 1, 64:64 + E * NT], onesq[:, :], sel[:, :, :].rearrange("p e t -> p (e t)"),
               start=True, stop=True).then_inc(S["pos_psum"], 1)
            for w in range(4):
                pe.wait_ge(W_loaded[w], 32)
            for t in range(NT):
                for w in range(4):
                    if t:
                        pe.wait_ge(S["f_act"], 4 * (t - 1) + w + 1)
                    project(bank[0:P, 2 + w, :], t, w).then_inc(S["f_psum"], 1)
            pe.wait_ge(S["gb_ready"], 1)
            g2 = gs[:, :, :].rearrange("p c h -> p (c h)")
            mm(bank[0:P, 6, 0:NCH * H], LE, g2, start=True, stop=True)
            mm(bank[0:P, 6, 160:160 + NCH * H], GT, g2, start=True, stop=True)
            mm(bank[0:64, 6, 320:320 + NCH * H], ones[0:P, 0:64], g2, start=True, stop=True).then_inc(S["decay_psum"], 1)
            pe.wait_ge(S["decay_exp"], 1)
            pe.wait_ge(S["f_act"], 4 * NT)
            pe.wait_ge(S["state_zero"], 1)
            def chunk_step(c):
                pe.wait_ge(S["k_loaded"], c * 16 + 16)
                pe.wait_ge(S["q_loaded"], c * 16 + 16)
                for h in range(2):
                    pe.wait_ge(HS["rg_built"][h], c + 1)
                    prior(pe, HS["z_done"][h], c)
                    mm(bank[0:P, h, 0:CW], GT, cmat(RG, h).rearrange("p h i -> p (h i)"), start=True, stop=True).then_inc(HS["e_psum"][h], 1)
                for h in range(2):
                    settled(pe)
                    prior(pe, HS["state_done"][h], c)
                    for j in range(HH):
                        last = nc.tensor.transpose(bank[0:64, 6 + h, j * P:(j + 1) * P],
                                                   ktile[:, (h * HH + j) * DH:(h * HH + j + 1) * DH], ident[0:P, 0:P])
                    last.then_inc(HS["kT_psum"][h], 1)
                for h in range(2):
                    settled(pe)
                    prior(pe, HS["o_done"][h], c)
                    for j in range(HH):
                        last = nc.tensor.transpose(bank[0:64, 2 + h, j * P:(j + 1) * P],
                                                   qtile[:, (h * HH + j) * DH:(h * HH + j + 1) * DH], ident[0:P, 0:P])
                    last.then_inc(HS["qT_psum"][h], 1)
                for h in range(2):
                    pe.wait_ge(HS["kT_done"][h], c + 1)
                    prior(pe, HS["og_done"][h], c)
                    for j in range(HH):
                        kj = kT2[:, h, j * P:(j + 1) * P]
                        last = mm(bank[0:P, 4 + h, j * P:(j + 1) * P], kj, kj, start=True, stop=True)
                    last.then_inc(HS["kk_psum"][h], 1)
                for h in range(2):
                    pe.wait_ge(HS["qT_done"][h], c + 1)
                    pe.wait_ge(HS["dt_done"][h], c + 1)
                    for j in range(HH):
                        last = mm(bank[0:P, h, j * P:(j + 1) * P], kT2[:, h, j * P:(j + 1) * P],
                                  qT2[:, h, j * P:(j + 1) * P], start=True, stop=True)
                    last.then_inc(HS["kq_psum"][h], 1)
                for h in range(2):
                    pe.wait_ge(HS["at_done"][h], c + 1)
                    for j in range(HH):
                        last = mm(bank[0:P, 2 + h, j * P:(j + 1) * P], cmat(AT, h)[:, j, :], ident[0:P, 0:P], start=True, stop=True)
                    last.then_inc(HS["a_psum"][h], 1)
                for lv in range(1, LEVELS):
                    for h in range(2):
                        if lv == 1:
                            pe.wait_ge(HS["m_done"][h], c * LEVELS + 1)
                        else:
                            pe.wait_ge(HS["t_done"][h], c * (LEVELS - 2) + (lv - 1))
                        for j in range(HH):
                            rhs = cmat(MM if lv == 1 else TM, h)[:, j, :]
                            last = mm(bank[0:P, 4 + h, j * P:(j + 1) * P], cmat(AT, h)[:, j, :], rhs, start=True, stop=True)
                        last.then_inc(HS["m_psum"][h], 1)
                    for h in range(2):
                        pe.wait_ge(HS["m_done"][h], c * LEVELS + (lv + 1))
                        if lv == 1:
                            pe.wait_ge(HS["tt1_done"][h], c + 1)
                            pe.wait_ge(HS["pt_done"][h], c + 1)
                        else:
                            pe.wait_ge(HS["tt_done"][h], c * (LEVELS - 1) + (lv - 1))
                        if lv < LEVELS - 1:
                            for j in range(HH):
                                last = mm(bank[0:P, h, j * P:(j + 1) * P], cmat(TT, h)[:, j, :], cmat(BM, h)[:, j, :], start=True, stop=True)
                            last.then_inc(HS["t_psum"][h], 1)
                        for j in range(HH):
                            last = mm(bank[0:P, 2 + h, j * P:(j + 1) * P], cmat(BM, h)[:, j, :], cmat(TT, h)[:, j, :], start=True, stop=True)
                        last.then_inc(HS["tt_psum"][h], 1)
                for h in range(2):
                    prior(pe, HS["state_done"][h], c)
                    for j in range(HH):
                        mm(bank[0:P, 4 + h, j * DH:(j + 1) * DH], kT2[:, h, j * P:(j + 1) * P], state[:, h * HH + j, :], start=True, stop=True)
                    for j in range(HH):
                        last = mm(bank[0:P, 4 + h, 256 + j * DH:256 + (j + 1) * DH], qT2[:, h, j * P:(j + 1) * P], state[:, h * HH + j, :], start=True, stop=True)
                    last.then_inc(HS["ks_psum"][h], 1)
                for h in range(2):
                    pe.wait_ge(HS["tt_done"][h], c * (LEVELS - 1) + (LEVELS - 1))
                    pe.wait_ge(HS["y_ready"][h], c + 1)
                    for j in range(HH):
                        last = mm(bank[0:P, h, j * DH:(j + 1) * DH], cmat(TT, h)[:, j, :], half(tA[0:P, 0, :], h)[:, j * DH:(j + 1) * DH], start=True, stop=True)
                    last.then_inc(HS["z_psum"][h], 1)
                pe.wait_ge(S["kdec_done"], c + 1)
                for h in range(2):
                    pe.wait_ge(HS["z_done"][h], c + 1)
                    for j in range(HH):
                        last = mm(bank[0:64, 6 + h, j * DH:(j + 1) * DH], half(kdec, h)[:, j * DH:(j + 1) * DH],
                                  half(zt, h)[:, j * DH:(j + 1) * DH], start=True, stop=True)
                    last.then_inc(HS["s_psum"][h], 1)
                    for j in range(HH):
                        last = mm(bank[0:P, 2 + h, j * DH:(j + 1) * DH], cmat(PT, h)[:, j, :],
                                  half(zt, h)[:, j * DH:(j + 1) * DH], start=True, stop=True)
                    last.then_inc(HS["o_psum"][h], 1)

            chunk_step(0)
            with pe.Fori(1, NCH) as c:
                chunk_step(c)
            for h in range(2):
                pe.wait_ge(HS["o_done"][h], NCH)
                pe.wait_ge(HS["state_done"][h], NCH)
                pe.wait_ge(HS["og_done"][h], NCH)
            pe.wait_ge(W_loaded[4], 32)
            for t in range(NT):
                b = t % 2
                pe.wait_ge(S["f_gated"], t + 1)
                if t >= 2:
                    pe.wait_ge(S["fT_done"], t - 1)
                for k in range(KC):
                    last = nc.tensor.transpose(bank[:, 4 + b, k * P:(k + 1) * P], tA[0:P, b, k * 128:(k + 1) * 128], ident[0:P, 0:P])
                last.then_inc(S["fT_psum"], 1)
                pe.wait_ge(S["fT_done"], t + 1)
                if t >= 2:
                    pe.wait_ge(S["y_done"], t - 1)
                for k in range(KC):
                    last = mm(bank[0:P, 6 + b, :], qT[:, b, k * P:(k + 1) * P], W[:, 4, k, :], start=(k == 0), stop=(k == KC - 1))
                last.then_inc(S["y_psum"], 1)

        @block.scalar
        def _(act):
            A = nc.scalar.activation

            def copy_tiles(at, base):
                for t in range(NT):
                    act.wait_ge(S["xT_psum"], base + t + 1)
                    A(xT[:, :, t * P:(t + 1) * P], bank[:, 6 + t % 2, 0:KC * P].rearrange("p (k n) -> p k n", k=KC),
                      ACT.Copy).then_inc(S["xT_done"], 1)

            copy_tiles(0, 0)
            for u in range(NT):
                act.wait_ge(S["proj_neg"], u + 1)
                A(tB[0:P, u % 2, :], tB[0:P, u % 2, :], ACT.Exp).then_inc(S["proj_exp"], 1)
            for u in range(NT, NT + KC * len(QSEG)):
                n = QSEG[(u - NT) % 3][1]
                act.wait_ge(S["proj_neg"], u + 1)
                A(tB[:, u % 2, 0:n], tB[:, u % 2, 0:n], ACT.Exp).then_inc(S["proj_exp"], 1)
            for t in range(NT):
                act.wait_ge(S["h_psum"], NT + t + 1)
                A(hs[:, t, :], bank[0:P, 2 + t % 2, :], ACT.Copy).then_inc(S["h_done"], 1)
            for t in range(NT):
                act.wait_ge(S["attT_psum"], t + 1)
                if t >= 2:
                    act.wait_ge(S["mix_psum"], t - 1)
                A(tB[:, t % 2, 0:KC * P], bank[:, 4 + t % 2, 0:KC * P], ACT.Copy).then_inc(S["attT_done"], 1)
            for q in range(GP):
                act.wait_ge(S["onehots_used"], 2 + (q + 1) * EPP)
                A(cnt[:, :, q * GC:(q + 1) * GC], bank[0:P, 0:5, :].rearrange("p b (s n) -> p (b s) n", s=2)[:, :, 0:GC],
                  ACT.Copy).then_inc(S["count_done"], 1)
            copy_tiles(NT, NT)
            act.wait_ge(S["gate_exp"], 1)
            A(rt[:, 0, :, 0:E], rt[:, 0, :, 0:E], ACT.Exp).then_inc(S["ln_table"], 1)
            A(rt[:, 1, :, :], rt[:, 1, :, :], ACT.Exp).then_inc(S["ln_table"], 1)
            A(rt[:, 2, :, :], rt[:, 2, :, :], ACT.Exp).then_inc(S["ln_table"], 1)
            A(rt[:, 9, 0, :], alog[:, :], ACT.Exp).then_inc(S["ln_table"], 1)
            act.wait_ge(S["gate_exp"], 2)
            A(rt[:, 4, :, :], rt[:, 3, :, :], ACT.Ln).then_inc(S["ln_table"], 1)
            for t in range(NT):
                for w in range(4):
                    act.wait_ge(S["f_psum"], 4 * t + w + 1)
                    if w == 0 and t >= 2:
                        act.wait_ge(scattered[t % 2], 32 * (t // 2))
                    dst = hs[:, t, :] if w == 3 else rows[:, t % 2, w * D:(w + 1) * D]
                    A(dst, bank[0:P, 2 + w, :], ACT.Silu).then_inc(S["f_act"], 1)
            act.wait_ge(S["decay_psum"], 1)
            g2 = lambda a: a[:, :, :].rearrange("p c h -> p (c h)")
            A(g2(gam), bank[0:P, 6, 0:NCH * H], ACT.Exp)
            A(g2(bdec), bank[0:P, 6, 160:160 + NCH * H], ACT.Exp)
            A(g2(gtot), bank[0:64, 6, 320:320 + NCH * H], ACT.Exp).then_inc(S["decay_exp"], 1)
            def chunk_step(c):
                for h in range(2):
                    act.wait_ge(HS["e_psum"][h], c + 1)
                    prior(act, HS["pt_done"][h], c)
                    A(cmat(DT, h).rearrange("p h i -> p (h i)"), bank[0:P, h, 0:CW], ACT.Exp).then_inc(HS["dt_done"][h], 1)
                for h in range(2):
                    act.wait_ge(HS["kT_psum"][h], c + 1)
                    prior(act, HS["ks_psum"][h], c)
                    A(kT2[:, h, :], bank[0:64, 6 + h, 0:CW], ACT.Copy).then_inc(HS["kT_done"][h], 1)
                for h in range(2):
                    act.wait_ge(HS["qT_psum"][h], c + 1)
                    A(qT2[:, h, :], bank[0:64, 2 + h, 0:CW], ACT.Copy).then_inc(HS["qT_done"][h], 1)
                for lv in range(1, LEVELS):
                    for h in range(2):
                        if lv < LEVELS - 1:
                            act.wait_ge(HS["t_psum"][h], c * (LEVELS - 2) + lv)
                            A(cmat(TM, h).rearrange("p h i -> p (h i)"), bank[0:P, h, 0:CW], ACT.Copy).then_inc(HS["t_done"][h], 1)
                        act.wait_ge(HS["tt_psum"][h], c * (LEVELS - 1) + lv)
                        A(cmat(TT, h).rearrange("p h i -> p (h i)"), bank[0:P, 2 + h, 0:CW], ACT.Copy).then_inc(HS["tt_done"][h], 1)
                for h in range(2):
                    act.wait_ge(HS["z_psum"][h], c + 1)
                    prior(act, HS["o_psum"][h], c)
                    A(half(zt, h), bank[0:P, h, 0:HH * DH], ACT.Copy).then_inc(HS["z_done"][h], 1)

            chunk_step(0)
            with act.Fori(1, NCH) as c:
                chunk_step(c)
            for t in range(NT):
                act.wait_ge(S["fT_psum"], t + 1)
                if t >= 2:
                    act.wait_ge(S["y_psum"], t - 1)
                A(qT[:, t % 2, 0:KC * P], bank[:, 4 + t % 2, 0:KC * P], ACT.Copy).then_inc(S["fT_done"], 1)

        @block.gpsimd
        def _(pool):
            G = nc.gpsimd
            G.memset(ones[:, :], 1.0)
            G.memset(onesq[:, :], 1.0)
            G.memset(one40[:, :], 1.0).then_inc(S["ones_done"], 1)
            G.memset(zeros16[:, :], 0.0).then_inc(S["zeros_done"], 1)
            G.memset(phalf[:, :], -0.5).then_inc(S["phalf_done"], 1)
            G.memset(kvbd[:, :, :], 0.0).then_inc(S["kv_zero"], 1)
            G.memset(ksbd[:, :, :], 0.0).then_inc(S["kv_zero"], 1)
            G.memset(state[:, :, :], 0.0).then_inc(S["state_zero"], 1)
            pool.wait_ge(S["phalf_done"], 1)

            def rstd_of(n):
                pool.wait_ge(S["eps_added"], n)
                G.tensor_tensor(rstd[:, :], mv[:, :, 1], phalf[:, 0:NT], ALU.pow).then_inc(S["rstd_done"], 1)

            rstd_of(1)
            for u in range(NT):
                pool.wait_ge(S["proj_sum"], u + 1)
                if u >= 2:
                    pool.wait_ge(S["proj_done"], u - 1)
                G.tensor_scalar(tB[0:P, u % 2, :], tA[0:P, u % 2, :], 0.0, None, ALU.min).then_inc(S["proj_neg"], 1)
            for u in range(NT, NT + KC * len(QSEG)):
                n = QSEG[(u - NT) % 3][1]
                pool.wait_ge(S["proj_sum"], u + 1)
                pool.wait_ge(S["proj_done"], u - 1)
                G.tensor_scalar(tB[:, u % 2, 0:n], tA[:, u % 2, 0:n], 0.0, None, ALU.min).then_inc(S["proj_neg"], 1)
            pool.wait_ge(S["count_done"], GP)
            for t in range(NT):
                v = cnt[:, t, t * P:(t + 1) * P]
                G.tensor_tensor(v, v, ident[0:P, 0:P], ALU.add).then_inc(S["loops_added"], 1)
            pool.wait_ge(S["deg_done"], 1)
            G.tensor_tensor(dinv[:, :], deg[:, :], phalf[:, 0:NT], ALU.pow).then_inc(S["dinv_done"], 1)
            rstd_of(2)
            pool.wait_ge(S["pos_ready"], 1)
            for t in range(NT):
                for c in range(2):
                    G.indirect_dma_start(gb_slots, bass.IndirectOffsetOnAxis(ap=posi[:, c, t:t + 1], axis=0),
                                         gb[:, t, c, :], None).then_inc(S["gb_scattered"], 16)
            for t in range(NT):
                pool.wait_ge(S["ss_done"], t + 1)
                G.tensor_tensor(nrm[:, t % 2, :], nrm[:, t % 2, :], phalf[:, 0:2 * H], ALU.pow).then_inc(S["rn_done"], 1)
                pool.wait_ge(S["rows_done"], t + 1)
                for c in range(2):
                    G.indirect_dma_start(qkv_slots, bass.IndirectOffsetOnAxis(ap=posi[:, c, t:t + 1], axis=0),
                                         rows[:, t % 2, :], None).then_inc(scattered[t % 2], 16)
            pool.wait_ge(S["scal_done"], 1)
            def chunk_step(c):
                for h in range(2):
                    prior(pool, HS["e_psum"][h], c)
                    G.tensor_tensor(cmat(RG, h), bc(chunk(gs, c, h), P), bm(LE, HH), ALU.mult).then_inc(HS["rg_built"][h], 1)
                    prior(pool, HS["tt_psum"][h], c * (LEVELS - 1))
                    G.tensor_tensor(cmat(BM, h), bc(chunk(bet, c, h), P), bm(LE, HH), ALU.mult).then_inc(HS["bm_built"][h], 1)
                pool.wait_ge(S["k_loaded"], c * 16 + 16)
                for h in range(2):
                    prior(pool, HS["s_psum"][h], c)
                G.tensor_tensor(tt3(kdec), tt3(ktile), bc(bdec[:, bass.ds(c, 1), :].rearrange("p a h -> p (a h)"), DH), ALU.mult).then_inc(S["kdec_done"], 1)
                for h in range(2):
                    pool.wait_ge(HS["at_raw"][h], c + 1)
                    G.tensor_tensor(cmat(AT, h), cmat(AT, h), bm(LT, HH), ALU.mult).then_inc(HS["at_strict"][h], 1)
                    pool.wait_ge(HS["at_strict"][h], c + 1)
                    G.tensor_tensor(cmat(AT, h), cmat(AT, h), bm(ident[0:P, 0:P], HH), ALU.add).then_inc(HS["at_done"][h], 1)
                    pool.wait_ge(HS["at_done"][h], c + 1)
                    prior(pool, HS["z_psum"][h], c)
                    G.tensor_tensor(cmat(TT, h), cmat(AT, h), bm(mask1T, HH), ALU.mult).then_inc(HS["tt1_done"][h], 1)
                for h in range(2):
                    prior(pool, HS["state_done"][h], c)
                hh = gtot[:, bass.ds(c, 1), :].rearrange("p a h -> p (a h)")
                G.tensor_tensor(sdec[:, :, :], state[:, :, :], bc(hh, DH), ALU.mult).then_inc(S["sdec_done"], 1)

            chunk_step(0)
            with pool.Fori(1, NCH) as c:
                chunk_step(c)
            pool.wait_ge(S["o_stored"], 16 * NCH)
            for t in range(NT):
                if t >= 2:
                    pool.wait_ge(S["mixed"], t - 1)
                for c in range(2):
                    G.indirect_dma_start(rows[:, t % 2, c * D:(c + 1) * D], None, o_slots,
                                         bass.IndirectOffsetOnAxis(ap=posi[:, c, t:t + 1], axis=0)).then_inc(gathered[t % 2], 16)
                if t >= 1:
                    norm_tile(pool, t - 1)
            norm_tile(pool, NT - 1)

        @block.vector
        def _(dve):
            V = nc.vector
            step = Step(dve, S["pool_step"])

            def layer_norm(n, psum_base):
                for t in range(NT):
                    if n:
                        dve.wait_ge(S["agg_done"], t + 1)
                    V.bn_stats(stats[:, t, :], x_all[:, t, :]).then_inc(S["stats_done"], 1)
                for t in range(NT):
                    dve.wait_ge(S["stats_done"], n * NT + t + 1)
                    V.bn_aggr(mv[:, t, :], stats[:, t, :]).then_inc(S["moments_done"], 1)
                dve.wait_ge(S["moments_done"], (n + 1) * NT)
                V.tensor_scalar(mv[:, :, 1], mv[:, :, 1], 1e-5, None, ALU.add).then_inc(S["eps_added"], 1)
                dve.wait_ge(S["rstd_done"], n + 1)
                for t in range(NT):
                    if t >= 2 or n:
                        dve.wait_ge(S["xT_psum"], n * NT + t - 1)
                    V.tensor_scalar(xn[:, t % 2, :], x_all[:, t, :], mv[:, t, 0:1], rstd[:, t:t + 1],
                                    ALU.subtract, ALU.mult).then_inc(S["xn_done"], 1)

            dve.wait_ge(S["x_loaded"], 16)
            layer_norm(0, 0)
            dve.wait_ge(S["bias_loaded"], 80)

            def finish(u, rowsn, n, dst):
                dve.wait_ge(S["proj_exp"], u + 1)
                V.scalar_tensor_tensor(dst, tA[0:rowsn, u % 2, 0:n], 0.0, tB[0:rowsn, u % 2, 0:n],
                                       ALU.max, ALU.add).then_inc(S["proj_done"], 1)

            for t in range(NT):
                dve.wait_ge(S["proj_psum"], t + 1)
                V.tensor_tensor(tA[0:P, t % 2, :], bank[0:P, t % 2, :], b_k[:, :], ALU.add).then_inc(S["proj_sum"], 1)
                dve.wait_ge(S["h_psum"], t + 1)
                if t >= 2:
                    dve.wait_ge(S["kv_psum"], t - 1)
                elif t == 0:
                    dve.wait_ge(S["xT_psum"], NT)
                V.tensor_tensor(xn[:, t % 2, :], bank[0:P, 2 + t % 2, :], b_v[:, :], ALU.add).then_inc(S["vec_step"], 1)
                finish(t, P, D, tC[0:P, t % 2, :])
            dve.wait_ge(S["kv_psum"], NT)
            dve.wait_ge(S["kv_zero"], 2)
            for a in range(2):
                q = slice(64 * a, 64 * a + 64)
                V.tensor_copy(kvbd[q, :, q], bank[q, 4, :].rearrange("p (c n) -> p c n", c=KC)[:, :, q]).then_inc(S["kv_done"], 1)
                V.tensor_copy(ksbd[q, :, a:a + 1], bank[q, 5, 0:KC].unsqueeze(2)).then_inc(S["kv_done"], 1)
            u = NT
            for c in range(KC):
                for s0, n in QSEG:
                    dve.wait_ge(S["proj_psum"], u + 1)
                    dve.wait_ge(S["proj_done"], u - 1)
                    V.tensor_scalar(tA[:, u % 2, 0:n], bank[:, u % 2, 0:n], b_q[:, c:c + 1], None, ALU.add).then_inc(S["proj_sum"], 1)
                    if u > NT:
                        finish(u - 1, 128, prev[1], prev[0])
                    prev = (qT[:, c, s0:s0 + n], n)
                    u += 1
            finish(u - 1, 128, prev[1], prev[0])
            for t in range(NT):
                b = t % 2
                dve.wait_ge(S["att_psum"], t + 1)
                V.tensor_scalar(den[:, b, :], bank[0:P, 2 + b, 0:H], 1e-6, None, ALU.add).then_inc(S["den_done"], 1)
                dve.wait_ge(S["den_done"], 2 * t + 1)
                V.reciprocal(den[:, b, :], den[:, b, :]).then_inc(S["den_done"], 1)
                dve.wait_ge(S["den_done"], 2 * t + 2)
                if t >= 2:
                    dve.wait_ge(S["attT_psum"], t - 1)
                elif t == 0:
                    dve.wait_ge(S["proj_done"], u)
                V.tensor_tensor(tt3(tA[0:P, b, :]), tt3(bank[0:P, b, :]), bc(den[:, b, :], DH), ALU.mult).then_inc(S["att_done"], 1)
                if t >= 1:
                    mix_out(dve, V, t - 1)
            mix_out(dve, V, NT - 1)
            dve.wait_ge(S["edges_loaded"], 32)
            dve.wait_ge(S["consts_loaded"], 48)
            step(V.tensor_copy(ef[:, :, :], ei[:, :, :]))
            for q in range(GP):
                with dve.Fori(0, EPP // 2) as i:
                    for w in range(2):
                        dve.wait_ge(S["onehots_used"], i * 2 + (q * EPP + w + 1))
                        V.tensor_scalar(oh_s[:, w, :], iota[:, :], ef[:, 0, bass.ds(i * 2 + w, 1)], None,
                                        ALU.is_equal).then_inc(S["onehots_done"], 1)
                        V.tensor_scalar(oh_d[:, w, :], iota[:, q * GC:(q + 1) * GC], ef[:, 1, bass.ds(i * 2 + w, 1)], None,
                                        ALU.is_equal).then_inc(S["onehots_done"], 1)
            dve.wait_ge(S["deg_psum"], 1)
            V.tensor_copy(deg[:, :], bank[0:P, 6, 0:NT]).then_inc(S["deg_done"], 1)
            dve.wait_ge(S["dinv_done"], 1)
            for t in range(NT):
                if t == 0:
                    dve.wait_ge(S["h_done"], NT)
                V.tensor_scalar(hs[:, t, :], hs[:, t, :], dinv[:, t:t + 1], None, ALU.mult).then_inc(S["hs_done"], 1)
            for t in range(NT):
                b = t % 2
                dve.wait_ge(S["agg_psum"], t + 1)
                V.scalar_tensor_tensor(tA[0:P, b, :], bank[0:P, b, :], dinv[:, t:t + 1], b_g[:, :],
                                       ALU.mult, ALU.add).then_inc(S["agg_sum"], 1)
                dve.wait_ge(S["agg_sum"], t + 1)
                V.scalar_tensor_tensor(x_all[:, t, :], tA[0:P, b, :], 0.0, x_all[:, t, :],
                                       ALU.max, ALU.add).then_inc(S["agg_done"], 1)
            layer_norm(1, 0)
            dve.wait_ge(S["logit_psum"], 1)
            step(V.tensor_copy(lg[:, :, :], bank[0:P, 0, 0:NT * 20].rearrange("p (t n) -> p t n", t=NT)))
            step(V.tensor_reduce(sp_t[:, 0, :], lg[:, :, 0:E], AX, ALU.max))
            step(V.tensor_tensor(rt[:, 0, :, 0:E], lg[:, :, 0:E], bc(sp_t[:, 0, :], E), ALU.subtract))
            step(V.tensor_scalar(rt[:, 1, :, :], lg[:, :, E:E + H], -1.0, None, ALU.mult))
            step(V.tensor_tensor(rt[:, 5, :, :], lg[:, :, E + H:E + 2 * H], bm(dtb[:, :], NT), ALU.add))
            step(V.tensor_scalar(rt[:, 6, :, :], rt[:, 5, :, :], -1.0, None, ALU.mult))
            V.tensor_tensor(rt[:, 2, :, :], rt[:, 5, :, :], rt[:, 6, :, :], ALU.min).then_inc(S["gate_exp"], 1)
            dve.wait_ge(S["ln_table"], 4)
            V.tensor_scalar(rt[:, 3, :, :], rt[:, 2, :, :], 1.0, None, ALU.add).then_inc(S["gate_exp"], 1)
            dve.wait_ge(S["gate_exp"], 2)
            step(V.tensor_scalar(rt[:, 6, :, :], rt[:, 3, :, :], -1.0, None, ALU.add))
            step(V.tensor_tensor(rt[:, 6, :, :], rt[:, 2, :, :], rt[:, 6, :, :], ALU.subtract))
            step(V.reciprocal(rt[:, 7, :, :], rt[:, 3, :, :]))
            step(V.tensor_tensor(rt[:, 6, :, :], rt[:, 6, :, :], rt[:, 7, :, :], ALU.mult))
            dve.wait_ge(S["ln_table"], 5)
            step(V.tensor_tensor(rt[:, 6, :, :], rt[:, 6, :, :], rt[:, 4, :, :], ALU.add))
            step(V.scalar_tensor_tensor(rt[:, 6, :, :], rt[:, 5, :, :], 0.0, rt[:, 6, :, :], ALU.max, ALU.add))
            step(V.tensor_tensor(rt[:, 6, :, :], rt[:, 6, :, :], bm(rt[:, 9, 0, :], NT), ALU.mult))
            step(V.tensor_scalar(rt[:, 6, :, :], rt[:, 6, :, :], -1.0, G_FLOOR, ALU.mult, ALU.max))
            step(V.tensor_scalar(rt[:, 1, :, :], rt[:, 1, :, :], 1.0, None, ALU.add))
            step(V.reciprocal(rt[:, 8, :, :], rt[:, 1, :, :]))
            step(V.tensor_reduce(sp_t[:, 1, :], rt[:, 0, :, 0:E], AX, ALU.add))
            step(V.reciprocal(sp_t[:, 2, :], sp_t[:, 1, :]))
            step(V.tensor_tensor(sc[:, :, :], rt[:, 0, :, 0:E].rearrange("p t e -> p e t"), bm(sp_t[:, 2, :], E), ALU.mult))
            step(V.memset(rk[:, :, :], 0.0))
            for a in range(E):
                for b in range(a + 1, E):
                    step(V.tensor_tensor(t4[:, 0, 0, :], sc[:, a, :], sc[:, b, :], ALU.is_ge))
                    step(V.tensor_tensor(rk[:, b, :], rk[:, b, :], t4[:, 0, 0, :], ALU.add))
                    step(V.scalar_tensor_tensor(rk[:, a, :], rk[:, a, :], 1.0, t4[:, 0, 0, :], ALU.add, ALU.subtract))
            V.tensor_scalar(sel[:, :, :], rk[:, :, :], 1.5, None, ALU.is_lt).then_inc(S["gate_step"], 1)
            dve.wait_ge(S["gate_step"], 1)
            dve.wait_ge(S["pos_psum"], 1)
            step(V.tensor_copy(tots[:, :], bank[0:P, 1, 64:64 + E * NT]))
            step(V.tensor_tensor_scan(offs[:, :], one40[:, :], tots[:, :], 0.0, ALU.mult, ALU.add))
            step(V.tensor_tensor(offs[:, :], offs[:, :], tots[:, :], ALU.subtract))
            pf = pos[:, :, :].rearrange("p e t -> p (e t)")
            step(V.tensor_tensor(pf, bank[0:P, 1, 0:E * NT], offs[:, :], ALU.add))
            of = offs[:, :].rearrange("p (e t) -> p e t", e=E)[:, :, 0:1].broadcast_to([P, E, NT])
            step(V.tensor_tensor(fst[:, :, :], pos[:, :, :], of, ALU.is_equal))
            for c in range(2):
                step(V.tensor_scalar(t4[:, 0], rk[:, :, :], float(c), None, ALU.is_equal))
                for dst, src in ((c_pos, pos), (c_w, sc), (c_f, fst)):
                    step(V.tensor_tensor(t4[:, 1], t4[:, 0], src[:, :, :], ALU.mult))
                    step(V.tensor_reduce(dst[:, c, :], t4[:, 1].rearrange("p e t -> p t e"), AX, ALU.add))
            step(V.tensor_copy(posi[:, :, :], c_pos[:, :, :]))
            step(V.tensor_tensor(sp_t[:, 3, :], c_w[:, 0, :], c_w[:, 1, :], ALU.add))
            step(V.reciprocal(sp_t[:, 3, :], sp_t[:, 3, :]))
            step(V.tensor_tensor(c_w[:, :, :], c_w[:, :, :], bm(sp_t[:, 3, :], 2), ALU.mult))
            step(V.tensor_scalar(c_m[:, :, :], c_w[:, :, :], 0.0, None, ALU.is_gt))
            step(V.tensor_scalar(c_f[:, :, :], c_f[:, :, :], G_FLOOR, None, ALU.mult))
            for c in range(2):
                step(V.tensor_tensor(gb[:, :, c, 0:H], rt[:, 6, :, :], bc(c_m[:, c, :], H), ALU.mult))
                step(V.tensor_tensor(gb[:, :, c, 0:H], gb[:, :, c, 0:H], bc(c_f[:, c, :], H), ALU.add))
                step(V.tensor_tensor(gb[:, :, c, H:2 * H], rt[:, 8, :, :], bc(c_m[:, c, :], H), ALU.mult))
            V.tensor_copy(c_t[:, :, :], c_w[:, :, :]).then_inc(S["pos_ready"], 1)
            for t in range(NT):
                b = t % 2
                dve.wait_ge(S["f_act"], 4 * t + 2)
                qk = rows[:, b, 0:2 * D]
                sq = qT[0:P, 0:2, 0:D]
                if t >= 1:
                    dve.wait_ge(S["ss_done"], t)
                V.tensor_tensor(sq, qk.rearrange("p (a n) -> p a n", a=2), qk.rearrange("p (a n) -> p a n", a=2), ALU.mult).then_inc(S["sq_done"], 1)
                dve.wait_ge(S["sq_done"], 2 * t + 1)
                V.tensor_reduce(nrm[:, b, :].rearrange("p (a h) -> p a h", a=2), sq.rearrange("p a (h e) -> p a h e", e=DH), AX, ALU.add).then_inc(S["sq_done"], 1)
                dve.wait_ge(S["sq_done"], 2 * t + 2)
                V.tensor_scalar(nrm[:, b, :], nrm[:, b, :], 1e-6, None, ALU.add).then_inc(S["ss_done"], 1)
                dve.wait_ge(S["rn_done"], t + 1)
                V.scalar_tensor_tensor(tt3(qk[:, 0:D]), tt3(qk[:, 0:D]), DH ** -0.5, bc(nrm[:, b, 0:H], DH), ALU.mult, ALU.mult)
                dve.wait_ge(S["f_act"], 4 * t + 3)
                V.tensor_tensor(tt3(qk[:, D:2 * D]), tt3(qk[:, D:2 * D]), bc(nrm[:, b, H:2 * H], DH), ALU.mult).then_inc(S["rows_done"], 1)
            dve.wait_ge(S["gb_loaded"], 16)
            step(V.tensor_copy(gs[:, :, :], gbs[:, :, 0:H]))
            V.tensor_copy(bet[:, :, :], gbs[:, :, H:2 * H]).then_inc(S["gb_ready"], 1)
            dve.wait_ge(S["gb_ready"], 1)
            dve.wait_ge(S["decay_exp"], 1)
            V.tensor_tensor(bdec[:, :, :], bdec[:, :, :], bet[:, :, :], ALU.mult).then_inc(S["scal_done"], 1)
            def chunk_step(c):
                for h in range(2):
                    dve.wait_ge(HS["dt_done"][h], c + 1)
                    dve.wait_ge(HS["bm_built"][h], c + 1)
                    V.tensor_tensor(cmat(DT, h), cmat(DT, h), cmat(BM, h), ALU.mult).then_inc(HS["db_raw"][h], 1)
                for h in range(2):
                    dve.wait_ge(HS["db_raw"][h], c + 1)
                    dve.wait_ge(HS["kk_psum"][h], c + 1)
                    V.tensor_tensor(cmat(AT, h), bank[0:P, 4 + h, 0:CW].rearrange("p (h i) -> p h i", h=HH), cmat(DT, h), ALU.mult).then_inc(HS["at_raw"][h], 1)
                for h in range(2):
                    dve.wait_ge(HS["kq_psum"][h], c + 1)
                    prior(dve, HS["o_psum"][h], c)
                    V.tensor_tensor(cmat(PT, h), bank[0:P, h, 0:CW].rearrange("p (h i) -> p h i", h=HH), cmat(DT, h), ALU.mult).then_inc(HS["pt_done"][h], 1)
                for h in range(2):
                    dve.wait_ge(HS["a_psum"][h], c + 1)
                    V.tensor_tensor(cmat(MM, h), bank[0:P, 2 + h, 0:CW].rearrange("p (h i) -> p h i", h=HH), bm(level_mask(0), HH), ALU.mult).then_inc(HS["m_done"][h], 1)
                for lv in range(1, LEVELS):
                    for h in range(2):
                        dve.wait_ge(HS["m_psum"][h], c * (LEVELS - 1) + lv)
                        V.tensor_tensor(cmat(BM, h), bank[0:P, 4 + h, 0:CW].rearrange("p (h i) -> p h i", h=HH), bm(level_mask(lv), HH), ALU.mult).then_inc(HS["m_done"][h], 1)
                dve.wait_ge(S["v_loaded"], c * 16 + 16)
                for h in range(2):
                    gh = chunk(gam, c, h)
                    dve.wait_ge(HS["ks_psum"][h], c + 1)
                    prior(dve, HS["z_psum"][h], c)
                    y = half(tA[0:P, 0, :], h)
                    V.tensor_tensor(tt3(y), tt3(bank[0:P, 4 + h, 0:256]), bc(gh, DH), ALU.mult).then_inc(HS["ks_dec"][h], 1)
                    dve.wait_ge(HS["ks_dec"][h], c + 1)
                    V.tensor_tensor(y, half(vtile, h), y, ALU.subtract).then_inc(HS["y_ready"][h], 1)
                    og = half(tB[0:P, 0, :], h)
                    V.tensor_tensor(tt3(og), tt3(bank[0:P, 4 + h, 256:512]), bc(gh, DH), ALU.mult).then_inc(HS["og_done"][h], 1)
                dve.wait_ge(S["sdec_done"], c + 1)
                prior(dve, S["o_stored"], c * 16)
                for h in range(2):
                    dve.wait_ge(HS["s_psum"][h], c + 1)
                    V.tensor_tensor(state[:, h * HH:(h + 1) * HH, :], tt3(bank[0:64, 6 + h, 0:256]), sdec[:, h * HH:(h + 1) * HH, :], ALU.add).then_inc(HS["state_done"][h], 1)
                    dve.wait_ge(HS["o_psum"][h], c + 1)
                    dve.wait_ge(HS["og_done"][h], c + 1)
                    V.tensor_tensor(half(ot, h), bank[0:P, 2 + h, 0:256], half(tB[0:P, 0, :], h), ALU.add).then_inc(HS["o_done"][h], 1)

            chunk_step(0)
            with dve.Fori(1, NCH) as c:
                chunk_step(c)
            for t in range(NT):
                b = t % 2
                dve.wait_ge(gathered[t % 2], 32 * (t // 2 + 1))
                r0, r1 = rows[:, b, 0:D], rows[:, b, D:2 * D]
                step(V.tensor_scalar(r0, r0, c_t[:, 0, t:t + 1], None, ALU.mult))
                if t >= 2:
                    dve.wait_ge(S["fT_psum"], t - 1)
                V.scalar_tensor_tensor(tA[0:P, b, :], r1, c_t[:, 1, t:t + 1], r0, ALU.mult, ALU.add).then_inc(S["mixed"], 1)
                dve.wait_ge(S["mixed"], t + 1)
                step(V.tensor_tensor(tB[0:P, b, :], tA[0:P, b, :], tA[0:P, b, :], ALU.mult))
                step(V.tensor_reduce(nrm[:, b, 0:H], tt3(tB[0:P, b, :]), AX, ALU.add))
                V.tensor_scalar(nrm[:, b, 0:H], nrm[:, b, 0:H], 1.0 / DH, 1e-5, ALU.mult, ALU.add).then_inc(S["f_ms"], 1)
                step(V.tensor_tensor(tt3(hs[:, t, :]), tt3(hs[:, t, :]), bm(onorm[:, :], H), ALU.mult))
                dve.wait_ge(S["f_rs"], t + 1)
                step(V.tensor_tensor(tt3(tA[0:P, b, :]), tt3(tA[0:P, b, :]), bc(nrm[:, b, 0:H], DH), ALU.mult))
                V.tensor_tensor(tA[0:P, b, :], tA[0:P, b, :], hs[:, t, :], ALU.mult).then_inc(S["f_gated"], 1)
                if t >= 1:
                    last_sum(dve, V, t - 1)
            last_sum(dve, V, NT - 1)


_SHARED = ("x", "src", "dst")


def kernel(**inputs):
    import concourse.bacc as bacc
    from concourse.bass_utils import run_bass_kernel_spmd

    nc = bacc.Bacc("TRN2", target_bir_lowering=False, num_devices=1)
    a = {k: np.asarray(v) for k, v in inputs.items()}
    for name in ("L0_mix_Wq", "L0_mix_Wk", "L0_mix_Wv", "L0_mix_Wo"):
        a[name] = a[name].T
    a["L0_mix_bq"] = a["L0_mix_bq"].reshape(KC, 128).T
    a["wsmall"] = np.concatenate([a.pop("L0_ffn_Wgate"), a.pop("L0_ffn_Wb"), a.pop("L0_ffn_Wa")], axis=1)
    a.update(consts())
    arrays, d = {}, {}
    for name, v in a.items():
        v = np.ascontiguousarray(v)
        arrays["in_" + name] = v
        d[name] = nc.dram_tensor("in_" + name, v.shape, mybir.dt.from_np(v.dtype), kind="ExternalInput").ap()
    out = nc.dram_tensor("out_0", (N, D), mybir.dt.float32, kind="ExternalOutput").ap()
    gps_layer(nc, d, out)
    r = run_bass_kernel_spmd(nc, [arrays], core_ids=[0])
    return r.results[0]["out_0"]
```

```python
import concourse.bass as bass
from concourse import mybir
from contextlib import ExitStack
import numpy as np

N, D, H, DH = 1250, 512, 8, 64
P = 125
NT = N // P
KC = D // 128
NE = 20000
EPP = NE // P
E = 4
SLOTS = 2 * N
NCH = SLOTS // P
HH = H // 2
CW = HH * P
GP, GC = 5, 250
SC = 18
SW = NT * SC
PLACES = SC * 128
UC = 16
MAXR = -(-NE // PLACES)
ROUND_STEPS = 10
FILLS = 8
OW = 126
LEVELS = 7
QSEG = [(0, 418), (418, 416), (834, 416)]
G_FLOOR = -110.0


def consts():
    i = np.arange(P)
    row, col = i[:, None], i[None, :]
    parts = [row <= col, row > col, row < col]
    for lv in range(LEVELS):
        s = 1 << lv
        off = (row // (2 * s) == col // (2 * s)) & (row // s % 2 == 1) & (col // s % 2 == 0)
        parts.append((row == col).astype(np.float32) - off)
    off = (row // 2 == col // 2) & (row % 2 == 1) & (col % 2 == 0)
    parts.append(((row == col).astype(np.float32) - off).T)
    tri = np.concatenate([np.asarray(p, np.float32) for p in parts], axis=1)
    iota = np.tile(np.arange(N, dtype=np.float16), (128, 1))
    return {"ident": np.eye(128, dtype=np.float32), "tri": np.ascontiguousarray(tri), "iota": iota}


def gps_layer(nc, d, out):
    f32, i32, f16 = mybir.dt.float32, mybir.dt.int32, mybir.dt.float16
    ALU = mybir.AluOpType
    ACT = mybir.ActivationFunctionType
    AX = mybir.AxisListType.X
    ctx = ExitStack()
    with ctx:
        def sb(name, shape, dt=f32):
            return ctx.enter_context(nc.sbuf_tensor(name, shape, dt))

        def sem(name):
            return ctx.enter_context(nc.semaphore(name))

        qkv_slots = nc.dram_tensor("qkv_slots", [SLOTS, 3 * D], f32, kind="Internal").ap()
        gb_slots = nc.dram_tensor("gb_slots", [SLOTS, 2 * H], f32, kind="Internal").ap()
        o_slots = nc.dram_tensor("o_slots", [SLOTS, D], f32, kind="Internal").ap()

        x_all = sb("x_all", [P, NT, D])
        xT = sb("xT", [128, KC, N])
        big = sb("big", [128, NT * N])
        cnt = big[0:P, :].rearrange("p (t n) -> p t n", t=NT)
        qT = big[:, 0:KC * N].rearrange("p (k n) -> p k n", k=KC)
        hs = sb("hs", [P, NT, D])
        W = sb("W", [128, 5, KC, D])
        ident = sb("ident_sb", [128, 128])
        tri = sb("tri_sb", [P, (3 + LEVELS + 1) * P])
        iota = sb("iota_sb", [128, N], f16)
        ones = sb("ones", [128, 64])
        onesq = sb("onesq", [P, P])
        zeros16 = sb("zeros16", [P, 512], f16)
        phalf = sb("phalf", [P, 16 + 64])
        b_k, b_v, b_o = (big[0:P, KC * N + n * D:KC * N + (n + 1) * D] for n in range(3))
        b_g = sb("b_g", [P, D])
        b_q = sb("b_q", [128, KC])
        onorm = sb("onorm", [P, DH])
        alog = sb("alog", [P, H])
        dtb = sb("dtb", [P, H])
        wsm = sb("wsm", [128, KC, E + 2 * H])
        ei = sb("ei", [P, 2, EPP], i32)
        ef = sb("ef", [P, 2, EPP])
        stats = sb("stats", [P, NT, 6])
        mv = sb("mv", [P, NT, 2])
        rstd = sb("rstd", [P, NT])
        xn = sb("xn", [P, 2, D])
        tA = sb("tA", [128, 2, D])
        tB = sb("tB", [128, 2, D])
        tC = sb("tC", [128, 2, D])
        rows_all = sb("rows", [128, 6 * D])
        rows = rows_all[0:P, :].rearrange("p (a n) -> p a n", a=2)
        kvbd = sb("kvbd", [128, KC, 128])
        ksbd = sb("ksbd", [128, KC, 2])
        den = sb("den", [P, 2, H])
        dinv = sb("dinv", [P, NT])
        deg = sb("deg", [P, NT])
        xTf = xT[0:P, :, :].rearrange("p k n -> p (k n)")
        over = xTf[:, 0:11 * EPP].rearrange("p (b j) -> p b j", b=11)
        binm = xTf[:, 11 * EPP:21 * EPP].rearrange("p (b j) -> p b j", b=NT)
        seen = xTf[:, 21 * EPP:31 * EPP].rearrange("p (b j) -> p b j", b=NT)
        tAf = tA[0:P, :, :].rearrange("p a n -> p (a n)")
        e_row, e_col, e_loc, e_dst, e_tile, e_rank = (tAf[:, n * EPP:(n + 1) * EPP] for n in range(6))
        e_all = tAf[:, 0:4 * EPP].rearrange("p (a j) -> p a j", a=4)
        tBf = tB[0:P, :, :].rearrange("p a n -> p (a n)")
        e_int = tBf[:, 0:EPP].bitcast(i32)
        e_q = tBf[:, EPP:2 * EPP]
        e_ok = tBf[:, 600:600 + EPP]
        s_cols = tBf[:, 800:800 + 4 * UC].rearrange("p (a j) -> p a j", a=4)
        cnt_pb, off_pb, tot_b = (tBf[:, 400 + 16 * n:400 + 16 * n + NT] for n in range(3))
        over_r = tBf[:, 480:480 + MAXR - 1]
        n_max, n_r = tBf[:, 500:501], tBf[:, 502:503]
        rounds = sb("rounds", [P, 1], i32)
        srt = tC[:, 0, 0:2 * SW].rearrange("p (a n) -> p a n", a=2)
        rowsf = rows_all[:, :].bitcast(f16)
        oh_row = rowsf[0:P, 0:2 * 128].rearrange("p (u n) -> p u n", u=2)
        oh_col = rowsf[0:P, 256:256 + 4 * SW].rearrange("p (u n) -> p u n", u=2)
        oh_dst = rowsf[:, 1024:1024 + NT * GC].rearrange("p (u n) -> p u n", u=NT)
        Wf = W[:, :, :, :].rearrange("p w k n -> p (w k n)").bitcast(f16)
        xTh = xT[:, :, :].rearrange("p k n -> p (k n)").bitcast(f16)

        def oh_src(b, at, n):
            return Wf[:, bass.ds(at + b * SC * OW, n)] if b < NT - 1 else xTh[:, bass.ds(at, n)]

        LE, GT, LT = tri[:, 0:P], tri[:, P:2 * P], tri[:, 2 * P:3 * P]

        def level_mask(lv):
            return tri[:, (3 + lv) * P:(4 + lv) * P]

        mask1T = level_mask(LEVELS)
        lg = sb("lg", [P, NT, E + 2 * H])
        rt = big[0:P, 20 * CW:20 * CW + 10 * NT * H].rearrange("p (a t h) -> p a t h", a=10, t=NT)
        sc = sb("sc", [P, E, NT])
        rk = sb("rk", [P, E, NT])
        sel = sb("sel", [P, E, NT])
        pos = sb("pos", [P, E, NT])
        tots = sb("tots", [P, E * NT])
        offs = sb("offs", [P, E * NT])
        one40 = sb("one40", [P, E * NT])
        fst = sb("fst", [P, E, NT])
        t4 = sb("t4", [P, 4, E, NT])
        c_pos = sb("c_pos", [P, 2, NT])
        c_w = sb("c_w", [P, 2, NT])
        c_m = sb("c_m", [P, 2, NT])
        c_f = sb("c_f", [P, 2, NT])
        c_t = sb("c_t", [P, 2, NT])
        sp_t = sb("sp_t", [P, 4, NT])
        posi = sb("posi", [P, 2, NT], i32)
        gb = sb("gb", [P, NT, 2, 2 * H])
        nrm = sb("nrm", [P, 2, 2 * H])
        gbs = sb("gbs", [P, NCH, 2 * H])
        gs = sb("gs", [P, NCH, H])
        gam = sb("gam", [P, NCH, H])
        bet = sb("bet", [P, NCH, H])
        bdec = sb("bdec", [P, NCH, H])
        gtot = sb("gtot", [64, NCH, H])
        state = sb("state", [64, H, DH])
        ktile, qtile, vtile = rows[:, 0, 0:D], rows[:, 0, D:2 * D], rows[:, 0, 2 * D:3 * D]
        kdec = rows[:, 1, 0:D]
        zt = rows[:, 1, D:2 * D]
        ot = rows[:, 1, 2 * D:3 * D]
        sdec = sb("sdec", [64, H, DH])

        def cmat(n, half, parts=P):
            at = (n * 2 + half) * CW
            return big[0:parts, at:at + CW].rearrange("p (h i) -> p h i", h=HH)

        RG, BM, DT, AT, PT, TT = range(6)
        RES, T0 = 10, 11
        UU = T0

        def cmat16(n, half):
            at = (12 + n // 2 * 2 + half) * CW + n % 2 * CW // 2
            return big[0:P, at:at + CW // 2].bitcast(f16).rearrange("p (h i) -> p h i", h=HH)

        T16, TT16, B16, AT16 = range(4)
        ident16 = big[0:P, 24 * CW:24 * CW + 64].bitcast(f16)[:, 0:P]
        kT2 = big[0:64, 16 * CW:18 * CW].rearrange("p (h n) -> p h n", h=2)
        qT2 = big[0:64, 18 * CW:20 * CW].rearrange("p (h n) -> p h n", h=2)

        bank = ctx.enter_context(nc.psum_tensor("bank", [128, 8, 512], f32))

        S = {n: sem(n) for n in (
            "x_loaded", "consts_loaded", "edges_loaded", "bias_loaded", "small_loaded",
            "eps_added", "rstd_done", "xn_done", "xT_psum", "xT_done",
            "proj_psum", "proj_sum", "proj_neg", "proj_exp", "proj_done", "kv_psum", "kv_done",
            "h_psum", "h_done", "att_psum", "att_done", "attT_psum", "attT_done",
            "mix_psum", "mix_done", "mix_added", "filled", "onehots_done", "cells_done", "sort_oh", "sort_used", "sorted", "src_oh", "rounds_done", "off_psum", "counts_ready", "round_step", "scalars", "at16_done",
            "onehots_used", "count_done", "loops_added", "deg_psum", "deg_done",
            "dinv_done", "hs_done", "agg_psum", "agg_sum", "agg_done",
            "logit_psum", "gate_step", "gate_exp", "pos_psum", "pos_ready",
            "f_psum", "f_act", "ss_done", "rn_done", "rows_done",
            "gb_loaded", "gb_ready", "decay_psum", "decay_exp", "scal_done", 
            "k_loaded", "q_loaded", "v_loaded", "kdec_done", "sdec_done",
            "o_stored", "mixed", "f_ms", "f_rs", "f_gated", "fT_psum",
            "fT_done", "y_psum", "y_done", "ln_table", "vec_step", "gb_scattered", "vec_order", "at_strict", "ks_dec", "db_raw", "kk_psum", "tt1_done")}
        W_loaded = [sem(f"W{i}_loaded") for i in range(5)]
        HS = {n: [sem(f"{n}{h}") for h in range(2)] for n in (
            "rg_built", "bm_built", "e_psum", "dt_done", "kT_psum", "kT_done", "qT_psum", "qT_done",
            "kq_psum", "at_raw", "at_done", "pt_done", "a_psum",
            "m_psum", "m_done", "t_psum", "tt_psum", "t_done", "tt_done", "ks_psum", "y_ready",
            "og_done", "z_psum", "z_done", "o_psum", "s_psum", "o_done", "state_done")}
        scattered, gathered, out_stored = ([sem(f"{n}{b}") for b in range(2)] for n in ("scattered", "gathered", "out_stored"))
        block = ctx.enter_context(nc.Block())

        class Step:
            def __init__(self, eng, s, base=0):
                self.eng, self.s, self.n, self.base = eng, s, 0, base

            def __call__(self, ins):
                self.n += 1
                ins.then_inc(self.s, 1)
                self.eng.wait_ge(self.s, self.base + self.n)

        def tt3(ap):
            return ap.rearrange("p (h e) -> p h e", e=DH)

        def bc(ap, n):
            return ap.unsqueeze(2).broadcast_to([ap.shape[0], ap.shape[1], n])

        def bm(ap, n):
            return ap.unsqueeze(1).broadcast_to([ap.shape[0], n, ap.shape[1]])

        def chunk(ap, c, h):
            return ap[:, bass.ds(c, 1), h * HH:(h + 1) * HH].rearrange("p a h -> p (a h)")

        def half(ap, h):
            return ap[:, h * HH * DH:(h + 1) * HH * DH]

        def count_banks(ps):
            return ps[0:P, 0:5, :].rearrange("p b (s n) -> p (b s) n", s=2)[:, :, 0:GC]

        def prior(eng, s, n):
            if not (isinstance(n, int) and n == 0):
                eng.wait_ge(s, n)

        def settled(eng):
            eng.wait_ge(S["filled"], FILLS)

        def norm_tile(pool, t):
            pool.wait_ge(S["f_ms"], t + 1)
            nc.gpsimd.tensor_tensor(nrm[:, t % 2, 0:H], nrm[:, t % 2, 0:H], phalf[:, 0:H], ALU.pow).then_inc(S["f_rs"], 1)

        def mix_out(dve, V, t):
            dve.wait_ge(S["mix_psum"], t + 1)
            V.tensor_tensor(x_all[:, t, :], bank[0:P, 6 + t % 2, :], x_all[:, t, :], ALU.add).then_inc(S["mix_done"], 1)
            dve.wait_ge(S["mix_done"], t + 1)
            V.tensor_tensor(x_all[:, t, :], x_all[:, t, :], b_o[:, :], ALU.add).then_inc(S["mix_added"], 1)

        def last_sum(dve, V, t):
            dve.wait_ge(S["y_psum"], t + 1)
            if t >= 2:
                dve.wait_ge(out_stored[t % 2], 16 * (t // 2))
            V.tensor_tensor(tC[0:P, t % 2, :], bank[0:P, 6 + t % 2, :], x_all[:, t, :], ALU.add).then_inc(S["y_done"], 1)

        @block.sync
        def _(sp):
            sp.dma_start(x_all[:, :, :], d["x"].rearrange("(t p) d -> p t d", p=P)).then_inc(S["x_loaded"], 16)
            sp.dma_start(ident[:, :], d["ident"]).then_inc(S["consts_loaded"], 16)
            sp.dma_start(tri[:, :], d["tri"]).then_inc(S["consts_loaded"], 16)
            sp.dma_start(iota[:, :], d["iota"]).then_inc(S["consts_loaded"], 16)
            for n, name in enumerate(("L0_mix_Wk", "L0_mix_Wv", "L0_mix_Wq", "L0_mix_Wo", "L0_gnn_W")):
                sp.dma_start(W[:, n], d[name].rearrange("(k p) n -> p k n", p=128)).then_inc(W_loaded[n], 16)
            for buf, name in ((b_k, "L0_mix_bk"), (b_v, "L0_mix_bv"), (b_o, "L0_mix_bo"), (b_g, "L0_gnn_b")):
                sp.dma_start(buf[:, :], d[name].partition_broadcast(P)).then_inc(S["bias_loaded"], 16)
            sp.dma_start(b_q[:, :], d["L0_mix_bq"]).then_inc(S["bias_loaded"], 16)
            for n, name in enumerate(("src", "dst")):
                sp.dma_start(ei[:, n, :], d[name].rearrange("(p j) -> p j", p=P)).then_inc(S["edges_loaded"], 16)
            sp.dma_start(onorm[:, :], d["L0_ffn_o_norm_weight"].partition_broadcast(P)).then_inc(S["small_loaded"], 16)
            sp.dma_start(alog[:, :], d["L0_ffn_A_log"].partition_broadcast(P)).then_inc(S["small_loaded"], 16)
            sp.dma_start(dtb[:, :], d["L0_ffn_dt_bias"].partition_broadcast(P)).then_inc(S["small_loaded"], 16)
            sp.dma_start(wsm[:, :, :], d["wsmall"].rearrange("(k p) n -> p k n", p=128)).then_inc(S["small_loaded"], 16)
            sp.wait_ge(S["counts_ready"], 1)
            for n, name in enumerate(("L0_ffn_Wq", "L0_ffn_Wk", "L0_ffn_Wv", "L0_ffn_Wg", "L0_ffn_Wo")):
                sp.dma_start(W[:, n], d[name].rearrange("(k p) n -> p k n", p=128)).then_inc(W_loaded[n], 16)
            sp.wait_ge(S["gb_scattered"], 16 * 2 * NT)
            sp.dma_start(gbs[:, :, :], gb_slots.rearrange("(c p) n -> p c n", p=P)).then_inc(S["gb_loaded"], 16)
            for b in range(2):
                sp.wait_ge(scattered[b], 16 * NT)
            sp.dma_start(ktile, qkv_slots[0:P, D:2 * D]).then_inc(S["k_loaded"], 16)
            sp.dma_start(qtile, qkv_slots[0:P, 0:D]).then_inc(S["q_loaded"], 16)
            sp.dma_start(vtile, qkv_slots[0:P, 2 * D:3 * D]).then_inc(S["v_loaded"], 16)
            with sp.Fori(1, NCH) as c:
                r0 = c * P
                for h in range(2):
                    prior(sp, HS["kT_psum"][h], c)
                    prior(sp, HS["qT_psum"][h], c)
                prior(sp, S["kdec_done"], c)
                sp.dma_start(ktile, qkv_slots[bass.ds(r0, P), D:2 * D]).then_inc(S["k_loaded"], 16)
                sp.dma_start(qtile, qkv_slots[bass.ds(r0, P), 0:D]).then_inc(S["q_loaded"], 16)
                for h in range(2):
                    prior(sp, HS["y_ready"][h], c)
                sp.dma_start(vtile, qkv_slots[bass.ds(r0, P), 2 * D:3 * D]).then_inc(S["v_loaded"], 16)
                for h in range(2):
                    prior(sp, HS["o_done"][h], c)
                sp.dma_start(o_slots[bass.ds(r0 - P, P), :], ot).then_inc(S["o_stored"], 16)
            for h in range(2):
                sp.wait_ge(HS["o_done"][h], NCH)
            sp.dma_start(o_slots[SLOTS - P:SLOTS, :], ot).then_inc(S["o_stored"], 16)
            for t in range(NT):
                sp.wait_ge(S["y_done"], t + 1)
                sp.dma_start(out[t * P:(t + 1) * P, :], tC[0:P, t % 2, :]).then_inc(out_stored[t % 2], 16)
            for b in range(2):
                sp.wait_ge(out_stored[b], 16 * NT // 2)
            sp.wait_ge(S["o_stored"], 16 * NCH)

        @block.tensor
        def _(pe):
            mm = nc.tensor.matmul
            pe.wait_ge(S["consts_loaded"], 48)
            pe.wait_ge(S["filled"], FILLS)

            def transpose_tiles(src, ready, base, psum_sem, done, banks, at=0):
                for t in range(NT):
                    pe.wait_ge(ready, base + t + 1)
                    if t >= 2 or at:
                        pe.wait_ge(done, at + t - 1)
                    for k in range(KC):
                        last = nc.tensor.transpose(bank[:, banks + t % 2, k * P:(k + 1) * P],
                                                   src(t)[:, k * 128:(k + 1) * 128], ident[0:P, 0:P])
                    last.then_inc(psum_sem, 1)

            def project(dst, t, w):
                for k in range(KC):
                    last = mm(dst, xT[:, k, t * P:(t + 1) * P], W[:, w, k, :], start=(k == 0), stop=(k == KC - 1))
                return last

            transpose_tiles(lambda t: xn[:, t % 2, :], S["xn_done"], 0, S["xT_psum"], S["xT_done"], 6)
            pe.wait_ge(S["xT_done"], NT)
            pe.wait_ge(W_loaded[0], 16)
            pe.wait_ge(W_loaded[1], 16)
            mm(bank[:, 4, :], zeros16[:, 0:128], zeros16[:, :], start=True, stop=True)
            mm(bank[:, 5, :], zeros16[:, 0:128], zeros16[:, :], start=True, stop=True)
            unit = 0

            def kv_sums(t):
                pe.wait_ge(S["proj_done"], t + 1)
                pe.wait_ge(S["vec_step"], t + 1)
                for c in range(KC):
                    mm(bank[:, 4, c * 128:(c + 1) * 128], tC[0:P, t % 2, c * 128:(c + 1) * 128],
                       xn[:, t % 2, c * 128:(c + 1) * 128], start=False, stop=True, skip_group_check=True)
                for c in range(KC):
                    last = mm(bank[:, 5, c:c + 1], tC[0:P, t % 2, c * 128:(c + 1) * 128], ones[0:P, 0:1],
                              start=False, stop=True, skip_group_check=True)
                last.then_inc(S["kv_psum"], 1)

            for t in range(NT):
                if unit >= 2:
                    pe.wait_ge(S["proj_sum"], unit - 1)
                project(bank[0:P, unit % 2, :], t, 0).then_inc(S["proj_psum"], 1)
                if t >= 2:
                    pe.wait_ge(S["vec_step"], t - 1)
                project(bank[0:P, 2 + t % 2, :], t, 1).then_inc(S["h_psum"], 1)
                unit += 1
                if t >= 1:
                    kv_sums(t - 1)
            kv_sums(NT - 1)
            pe.wait_ge(W_loaded[2], 16)
            for c in range(KC):
                for s0, n in QSEG:
                    pe.wait_ge(S["proj_sum"], unit - 1)
                    for k in range(KC):
                        last = mm(bank[:, unit % 2, 0:n], W[:, 2, k, c * 128:(c + 1) * 128], xT[:, k, s0:s0 + n],
                                  start=(k == 0), stop=(k == KC - 1))
                    last.then_inc(S["proj_psum"], 1)
                    unit += 1
            pe.wait_ge(W_loaded[4], 16)
            for t in range(NT):
                if t < 2:
                    pe.wait_ge(S["vec_step"], NT)
                else:
                    pe.wait_ge(S["h_done"], t - 1)
                project(bank[0:P, 2 + t % 2, :], t, 4).then_inc(S["h_psum"], 1)
            pe.wait_ge(S["kv_done"], 4)
            pe.wait_ge(S["proj_done"], unit)
            pe.wait_ge(W_loaded[3], 16)
            for t in range(NT):
                b = t % 2
                if t >= 2:
                    pe.wait_ge(S["att_done"], t - 1)
                for c in range(KC):
                    mm(bank[0:P, b, c * 128:(c + 1) * 128], qT[:, c, t * P:(t + 1) * P], kvbd[:, c, :], start=True, stop=True)
                if t == 0:
                    pe.wait_ge(S["h_done"], NT)
                for c in range(KC):
                    last = mm(bank[0:P, 2 + b, 2 * c:2 * c + 2], qT[:, c, t * P:(t + 1) * P], ksbd[:, c, :], start=True, stop=True)
                last.then_inc(S["att_psum"], 1)
                pe.wait_ge(S["att_done"], t + 1)
                if t >= 2:
                    pe.wait_ge(S["attT_done"], t - 1)
                for k in range(KC):
                    last = nc.tensor.transpose(bank[:, 4 + b, k * P:(k + 1) * P], tA[0:P, b, k * 128:(k + 1) * 128], ident[0:P, 0:P])
                last.then_inc(S["attT_psum"], 1)
                pe.wait_ge(S["attT_done"], t + 1)
                if t >= 2:
                    pe.wait_ge(S["mix_done"], t - 1)
                for k in range(KC):
                    last = mm(bank[0:P, 6 + b, :], tB[:, b, k * P:(k + 1) * P], W[:, 3, k, :], start=(k == 0), stop=(k == KC - 1))
                last.then_inc(S["mix_psum"], 1)
            pe.wait_ge(S["mix_done"], NT)
            pe.wait_ge(S["cells_done"], 1)
            mm(bank[0:P, 6, 0:NT], LT, cnt_pb, start=True, stop=True)
            mm(bank[0:P, 6, 64:64 + NT], onesq[:, :], cnt_pb, start=True, stop=True).then_inc(S["off_psum"], 1)

            def count_round(r):
                mm(bank[:, 5, :], zeros16[:, 0:128], zeros16[:, :], start=True, stop=True)
                with pe.Fori(0, EPP // UC) as i:
                    for u in range(UC):
                        pe.wait_ge(S["sort_oh"], i * UC + (r * EPP + u + 1))
                        mm(bank[:, 5, 0:2 * SW], oh_row[:, u % 2, :], oh_col[:, u % 2, :], start=False, stop=True,
                           skip_group_check=True).then_inc(S["sort_used"], 1)
                pe.wait_ge(S["src_oh"], r + 1)
                for q in range(GP):
                    if q:
                        pe.wait_ge(S["count_done"], r * GP + q)
                    for b in range(5):
                        mm(bank[:, b, :], zeros16[:, 0:128], zeros16[:, :], start=True, stop=True)
                    with pe.Fori(0, SC) as i:
                        for g in range(2):
                            pe.wait_ge(S["onehots_done"], i * 2 + ((r * GP + q) * 2 * SC + g + 1))
                            for b in range(5 * g, 5 * g + 5):
                                last = mm(bank[0:P, b // 2, b % 2 * 256:b % 2 * 256 + GC], oh_src(b, i * OW, P),
                                          oh_dst[:, b, :], start=False, stop=True, skip_group_check=True)
                            last.then_inc(S["onehots_used"], 1)

            for s in (S["sort_used"], S["onehots_used"]):
                for n in range(2):
                    mm(bank[:, 7, 0:128], zeros16[:, 0:128], zeros16[:, 0:128], start=True, stop=True).then_inc(s, 1)
            count_round(0)
            pe.wait_ge(S["rounds_done"], 1)
            n_rounds = pe.value_load(rounds[0:1, 0:1], min_val=1, max_val=MAXR)
            with pe.If(n_rounds > 1):
                with pe.Fori(1, n_rounds) as r:
                    pe.wait_ge(S["count_done"], r * GP)
                    count_round(r)
            pe.wait_ge(S["loops_added"], NT)
            for t in range(NT):
                for s in range(NT):
                    last = mm(bank[0:P, 6, t:t + 1], cnt[:, s, t * P:(t + 1) * P], ones[0:P, 0:1], start=(s == 0), stop=(s == NT - 1))
            last.then_inc(S["deg_psum"], 1)
            pe.wait_ge(S["hs_done"], NT)
            for t in range(NT):
                if t >= 2:
                    pe.wait_ge(S["agg_sum"], t - 1)
                for s in range(NT):
                    last = mm(bank[0:P, t % 2, :], cnt[:, s, t * P:(t + 1) * P], hs[:, s, :], start=(s == 0), stop=(s == NT - 1))
                last.then_inc(S["agg_psum"], 1)
            transpose_tiles(lambda t: xn[:, t % 2, :], S["xn_done"], NT, S["xT_psum"], S["xT_done"], 6, at=NT)
            pe.wait_ge(S["xT_done"], 2 * NT)
            pe.wait_ge(S["small_loaded"], 64)
            pe.wait_ge(S["agg_sum"], NT)
            for t in range(NT):
                n = E + 2 * H
                for k in range(KC):
                    last = mm(bank[0:P, 0, t * n:(t + 1) * n], xT[:, k, t * P:(t + 1) * P], wsm[:, k, :],
                              start=(k == 0), stop=(k == KC - 1))
            last.then_inc(S["logit_psum"], 1)
            pe.wait_ge(S["gate_step"], 1)
            mm(bank[0:P, 1, 0:E * NT], LT, sel[:, :, :].rearrange("p e t -> p (e t)"), start=True, stop=True)
            mm(bank[0:P, 1, 64:64 + E * NT], onesq[:, :], sel[:, :, :].rearrange("p e t -> p (e t)"),
               start=True, stop=True).then_inc(S["pos_psum"], 1)
            for w in range(4):
                pe.wait_ge(W_loaded[w], 32)
            for t in range(NT):
                for w in range(4):
                    if t:
                        pe.wait_ge(S["f_act"], 4 * (t - 1) + w + 1)
                    project(bank[0:P, 2 + w, :], t, w).then_inc(S["f_psum"], 1)
            pe.wait_ge(S["gb_ready"], 1)
            g2 = gs[:, :, :].rearrange("p c h -> p (c h)")
            mm(bank[0:P, 6, 0:NCH * H], LE, g2, start=True, stop=True)
            mm(bank[0:P, 6, 160:160 + NCH * H], GT, g2, start=True, stop=True)
            mm(bank[0:64, 6, 320:320 + NCH * H], ones[0:P, 0:64], g2, start=True, stop=True).then_inc(S["decay_psum"], 1)
            pe.wait_ge(S["decay_exp"], 1)
            pe.wait_ge(S["f_act"], 4 * NT)
            def chunk_step(c):
                pe.wait_ge(S["k_loaded"], c * 16 + 16)
                pe.wait_ge(S["q_loaded"], c * 16 + 16)
                for h in range(2):
                    pe.wait_ge(HS["rg_built"][h], c + 1)
                    prior(pe, HS["z_done"][h], c)
                    mm(bank[0:P, h, 0:CW], GT, cmat(RG, h).rearrange("p h i -> p (h i)"), start=True, stop=True).then_inc(HS["e_psum"][h], 1)
                for h in range(2):
                    settled(pe)
                    prior(pe, HS["state_done"][h], c)
                    for j in range(HH):
                        last = nc.tensor.transpose(bank[0:64, 6 + h, j * P:(j + 1) * P],
                                                   ktile[:, (h * HH + j) * DH:(h * HH + j + 1) * DH], ident[0:P, 0:P])
                    last.then_inc(HS["kT_psum"][h], 1)
                for h in range(2):
                    settled(pe)
                    prior(pe, HS["o_done"][h], c)
                    for j in range(HH):
                        last = nc.tensor.transpose(bank[0:64, 2 + h, j * P:(j + 1) * P],
                                                   qtile[:, (h * HH + j) * DH:(h * HH + j + 1) * DH], ident[0:P, 0:P])
                    last.then_inc(HS["qT_psum"][h], 1)
                for h in range(2):
                    pe.wait_ge(HS["kT_done"][h], c + 1)
                    prior(pe, HS["og_done"][h], c)
                    for j in range(HH):
                        kj = kT2[:, h, j * P:(j + 1) * P]
                        last = mm(bank[0:P, 4 + h, j * P:(j + 1) * P], kj, kj, start=True, stop=True)
                    last.then_inc(S["kk_psum"], 1)
                for h in range(2):
                    pe.wait_ge(HS["qT_done"][h], c + 1)
                    pe.wait_ge(HS["dt_done"][h], c + 1)
                    for j in range(HH):
                        last = mm(bank[0:P, h, j * P:(j + 1) * P], kT2[:, h, j * P:(j + 1) * P],
                                  qT2[:, h, j * P:(j + 1) * P], start=True, stop=True)
                    last.then_inc(HS["kq_psum"][h], 1)
                for h in range(2):
                    pe.wait_ge(S["at16_done"], c * 2 + (h + 1))
                    for j in range(HH):
                        last = mm(bank[0:P, 2 + h, j * P:(j + 1) * P], cmat16(AT16, h)[:, j, :], ident16[:, :], start=True, stop=True)
                    last.then_inc(HS["a_psum"][h], 1)
                for lv in range(1, LEVELS):
                    for h in range(2):
                        if lv == 1:
                            pe.wait_ge(HS["m_done"][h], c * (LEVELS + 1) + 1)
                        else:
                            pe.wait_ge(HS["t_done"][h], c * (LEVELS - 1) + (lv - 1))
                        for j in range(HH):
                            last = mm(bank[0:P, 4 + h, j * P:(j + 1) * P], cmat16(AT16, h)[:, j, :], cmat16(T16, h)[:, j, :], start=True, stop=True)
                        last.then_inc(HS["m_psum"][h], 1)
                    for h in range(2):
                        pe.wait_ge(HS["m_done"][h], c * (LEVELS + 1) + (lv + 1))
                        if lv == 1:
                            pe.wait_ge(S["tt1_done"], c * 2 + (h + 1))
                            pe.wait_ge(HS["pt_done"][h], c + 1)
                        else:
                            pe.wait_ge(HS["tt_done"][h], c * (LEVELS + 1) + (lv - 1))
                        for j in range(HH):
                            last = mm(bank[0:P, h, j * P:(j + 1) * P], cmat16(TT16, h)[:, j, :], cmat16(B16, h)[:, j, :], start=True, stop=True)
                        last.then_inc(HS["t_psum"][h], 1)
                        for j in range(HH):
                            last = mm(bank[0:P, 2 + h, j * P:(j + 1) * P], cmat16(B16, h)[:, j, :], cmat16(TT16, h)[:, j, :], start=True, stop=True)
                        last.then_inc(HS["tt_psum"][h], 1)
                for h in range(2):
                    pe.wait_ge(HS["t_done"][h], c * (LEVELS - 1) + (LEVELS - 1))
                    for j in range(HH):
                        last = mm(bank[0:P, 4 + h, j * P:(j + 1) * P], cmat(AT, h)[:, j, :], cmat(T0, h)[:, j, :], start=True, stop=True)
                    last.then_inc(HS["m_psum"][h], 1)
                for h in range(2):
                    pe.wait_ge(HS["m_done"][h], c * (LEVELS + 1) + (LEVELS + 1))
                    pe.wait_ge(HS["tt_done"][h], c * (LEVELS + 1) + (LEVELS - 1))
                    for j in range(HH):
                        last = mm(bank[0:P, 2 + h, j * P:(j + 1) * P], cmat(RES, h)[:, j, :], cmat(TT, h)[:, j, :], start=True, stop=True)
                    last.then_inc(HS["tt_psum"][h], 1)
                for h in range(2):
                    prior(pe, HS["state_done"][h], c)
                    for j in range(HH):
                        mm(bank[0:P, 4 + h, j * DH:(j + 1) * DH], kT2[:, h, j * P:(j + 1) * P], state[:, h * HH + j, :], start=True, stop=True)
                    for j in range(HH):
                        last = mm(bank[0:P, 4 + h, 256 + j * DH:256 + (j + 1) * DH], qT2[:, h, j * P:(j + 1) * P], state[:, h * HH + j, :], start=True, stop=True)
                    last.then_inc(HS["ks_psum"][h], 1)
                for h in range(2):
                    pe.wait_ge(HS["tt_done"][h], c * (LEVELS + 1) + LEVELS)
                    for j in range(HH):
                        last = mm(bank[0:P, 2 + h, j * P:(j + 1) * P], cmat(RES, h)[:, j, :], cmat(UU, h)[:, j, :], start=True, stop=True)
                    last.then_inc(HS["tt_psum"][h], 1)
                for h in range(2):
                    pe.wait_ge(HS["tt_done"][h], c * (LEVELS + 1) + (LEVELS + 1))
                    pe.wait_ge(HS["y_ready"][h], c + 1)
                    for j in range(HH):
                        last = mm(bank[0:P, h, j * DH:(j + 1) * DH], cmat(TT, h)[:, j, :], half(tA[0:P, 0, :], h)[:, j * DH:(j + 1) * DH], start=True, stop=True)
                    last.then_inc(HS["z_psum"][h], 1)
                pe.wait_ge(S["kdec_done"], c + 1)
                for h in range(2):
                    pe.wait_ge(HS["z_done"][h], c + 1)
                    for j in range(HH):
                        last = mm(bank[0:64, 6 + h, j * DH:(j + 1) * DH], half(kdec, h)[:, j * DH:(j + 1) * DH],
                                  half(zt, h)[:, j * DH:(j + 1) * DH], start=True, stop=True)
                    last.then_inc(HS["s_psum"][h], 1)
                    for j in range(HH):
                        last = mm(bank[0:P, 2 + h, j * DH:(j + 1) * DH], cmat(PT, h)[:, j, :],
                                  half(zt, h)[:, j * DH:(j + 1) * DH], start=True, stop=True)
                    last.then_inc(HS["o_psum"][h], 1)

            chunk_step(0)
            with pe.Fori(1, NCH) as c:
                chunk_step(c)
            for h in range(2):
                pe.wait_ge(HS["o_done"][h], NCH)
                pe.wait_ge(HS["state_done"][h], NCH)
                pe.wait_ge(HS["og_done"][h], NCH)
            pe.wait_ge(W_loaded[4], 32)
            for t in range(NT):
                b = t % 2
                pe.wait_ge(S["f_gated"], t + 1)
                if t >= 2:
                    pe.wait_ge(S["fT_done"], t - 1)
                for k in range(KC):
                    last = nc.tensor.transpose(bank[:, 4 + b, k * P:(k + 1) * P], tA[0:P, b, k * 128:(k + 1) * 128], ident[0:P, 0:P])
                last.then_inc(S["fT_psum"], 1)
                pe.wait_ge(S["fT_done"], t + 1)
                if t >= 2:
                    pe.wait_ge(S["y_done"], t - 1)
                for k in range(KC):
                    last = mm(bank[0:P, 6 + b, :], qT[:, b, k * P:(k + 1) * P], W[:, 4, k, :], start=(k == 0), stop=(k == KC - 1))
                last.then_inc(S["y_psum"], 1)

        @block.scalar
        def _(act):
            A = nc.scalar.activation

            def copy_tiles(at, base):
                for t in range(NT):
                    act.wait_ge(S["xT_psum"], base + t + 1)
                    A(xT[:, :, t * P:(t + 1) * P], bank[:, 6 + t % 2, 0:KC * P].rearrange("p (k n) -> p k n", k=KC),
                      ACT.Copy).then_inc(S["xT_done"], 1)

            copy_tiles(0, 0)
            for u in range(NT):
                act.wait_ge(S["proj_neg"], u + 1)
                A(tB[0:P, u % 2, :], tB[0:P, u % 2, :], ACT.Exp).then_inc(S["proj_exp"], 1)
            for u in range(NT, NT + KC * len(QSEG)):
                n = QSEG[(u - NT) % 3][1]
                act.wait_ge(S["proj_neg"], u + 1)
                A(tB[:, u % 2, 0:n], tB[:, u % 2, 0:n], ACT.Exp).then_inc(S["proj_exp"], 1)
            for t in range(NT):
                act.wait_ge(S["h_psum"], NT + t + 1)
                A(hs[:, t, :], bank[0:P, 2 + t % 2, :], ACT.Copy).then_inc(S["h_done"], 1)
            for t in range(NT):
                act.wait_ge(S["attT_psum"], t + 1)
                if t >= 2:
                    act.wait_ge(S["mix_psum"], t - 1)
                A(tB[:, t % 2, 0:KC * P], bank[:, 4 + t % 2, 0:KC * P], ACT.Copy).then_inc(S["attT_done"], 1)
            for q in range(GP):
                act.wait_ge(S["onehots_used"], 2 + (q + 1) * 2 * SC)
                A(cnt[:, :, q * GC:(q + 1) * GC], count_banks(bank), ACT.Copy).then_inc(S["count_done"], 1)
            copy_tiles(NT, NT)
            act.wait_ge(S["gate_exp"], 1)
            A(rt[:, 0, :, 0:E], rt[:, 0, :, 0:E], ACT.Exp).then_inc(S["ln_table"], 1)
            A(rt[:, 1, :, :], rt[:, 1, :, :], ACT.Exp).then_inc(S["ln_table"], 1)
            A(rt[:, 2, :, :], rt[:, 2, :, :], ACT.Exp).then_inc(S["ln_table"], 1)
            A(rt[:, 9, 0, :], alog[:, :], ACT.Exp).then_inc(S["ln_table"], 1)
            act.wait_ge(S["gate_exp"], 2)
            A(rt[:, 4, :, :], rt[:, 3, :, :], ACT.Ln).then_inc(S["ln_table"], 1)
            for t in range(NT):
                for w in range(4):
                    act.wait_ge(S["f_psum"], 4 * t + w + 1)
                    if w == 0 and t >= 2:
                        act.wait_ge(scattered[t % 2], 32 * (t // 2))
                    dst = hs[:, t, :] if w == 3 else rows[:, t % 2, w * D:(w + 1) * D]
                    A(dst, bank[0:P, 2 + w, :], ACT.Silu).then_inc(S["f_act"], 1)
            act.wait_ge(S["decay_psum"], 1)
            g2 = lambda a: a[:, :, :].rearrange("p c h -> p (c h)")
            A(ident16[:, :], ident[0:P, 0:P], ACT.Copy)
            A(g2(gam), bank[0:P, 6, 0:NCH * H], ACT.Exp)
            A(g2(bdec), bank[0:P, 6, 160:160 + NCH * H], ACT.Exp)
            A(g2(gtot), bank[0:64, 6, 320:320 + NCH * H], ACT.Exp).then_inc(S["decay_exp"], 1)
            def chunk_step(c):
                for h in range(2):
                    act.wait_ge(HS["e_psum"][h], c + 1)
                    prior(act, HS["pt_done"][h], c)
                    A(cmat(DT, h).rearrange("p h i -> p (h i)"), bank[0:P, h, 0:CW], ACT.Exp).then_inc(HS["dt_done"][h], 1)
                for h in range(2):
                    act.wait_ge(HS["kT_psum"][h], c + 1)
                    prior(act, HS["ks_psum"][h], c)
                    A(kT2[:, h, :], bank[0:64, 6 + h, 0:CW], ACT.Copy).then_inc(HS["kT_done"][h], 1)
                for h in range(2):
                    act.wait_ge(HS["qT_psum"][h], c + 1)
                    A(qT2[:, h, :], bank[0:64, 2 + h, 0:CW], ACT.Copy).then_inc(HS["qT_done"][h], 1)
                for h in range(2):
                    act.wait_ge(HS["at_done"][h], c + 1)
                    A(cmat16(AT16, h), cmat(AT, h), ACT.Copy).then_inc(S["at16_done"], 1)
                for lv in range(1, LEVELS):
                    for h in range(2):
                        if h == 0:
                            act.wait_ge(HS["t_psum"][h], c * (LEVELS - 1) + lv)
                            A(cmat(T0, h) if lv == LEVELS - 1 else cmat16(T16, h),
                              bank[0:P, h, 0:CW].rearrange("p (h i) -> p h i", h=HH), ACT.Copy).then_inc(HS["t_done"][h], 1)
                        act.wait_ge(HS["tt_psum"][h], c * (LEVELS + 1) + lv)
                        A(cmat(TT, h) if lv == LEVELS - 1 else cmat16(TT16, h),
                          bank[0:P, 2 + h, 0:CW].rearrange("p (h i) -> p h i", h=HH), ACT.Copy).then_inc(HS["tt_done"][h], 1)
                for h in range(2):
                    act.wait_ge(HS["z_psum"][h], c + 1)
                    prior(act, HS["o_psum"][h], c)
                    A(half(zt, h), bank[0:P, h, 0:HH * DH], ACT.Copy).then_inc(HS["z_done"][h], 1)

            chunk_step(0)
            with act.Fori(1, NCH) as c:
                chunk_step(c)
            for t in range(NT):
                act.wait_ge(S["fT_psum"], t + 1)
                if t >= 2:
                    act.wait_ge(S["y_psum"], t - 1)
                A(qT[:, t % 2, 0:KC * P], bank[:, 4 + t % 2, 0:KC * P], ACT.Copy).then_inc(S["fT_done"], 1)

        @block.gpsimd
        def _(pool):
            G = nc.gpsimd
            for buf, value in ((ones, 1.0), (onesq, 1.0), (one40, 1.0), (zeros16, 0.0), (phalf, -0.5),
                               (kvbd, 0.0), (ksbd, 0.0), (state, 0.0)):
                G.memset(buf[tuple(slice(None) for _ in buf.shape)], value).then_inc(S["filled"], 1)
            pool.wait_ge(S["filled"], FILLS)

            def rstd_of(n):
                pool.wait_ge(S["eps_added"], n)
                G.tensor_tensor(rstd[:, :], mv[:, :, 1], phalf[:, 0:NT], ALU.pow).then_inc(S["rstd_done"], 1)

            rstd_of(1)
            for u in range(NT):
                pool.wait_ge(S["proj_sum"], u + 1)
                if u >= 2:
                    pool.wait_ge(S["proj_done"], u - 1)
                G.tensor_scalar(tB[0:P, u % 2, :], tA[0:P, u % 2, :], 0.0, None, ALU.min).then_inc(S["proj_neg"], 1)
            for u in range(NT, NT + KC * len(QSEG)):
                n = QSEG[(u - NT) % 3][1]
                pool.wait_ge(S["proj_sum"], u + 1)
                pool.wait_ge(S["proj_done"], u - 1)
                G.tensor_scalar(tB[:, u % 2, 0:n], tA[:, u % 2, 0:n], 0.0, None, ALU.min).then_inc(S["proj_neg"], 1)
            pool.wait_ge(S["counts_ready"], 1)
            for t in range(NT):
                v = cnt[:, t, t * P:(t + 1) * P]
                G.tensor_tensor(v, v, ident[0:P, 0:P], ALU.add).then_inc(S["loops_added"], 1)
            pool.wait_ge(S["deg_done"], 1)
            G.tensor_tensor(dinv[:, :], deg[:, :], phalf[:, 0:NT], ALU.pow).then_inc(S["dinv_done"], 1)
            rstd_of(2)
            pool.wait_ge(S["pos_ready"], 1)
            for t in range(NT):
                for c in range(2):
                    G.indirect_dma_start(gb_slots, bass.IndirectOffsetOnAxis(ap=posi[:, c, t:t + 1], axis=0),
                                         gb[:, t, c, :], None).then_inc(S["gb_scattered"], 16)
            for t in range(NT):
                pool.wait_ge(S["ss_done"], t + 1)
                G.tensor_tensor(nrm[:, t % 2, :], nrm[:, t % 2, :], phalf[:, 0:2 * H], ALU.pow).then_inc(S["rn_done"], 1)
                pool.wait_ge(S["rows_done"], t + 1)
                for c in range(2):
                    G.indirect_dma_start(qkv_slots, bass.IndirectOffsetOnAxis(ap=posi[:, c, t:t + 1], axis=0),
                                         rows[:, t % 2, :], None).then_inc(scattered[t % 2], 16)
            pool.wait_ge(S["scal_done"], 1)
            def chunk_step(c):
                for h in range(2):
                    prior(pool, HS["e_psum"][h], c)
                    G.tensor_tensor(cmat(RG, h), bc(chunk(gs, c, h), P), bm(LE, HH), ALU.mult).then_inc(HS["rg_built"][h], 1)
                    prior(pool, S["db_raw"], c * 2)
                    G.tensor_tensor(cmat(BM, h), bc(chunk(bet, c, h), P), bm(LE, HH), ALU.mult).then_inc(HS["bm_built"][h], 1)
                pool.wait_ge(S["k_loaded"], c * 16 + 16)
                for h in range(2):
                    prior(pool, HS["s_psum"][h], c)
                G.tensor_tensor(tt3(kdec), tt3(ktile), bc(bdec[:, bass.ds(c, 1), :].rearrange("p a h -> p (a h)"), DH), ALU.mult).then_inc(S["kdec_done"], 1)
                for h in range(2):
                    pool.wait_ge(HS["at_raw"][h], c + 1)
                    G.tensor_tensor(cmat(AT, h), cmat(AT, h), bm(LT, HH), ALU.mult).then_inc(S["at_strict"], 1)
                    pool.wait_ge(S["at_strict"], c * 2 + (h + 1))
                    G.tensor_tensor(cmat(AT, h), cmat(AT, h), bm(ident[0:P, 0:P], HH), ALU.add).then_inc(HS["at_done"][h], 1)
                    pool.wait_ge(HS["at_done"][h], c + 1)
                    prior(pool, HS["z_psum"][h], c)
                    G.tensor_tensor(cmat16(TT16, h), cmat(AT, h), bm(mask1T, HH), ALU.mult).then_inc(S["tt1_done"], 1)
                for h in range(2):
                    prior(pool, HS["state_done"][h], c)
                hh = gtot[:, bass.ds(c, 1), :].rearrange("p a h -> p (a h)")
                G.tensor_tensor(sdec[:, :, :], state[:, :, :], bc(hh, DH), ALU.mult).then_inc(S["sdec_done"], 1)

            chunk_step(0)
            with pool.Fori(1, NCH) as c:
                chunk_step(c)
            pool.wait_ge(S["o_stored"], 16 * NCH)
            for t in range(NT):
                if t >= 2:
                    pool.wait_ge(S["mixed"], t - 1)
                for c in range(2):
                    G.indirect_dma_start(rows[:, t % 2, c * D:(c + 1) * D], None, o_slots,
                                         bass.IndirectOffsetOnAxis(ap=posi[:, c, t:t + 1], axis=0)).then_inc(gathered[t % 2], 16)
                if t >= 1:
                    norm_tile(pool, t - 1)
            norm_tile(pool, NT - 1)

        @block.vector
        def _(dve):
            V = nc.vector
            step = Step(dve, S["vec_order"])

            def layer_norm(n, psum_base):
                for t in range(NT):
                    if n:
                        dve.wait_ge(S["agg_done"], t + 1)
                    step(V.bn_stats(stats[:, t, :], x_all[:, t, :]))
                for t in range(NT):
                    step(V.bn_aggr(mv[:, t, :], stats[:, t, :]))
                V.tensor_scalar(mv[:, :, 1], mv[:, :, 1], 1e-5, None, ALU.add).then_inc(S["eps_added"], 1)
                dve.wait_ge(S["rstd_done"], n + 1)
                for t in range(NT):
                    if t >= 2 or n:
                        dve.wait_ge(S["xT_psum"], n * NT + t - 1)
                    V.tensor_scalar(xn[:, t % 2, :], x_all[:, t, :], mv[:, t, 0:1], rstd[:, t:t + 1],
                                    ALU.subtract, ALU.mult).then_inc(S["xn_done"], 1)

            dve.wait_ge(S["x_loaded"], 16)
            layer_norm(0, 0)
            dve.wait_ge(S["bias_loaded"], 80)

            def finish(u, rowsn, n, dst):
                dve.wait_ge(S["proj_exp"], u + 1)
                V.scalar_tensor_tensor(dst, tA[0:rowsn, u % 2, 0:n], 0.0, tB[0:rowsn, u % 2, 0:n],
                                       ALU.max, ALU.add).then_inc(S["proj_done"], 1)

            for t in range(NT):
                dve.wait_ge(S["proj_psum"], t + 1)
                V.tensor_tensor(tA[0:P, t % 2, :], bank[0:P, t % 2, :], b_k[:, :], ALU.add).then_inc(S["proj_sum"], 1)
                dve.wait_ge(S["h_psum"], t + 1)
                if t >= 2:
                    dve.wait_ge(S["kv_psum"], t - 1)
                elif t == 0:
                    dve.wait_ge(S["xT_psum"], NT)
                V.tensor_tensor(xn[:, t % 2, :], bank[0:P, 2 + t % 2, :], b_v[:, :], ALU.add).then_inc(S["vec_step"], 1)
                finish(t, P, D, tC[0:P, t % 2, :])
            dve.wait_ge(S["kv_psum"], NT)
            dve.wait_ge(S["filled"], FILLS)
            for a in range(2):
                q = slice(64 * a, 64 * a + 64)
                V.tensor_copy(kvbd[q, :, q], bank[q, 4, :].rearrange("p (c n) -> p c n", c=KC)[:, :, q]).then_inc(S["kv_done"], 1)
                V.tensor_copy(ksbd[q, :, a:a + 1], bank[q, 5, 0:KC].unsqueeze(2)).then_inc(S["kv_done"], 1)
            u = NT
            for c in range(KC):
                for s0, n in QSEG:
                    dve.wait_ge(S["proj_psum"], u + 1)
                    dve.wait_ge(S["proj_done"], u - 1)
                    V.tensor_scalar(tA[:, u % 2, 0:n], bank[:, u % 2, 0:n], b_q[:, c:c + 1], None, ALU.add).then_inc(S["proj_sum"], 1)
                    if u > NT:
                        finish(u - 1, 128, prev[1], prev[0])
                    prev = (qT[:, c, s0:s0 + n], n)
                    u += 1
            finish(u - 1, 128, prev[1], prev[0])
            for t in range(NT):
                b = t % 2
                dve.wait_ge(S["att_psum"], t + 1)
                step(V.tensor_scalar(den[:, b, :], bank[0:P, 2 + b, 0:H], 1e-6, None, ALU.add))
                step(V.reciprocal(den[:, b, :], den[:, b, :]))
                if t >= 2:
                    dve.wait_ge(S["attT_psum"], t - 1)
                elif t == 0:
                    dve.wait_ge(S["proj_done"], u)
                V.tensor_tensor(tt3(tA[0:P, b, :]), tt3(bank[0:P, b, :]), bc(den[:, b, :], DH), ALU.mult).then_inc(S["att_done"], 1)
                if t >= 1:
                    mix_out(dve, V, t - 1)
            mix_out(dve, V, NT - 1)
            dve.wait_ge(S["edges_loaded"], 32)
            dve.wait_ge(S["attT_psum"], NT)
            dve.wait_ge(S["mix_psum"], NT)
            dve.wait_ge(S["h_psum"], 2 * NT)
            step(V.tensor_copy(ef[:, :, :], ei[:, :, :]))
            for b in range(NT + 1):
                step(V.tensor_scalar(over[:, b, :], ef[:, 0, :], float(P * b), None, ALU.is_ge))
            step(V.tensor_tensor(binm[:, :, :], over[:, 0:NT, :], over[:, 1:NT + 1, :], ALU.subtract))
            step(V.tensor_reduce(e_tile, over[:, 1:NT + 1, :].rearrange("p b j -> p j b"), AX, ALU.add))
            step(V.scalar_tensor_tensor(e_loc, e_tile, float(-P), ef[:, 0, :], ALU.mult, ALU.add))
            step(V.tensor_scalar(e_loc, e_loc, 1.0, None, ALU.add))
            step(V.tensor_copy(e_dst, ef[:, 1, :]))
            step(V.memset(over[:, 0:NT, :], 1.0))
            step(V.memset(over[:, 0:NT, 0:1], 0.0))
            flat = lambda a: a.rearrange("p b j -> p (b j)")
            step(V.tensor_tensor_scan(flat(seen), flat(over[:, 0:NT, :]), flat(binm), 0.0, ALU.mult, ALU.add))
            V.tensor_copy(cnt_pb, seen[:, :, EPP - 1]).then_inc(S["cells_done"], 1)
            dve.wait_ge(S["off_psum"], 1)
            step(V.tensor_copy(off_pb, bank[0:P, 6, 0:NT]))
            step(V.tensor_copy(tot_b, bank[0:P, 6, 64:64 + NT]))
            step(V.tensor_reduce(n_max, tot_b, AX, ALU.max))
            step(V.tensor_scalar(over_r, iota[0:P, 1:MAXR], float(PLACES), n_max, ALU.mult, ALU.is_lt))
            step(V.tensor_reduce(n_r, over_r, AX, ALU.add))
            V.tensor_scalar(rounds[:, :], n_r, 1.0, None, ALU.add).then_inc(S["rounds_done"], 1)
            step(V.tensor_tensor(seen[:, :, :], seen[:, :, :], bc(off_pb, EPP), ALU.add))
            step(V.tensor_tensor(seen[:, :, :], seen[:, :, :], binm[:, :, :], ALU.mult))
            step(V.tensor_reduce(e_rank, seen[:, :, :].rearrange("p b j -> p j b"), AX, ALU.add))
            step(V.tensor_scalar(e_rank, e_rank, -1.0, None, ALU.add))

            def count_round(r):
                s2 = Step(dve, S["round_step"], r * ROUND_STEPS)
                s2(V.tensor_copy(e_int, e_rank))
                s2(V.tensor_scalar(e_int, e_int, 7, None, ALU.arith_shift_right))
                s2(V.tensor_copy(e_q, e_int))
                s2(V.scalar_tensor_tensor(e_row, e_q, -128.0, e_rank, ALU.mult, ALU.add))
                s2(V.tensor_scalar(e_ok, e_rank, 0.0, None, ALU.is_ge))
                s2(V.scalar_tensor_tensor(e_ok, e_rank, float(PLACES), e_ok, ALU.is_lt, ALU.mult))
                s2(V.scalar_tensor_tensor(e_col, e_tile, float(SC), e_q, ALU.mult, ALU.add))
                s2(V.scalar_tensor_tensor(e_col, e_col, 1.0, e_ok, ALU.add, ALU.mult))
                s2(V.tensor_scalar(e_col, e_col, -1.0, None, ALU.add))
                V.tensor_scalar(e_rank, e_rank, float(-PLACES), None, ALU.add).then_inc(S["round_step"], 1)
                with dve.Fori(0, EPP // UC) as i:
                    settled(dve)
                    dve.wait_ge(S["round_step"], r * ROUND_STEPS + ROUND_STEPS)
                    dve.wait_ge(S["sort_used"], i * UC + (r * EPP + 2))
                    V.tensor_copy(s_cols[:, :, :], e_all[:, :, bass.ds(i * UC, UC)]).then_inc(S["scalars"], 1)
                    dve.wait_ge(S["scalars"], i + (r * (EPP // UC) + 1))
                    for u in range(UC):
                        w = u % 2
                        dve.wait_ge(S["sort_used"], i * UC + (r * EPP + u + 1))
                        V.tensor_scalar(oh_row[:, w, :], iota[0:P, 0:128], s_cols[:, 0, u:u + 1], None, ALU.is_equal)
                        for a in range(2):
                            last = V.tensor_scalar(oh_col[:, w, a * SW:(a + 1) * SW], iota[0:P, 0:SW], s_cols[:, 1, u:u + 1],
                                                   s_cols[:, 2 + a, u:u + 1], ALU.is_equal, ALU.mult)
                        last.then_inc(S["sort_oh"], 1)
                dve.wait_ge(S["sort_used"], r * EPP + (EPP + 2))
                V.tensor_scalar(srt[:, 0, :], bank[:, 5, 0:SW], -1.0, None, ALU.add).then_inc(S["sorted"], 1)
                V.tensor_copy(srt[:, 1, :], bank[:, 5, SW:2 * SW]).then_inc(S["sorted"], 1)
                with dve.Fori(0, SC) as i:
                    settled(dve)
                    dve.wait_ge(S["sorted"], r * 2 + 2)
                    for b in range(NT):
                        V.tensor_scalar(oh_src(b, i * OW, OW), iota[:, 0:OW], srt[:, 0, bass.ds(i + b * SC, 1)],
                                        None, ALU.is_equal)
                V.tensor_copy(n_r, n_max).then_inc(S["src_oh"], 1)
                for q in range(GP):
                    with dve.Fori(0, SC) as i:
                        for g in range(2):
                            dve.wait_ge(S["onehots_used"], i * 2 + ((r * GP + q) * 2 * SC + g + 1))
                            for b in range(5 * g, 5 * g + 5):
                                last = V.tensor_scalar(oh_dst[:, b, :], iota[:, q * GC:(q + 1) * GC],
                                                       srt[:, 1, bass.ds(i + b * SC, 1)], None, ALU.is_equal)
                            last.then_inc(S["onehots_done"], 1)
                    if not (isinstance(r, int) and r == 0):
                        dve.wait_ge(S["onehots_used"], (r * GP + (q + 1)) * 2 * SC + 2)
                        cq = cnt[:, :, q * GC:(q + 1) * GC]
                        V.tensor_tensor(cq, count_banks(bank), cq, ALU.add).then_inc(S["count_done"], 1)

            count_round(0)
            dve.wait_ge(S["count_done"], GP)
            dve.wait_ge(S["rounds_done"], 1)
            n_rounds = dve.value_load(rounds[0:1, 0:1], min_val=1, max_val=MAXR)
            with dve.If(n_rounds > 1):
                with dve.Fori(1, n_rounds) as r:
                    count_round(r)
            V.tensor_copy(n_r, n_max).then_inc(S["counts_ready"], 1)
            dve.wait_ge(S["deg_psum"], 1)
            V.tensor_copy(deg[:, :], bank[0:P, 6, 0:NT]).then_inc(S["deg_done"], 1)
            dve.wait_ge(S["dinv_done"], 1)
            for t in range(NT):
                if t == 0:
                    dve.wait_ge(S["h_done"], NT)
                V.tensor_scalar(hs[:, t, :], hs[:, t, :], dinv[:, t:t + 1], None, ALU.mult).then_inc(S["hs_done"], 1)
            for t in range(NT):
                b = t % 2
                dve.wait_ge(S["agg_psum"], t + 1)
                V.scalar_tensor_tensor(tA[0:P, b, :], bank[0:P, b, :], dinv[:, t:t + 1], b_g[:, :],
                                       ALU.mult, ALU.add).then_inc(S["agg_sum"], 1)
                dve.wait_ge(S["agg_sum"], t + 1)
                V.scalar_tensor_tensor(x_all[:, t, :], tA[0:P, b, :], 0.0, x_all[:, t, :],
                                       ALU.max, ALU.add).then_inc(S["agg_done"], 1)
            layer_norm(1, 0)
            dve.wait_ge(S["logit_psum"], 1)
            step(V.tensor_copy(lg[:, :, :], bank[0:P, 0, 0:NT * 20].rearrange("p (t n) -> p t n", t=NT)))
            step(V.tensor_reduce(sp_t[:, 0, :], lg[:, :, 0:E], AX, ALU.max))
            step(V.tensor_tensor(rt[:, 0, :, 0:E], lg[:, :, 0:E], bc(sp_t[:, 0, :], E), ALU.subtract))
            step(V.tensor_scalar(rt[:, 1, :, :], lg[:, :, E:E + H], -1.0, None, ALU.mult))
            step(V.tensor_tensor(rt[:, 5, :, :], lg[:, :, E + H:E + 2 * H], bm(dtb[:, :], NT), ALU.add))
            step(V.tensor_scalar(rt[:, 6, :, :], rt[:, 5, :, :], -1.0, None, ALU.mult))
            V.tensor_tensor(rt[:, 2, :, :], rt[:, 5, :, :], rt[:, 6, :, :], ALU.min).then_inc(S["gate_exp"], 1)
            dve.wait_ge(S["ln_table"], 4)
            V.tensor_scalar(rt[:, 3, :, :], rt[:, 2, :, :], 1.0, None, ALU.add).then_inc(S["gate_exp"], 1)
            dve.wait_ge(S["gate_exp"], 2)
            step(V.tensor_scalar(rt[:, 6, :, :], rt[:, 3, :, :], -1.0, None, ALU.add))
            step(V.tensor_tensor(rt[:, 6, :, :], rt[:, 2, :, :], rt[:, 6, :, :], ALU.subtract))
            step(V.reciprocal(rt[:, 7, :, :], rt[:, 3, :, :]))
            step(V.tensor_tensor(rt[:, 6, :, :], rt[:, 6, :, :], rt[:, 7, :, :], ALU.mult))
            dve.wait_ge(S["ln_table"], 5)
            step(V.tensor_tensor(rt[:, 6, :, :], rt[:, 6, :, :], rt[:, 4, :, :], ALU.add))
            step(V.scalar_tensor_tensor(rt[:, 6, :, :], rt[:, 5, :, :], 0.0, rt[:, 6, :, :], ALU.max, ALU.add))
            step(V.tensor_tensor(rt[:, 6, :, :], rt[:, 6, :, :], bm(rt[:, 9, 0, :], NT), ALU.mult))
            step(V.tensor_scalar(rt[:, 6, :, :], rt[:, 6, :, :], -1.0, G_FLOOR, ALU.mult, ALU.max))
            step(V.tensor_scalar(rt[:, 1, :, :], rt[:, 1, :, :], 1.0, None, ALU.add))
            step(V.reciprocal(rt[:, 8, :, :], rt[:, 1, :, :]))
            step(V.tensor_reduce(sp_t[:, 1, :], rt[:, 0, :, 0:E], AX, ALU.add))
            step(V.reciprocal(sp_t[:, 2, :], sp_t[:, 1, :]))
            step(V.tensor_tensor(sc[:, :, :], rt[:, 0, :, 0:E].rearrange("p t e -> p e t"), bm(sp_t[:, 2, :], E), ALU.mult))
            step(V.memset(rk[:, :, :], 0.0))
            for a in range(E):
                for b in range(a + 1, E):
                    step(V.tensor_tensor(t4[:, 0, 0, :], sc[:, a, :], sc[:, b, :], ALU.is_ge))
                    step(V.tensor_tensor(rk[:, b, :], rk[:, b, :], t4[:, 0, 0, :], ALU.add))
                    step(V.scalar_tensor_tensor(rk[:, a, :], rk[:, a, :], 1.0, t4[:, 0, 0, :], ALU.add, ALU.subtract))
            V.tensor_scalar(sel[:, :, :], rk[:, :, :], 1.5, None, ALU.is_lt).then_inc(S["gate_step"], 1)
            dve.wait_ge(S["gate_step"], 1)
            dve.wait_ge(S["pos_psum"], 1)
            step(V.tensor_copy(tots[:, :], bank[0:P, 1, 64:64 + E * NT]))
            step(V.tensor_tensor_scan(offs[:, :], one40[:, :], tots[:, :], 0.0, ALU.mult, ALU.add))
            step(V.tensor_tensor(offs[:, :], offs[:, :], tots[:, :], ALU.subtract))
            pf = pos[:, :, :].rearrange("p e t -> p (e t)")
            step(V.tensor_tensor(pf, bank[0:P, 1, 0:E * NT], offs[:, :], ALU.add))
            of = offs[:, :].rearrange("p (e t) -> p e t", e=E)[:, :, 0:1].broadcast_to([P, E, NT])
            step(V.tensor_tensor(fst[:, :, :], pos[:, :, :], of, ALU.is_equal))
            for c in range(2):
                step(V.tensor_scalar(t4[:, 0], rk[:, :, :], float(c), None, ALU.is_equal))
                for dst, src in ((c_pos, pos), (c_w, sc), (c_f, fst)):
                    step(V.tensor_tensor(t4[:, 1], t4[:, 0], src[:, :, :], ALU.mult))
                    step(V.tensor_reduce(dst[:, c, :], t4[:, 1].rearrange("p e t -> p t e"), AX, ALU.add))
            step(V.tensor_copy(posi[:, :, :], c_pos[:, :, :]))
            step(V.tensor_tensor(sp_t[:, 3, :], c_w[:, 0, :], c_w[:, 1, :], ALU.add))
            step(V.reciprocal(sp_t[:, 3, :], sp_t[:, 3, :]))
            step(V.tensor_tensor(c_w[:, :, :], c_w[:, :, :], bm(sp_t[:, 3, :], 2), ALU.mult))
            step(V.tensor_scalar(c_m[:, :, :], c_w[:, :, :], 0.0, None, ALU.is_gt))
            step(V.tensor_scalar(c_f[:, :, :], c_f[:, :, :], G_FLOOR, None, ALU.mult))
            for c in range(2):
                step(V.tensor_tensor(gb[:, :, c, 0:H], rt[:, 6, :, :], bc(c_m[:, c, :], H), ALU.mult))
                step(V.tensor_tensor(gb[:, :, c, 0:H], gb[:, :, c, 0:H], bc(c_f[:, c, :], H), ALU.add))
                step(V.tensor_tensor(gb[:, :, c, H:2 * H], rt[:, 8, :, :], bc(c_m[:, c, :], H), ALU.mult))
            V.tensor_copy(c_t[:, :, :], c_w[:, :, :]).then_inc(S["pos_ready"], 1)
            for t in range(NT):
                b = t % 2
                dve.wait_ge(S["f_act"], 4 * t + 2)
                qk = rows[:, b, 0:2 * D]
                sq = qT[0:P, 0:2, 0:D]
                if t >= 1:
                    dve.wait_ge(S["ss_done"], t)
                step(V.tensor_tensor(sq, qk.rearrange("p (a n) -> p a n", a=2), qk.rearrange("p (a n) -> p a n", a=2), ALU.mult))
                step(V.tensor_reduce(nrm[:, b, :].rearrange("p (a h) -> p a h", a=2), sq.rearrange("p a (h e) -> p a h e", e=DH), AX, ALU.add))
                V.tensor_scalar(nrm[:, b, :], nrm[:, b, :], 1e-6, None, ALU.add).then_inc(S["ss_done"], 1)
                dve.wait_ge(S["rn_done"], t + 1)
                V.scalar_tensor_tensor(tt3(qk[:, 0:D]), tt3(qk[:, 0:D]), DH ** -0.5, bc(nrm[:, b, 0:H], DH), ALU.mult, ALU.mult)
                dve.wait_ge(S["f_act"], 4 * t + 3)
                V.tensor_tensor(tt3(qk[:, D:2 * D]), tt3(qk[:, D:2 * D]), bc(nrm[:, b, H:2 * H], DH), ALU.mult).then_inc(S["rows_done"], 1)
            dve.wait_ge(S["gb_loaded"], 16)
            step(V.tensor_copy(gs[:, :, :], gbs[:, :, 0:H]))
            V.tensor_copy(bet[:, :, :], gbs[:, :, H:2 * H]).then_inc(S["gb_ready"], 1)
            dve.wait_ge(S["gb_ready"], 1)
            dve.wait_ge(S["decay_exp"], 1)
            V.tensor_tensor(bdec[:, :, :], bdec[:, :, :], bet[:, :, :], ALU.mult).then_inc(S["scal_done"], 1)
            def chunk_step(c):
                for h in range(2):
                    dve.wait_ge(HS["dt_done"][h], c + 1)
                    dve.wait_ge(HS["bm_built"][h], c + 1)
                    V.tensor_tensor(cmat(DT, h), cmat(DT, h), cmat(BM, h), ALU.mult).then_inc(S["db_raw"], 1)
                for h in range(2):
                    dve.wait_ge(S["db_raw"], c * 2 + (h + 1))
                    dve.wait_ge(S["kk_psum"], c * 2 + (h + 1))
                    V.tensor_tensor(cmat(AT, h), bank[0:P, 4 + h, 0:CW].rearrange("p (h i) -> p h i", h=HH), cmat(DT, h), ALU.mult).then_inc(HS["at_raw"][h], 1)
                for h in range(2):
                    dve.wait_ge(HS["kq_psum"][h], c + 1)
                    prior(dve, HS["o_psum"][h], c)
                    V.tensor_tensor(cmat(PT, h), bank[0:P, h, 0:CW].rearrange("p (h i) -> p h i", h=HH), cmat(DT, h), ALU.mult).then_inc(HS["pt_done"][h], 1)
                for h in range(2):
                    dve.wait_ge(HS["a_psum"][h], c + 1)
                    V.tensor_tensor(cmat16(T16, h), bank[0:P, 2 + h, 0:CW].rearrange("p (h i) -> p h i", h=HH), bm(level_mask(0), HH), ALU.mult).then_inc(HS["m_done"][h], 1)
                pm = lambda n: bank[0:P, n, 0:CW].rearrange("p (h i) -> p h i", h=HH)
                for lv in range(1, LEVELS):
                    for h in range(2):
                        dve.wait_ge(HS["m_psum"][h], c * LEVELS + lv)
                        V.tensor_tensor(cmat16(B16, h), pm(4 + h), bm(level_mask(lv), HH), ALU.mult).then_inc(HS["m_done"][h], 1)
                    dve.wait_ge(HS["t_psum"][1], c * (LEVELS - 1) + lv)
                    V.tensor_copy(cmat(T0, 1) if lv == LEVELS - 1 else cmat16(T16, 1), pm(1)).then_inc(HS["t_done"][1], 1)
                for h in range(2):
                    dve.wait_ge(HS["m_psum"][h], c * LEVELS + LEVELS)
                    V.tensor_tensor(cmat(RES, h), bm(ident[0:P, 0:P], HH), pm(4 + h), ALU.subtract).then_inc(HS["m_done"][h], 1)
                for h in range(2):
                    dve.wait_ge(HS["tt_psum"][h], c * (LEVELS + 1) + LEVELS)
                    V.tensor_tensor(cmat(UU, h), pm(2 + h), cmat(TT, h), ALU.add).then_inc(HS["tt_done"][h], 1)
                dve.wait_ge(S["v_loaded"], c * 16 + 16)
                for h in range(2):
                    gh = chunk(gam, c, h)
                    dve.wait_ge(HS["ks_psum"][h], c + 1)
                    prior(dve, HS["z_psum"][h], c)
                    y = half(tA[0:P, 0, :], h)
                    V.tensor_tensor(tt3(y), tt3(bank[0:P, 4 + h, 0:256]), bc(gh, DH), ALU.mult).then_inc(S["ks_dec"], 1)
                    dve.wait_ge(S["ks_dec"], c * 2 + (h + 1))
                    V.tensor_tensor(y, half(vtile, h), y, ALU.subtract).then_inc(HS["y_ready"][h], 1)
                    og = half(tB[0:P, 0, :], h)
                    V.tensor_tensor(tt3(og), tt3(bank[0:P, 4 + h, 256:512]), bc(gh, DH), ALU.mult).then_inc(HS["og_done"][h], 1)
                for h in range(2):
                    dve.wait_ge(HS["tt_psum"][h], c * (LEVELS + 1) + (LEVELS + 1))
                    V.tensor_tensor(cmat(TT, h), pm(2 + h), cmat(TT, h), ALU.add).then_inc(HS["tt_done"][h], 1)
                dve.wait_ge(S["sdec_done"], c + 1)
                prior(dve, S["o_stored"], c * 16)
                for h in range(2):
                    dve.wait_ge(HS["s_psum"][h], c + 1)
                    V.tensor_tensor(state[:, h * HH:(h + 1) * HH, :], tt3(bank[0:64, 6 + h, 0:256]), sdec[:, h * HH:(h + 1) * HH, :], ALU.add).then_inc(HS["state_done"][h], 1)
                    dve.wait_ge(HS["o_psum"][h], c + 1)
                    dve.wait_ge(HS["og_done"][h], c + 1)
                    V.tensor_tensor(half(ot, h), bank[0:P, 2 + h, 0:256], half(tB[0:P, 0, :], h), ALU.add).then_inc(HS["o_done"][h], 1)

            chunk_step(0)
            with dve.Fori(1, NCH) as c:
                chunk_step(c)
            for t in range(NT):
                b = t % 2
                dve.wait_ge(gathered[t % 2], 32 * (t // 2 + 1))
                r0, r1 = rows[:, b, 0:D], rows[:, b, D:2 * D]
                step(V.tensor_scalar(r0, r0, c_t[:, 0, t:t + 1], None, ALU.mult))
                if t >= 2:
                    dve.wait_ge(S["fT_psum"], t - 1)
                V.scalar_tensor_tensor(tA[0:P, b, :], r1, c_t[:, 1, t:t + 1], r0, ALU.mult, ALU.add).then_inc(S["mixed"], 1)
                dve.wait_ge(S["mixed"], t + 1)
                step(V.tensor_tensor(tB[0:P, b, :], tA[0:P, b, :], tA[0:P, b, :], ALU.mult))
                step(V.tensor_reduce(nrm[:, b, 0:H], tt3(tB[0:P, b, :]), AX, ALU.add))
                V.tensor_scalar(nrm[:, b, 0:H], nrm[:, b, 0:H], 1.0 / DH, 1e-5, ALU.mult, ALU.add).then_inc(S["f_ms"], 1)
                step(V.tensor_tensor(tt3(hs[:, t, :]), tt3(hs[:, t, :]), bm(onorm[:, :], H), ALU.mult))
                dve.wait_ge(S["f_rs"], t + 1)
                step(V.tensor_tensor(tt3(tA[0:P, b, :]), tt3(tA[0:P, b, :]), bc(nrm[:, b, 0:H], DH), ALU.mult))
                V.tensor_tensor(tA[0:P, b, :], tA[0:P, b, :], hs[:, t, :], ALU.mult).then_inc(S["f_gated"], 1)
                if t >= 1:
                    last_sum(dve, V, t - 1)
            last_sum(dve, V, NT - 1)


_SHARED = ("x", "src", "dst")


def kernel(**inputs):
    import concourse.bacc as bacc
    from concourse.bass_utils import run_bass_kernel_spmd

    nc = bacc.Bacc("TRN2", target_bir_lowering=False, num_devices=1)
    a = {k: np.asarray(v) for k, v in inputs.items()}
    for name in ("L0_mix_Wq", "L0_mix_Wk", "L0_mix_Wv", "L0_mix_Wo"):
        a[name] = a[name].T
    a["L0_mix_bq"] = a["L0_mix_bq"].reshape(KC, 128).T
    a["wsmall"] = np.concatenate([a.pop("L0_ffn_Wgate"), a.pop("L0_ffn_Wb"), a.pop("L0_ffn_Wa")], axis=1)
    a.update(consts())
    arrays, d = {}, {}
    for name, v in a.items():
        v = np.ascontiguousarray(v)
        arrays["in_" + name] = v
        d[name] = nc.dram_tensor("in_" + name, v.shape, mybir.dt.from_np(v.dtype), kind="ExternalInput").ap()
    out = nc.dram_tensor("out_0", (N, D), mybir.dt.float32, kind="ExternalOutput").ap()
    gps_layer(nc, d, out)
    r = run_bass_kernel_spmd(nc, [arrays], core_ids=[0])
    return r.results[0]["out_0"]
```

```python
import concourse.bass as bass
from concourse import mybir
from contextlib import ExitStack
import numpy as np

N, D, H, DH = 1250, 512, 8, 64
P = 125
NT = N // P
KC = D // 128
NE = 20000
EPP = NE // P
E = 4
SLOTS = 2 * N
NCH = SLOTS // P
HH = H // 2
CW = HH * P
WB = 3
SC = 18
SW = NT * SC
PLACES = SC * 128
UC = 16
MAXR = -(-NE // PLACES)
ROUND_STEPS = 10
FILLS = 8
OW = 126
LEVELS = 6
QSEG = [(0, 418), (418, 416), (834, 416)]
G_FLOOR = -110.0


def consts():
    i = np.arange(P)
    row, col = i[:, None], i[None, :]
    parts = [row <= col, row > col, row < col]
    for lv in range(LEVELS):
        s = 1 << lv
        off = (row // (2 * s) == col // (2 * s)) & (row // s % 2 == 1) & (col // s % 2 == 0)
        parts.append((row == col).astype(np.float32) - off)
    off = (row // 2 == col // 2) & (row % 2 == 1) & (col % 2 == 0)
    parts.append(((row == col).astype(np.float32) - off).T)
    tri = np.concatenate([np.asarray(p, np.float32) for p in parts], axis=1)
    iota = np.tile(np.arange(N, dtype=np.float16), (128, 1))
    return {"ident": np.eye(128, dtype=np.float32), "tri": np.ascontiguousarray(tri), "iota": iota}


def gps_layer(nc, d, out):
    f32, i32, f16 = mybir.dt.float32, mybir.dt.int32, mybir.dt.float16
    ALU = mybir.AluOpType
    ACT = mybir.ActivationFunctionType
    AX = mybir.AxisListType.X
    ctx = ExitStack()
    with ctx:
        def sb(name, shape, dt=f32):
            return ctx.enter_context(nc.sbuf_tensor(name, shape, dt))

        def sem(name):
            return ctx.enter_context(nc.semaphore(name))

        qkv_slots = nc.dram_tensor("qkv_slots", [SLOTS, 3 * D], f32, kind="Internal").ap()
        gb_slots = nc.dram_tensor("gb_slots", [SLOTS, 2 * H], f32, kind="Internal").ap()
        o_slots = nc.dram_tensor("o_slots", [SLOTS, D], f32, kind="Internal").ap()

        x_all = sb("x_all", [P, NT, D])
        xT = sb("xT", [128, KC, N])
        big = sb("big", [128, NT * N])
        cnt = big[0:P, :].rearrange("p (t n) -> p t n", t=NT)
        qT = big[:, 0:KC * N].rearrange("p (k n) -> p k n", k=KC)
        hs = sb("hs", [P, NT, D])
        W = sb("W", [128, 5, KC, D])
        ident = sb("ident_sb", [128, 128])
        tri = sb("tri_sb", [P, (3 + LEVELS + 1) * P])
        iota = sb("iota_sb", [128, N], f16)
        ones = sb("ones", [128, 128])
        onesq = sb("onesq", [P, P])
        zeros16 = sb("zeros16", [P, 512], f16)
        phalf = sb("phalf", [P, 16 + 64])
        b_k, b_v, b_o = (big[0:P, KC * N + n * D:KC * N + (n + 1) * D] for n in range(3))
        b_g = sb("b_g", [P, D])
        b_q = sb("b_q", [128, KC])
        onorm = sb("onorm", [P, DH])
        alog = sb("alog", [P, H])
        dtb = sb("dtb", [P, H])
        wsm = sb("wsm", [128, KC, E + 2 * H])
        ei = sb("ei", [P, 2, EPP], i32)
        ef = sb("ef", [P, 2, EPP])
        stats = sb("stats", [P, NT, 6])
        mv = sb("mv", [P, NT, 2])
        rstd = sb("rstd", [P, NT])
        xn = sb("xn", [P, 2, D])
        tA = sb("tA", [128, 2, D])
        tB = sb("tB", [128, 2, D])
        tC = sb("tC", [128, 2, D])
        rows_all = sb("rows", [128, 6 * D])
        rows = rows_all[0:P, :].rearrange("p (a n) -> p a n", a=2)
        kvbd = sb("kvbd", [128, KC, 128])
        ksbd = sb("ksbd", [128, KC, 2])
        den = sb("den", [P, 2, H])
        dinv = sb("dinv", [P, NT])
        deg = sb("deg", [P, NT])
        xTf = xT[0:P, :, :].rearrange("p k n -> p (k n)")
        over = xTf[:, 0:11 * EPP].rearrange("p (b j) -> p b j", b=11)
        binm = xTf[:, 11 * EPP:21 * EPP].rearrange("p (b j) -> p b j", b=NT)
        seen = xTf[:, 21 * EPP:31 * EPP].rearrange("p (b j) -> p b j", b=NT)
        tAf = tA[0:P, :, :].rearrange("p a n -> p (a n)")
        e_row, e_col, e_loc, e_dst, e_tile, e_rank = (tAf[:, n * EPP:(n + 1) * EPP] for n in range(6))
        e_all = tAf[:, 0:4 * EPP].rearrange("p (a j) -> p a j", a=4)
        tBf = tB[0:P, :, :].rearrange("p a n -> p (a n)")
        e_int = tBf[:, 0:EPP].bitcast(i32)
        e_q = tBf[:, EPP:2 * EPP]
        e_ok = tBf[:, 600:600 + EPP]
        s_tile = tC[:, 1, 0:4 * SC].rearrange("p (w a j) -> p w a j", w=2, a=2)
        s_cols = tBf[:, 800:800 + 4 * UC].rearrange("p (a j) -> p a j", a=4)
        cnt_pb, off_pb, tot_b = (tBf[:, 400 + 16 * n:400 + 16 * n + NT] for n in range(3))
        over_r = tBf[:, 480:480 + MAXR - 1]
        n_max, n_r = tBf[:, 500:501], tBf[:, 502:503]
        rounds = sb("rounds", [P, 1], i32)
        srt = tC[:, 0, 0:2 * SW].rearrange("p (a n) -> p a n", a=2)
        rowsf = rows_all[:, :].bitcast(f16)
        oh_row = rowsf[0:P, 0:2 * 128].rearrange("p (u n) -> p u n", u=2)
        oh_col = rowsf[0:P, 256:256 + 4 * SW].rearrange("p (u n) -> p u n", u=2)
        Wf = W[:, :, :, :].rearrange("p w k n -> p (w k n)").bitcast(f16)
        oh_src = Wf[:, 0:WB * OW].rearrange("p (u n) -> p u n", u=WB)
        oh_dst = Wf[:, WB * OW:WB * (OW + N)].rearrange("p (u n) -> p u n", u=WB)
        TCOLS = ((0, 500), (500, 500), (1000, 250))

        LE, GT, LT = tri[:, 0:P], tri[:, P:2 * P], tri[:, 2 * P:3 * P]

        def level_mask(lv):
            return tri[:, (3 + lv) * P:(4 + lv) * P]

        mask1T = level_mask(LEVELS)
        lg = sb("lg", [P, NT, E + 2 * H])
        rt = big[0:P, 20 * CW:20 * CW + 10 * NT * H].rearrange("p (a t h) -> p a t h", a=10, t=NT)
        sc = sb("sc", [P, E, NT])
        rk = sb("rk", [P, E, NT])
        sel = sb("sel", [P, E, NT])
        pos = sb("pos", [P, E, NT])
        tots = sb("tots", [P, E * NT])
        offs = sb("offs", [P, E * NT])
        one40 = sb("one40", [P, E * NT])
        fst = sb("fst", [P, E, NT])
        t4 = sb("t4", [P, 4, E, NT])
        c_pos = sb("c_pos", [P, 2, NT])
        c_w = sb("c_w", [P, 2, NT])
        c_m = sb("c_m", [P, 2, NT])
        c_f = sb("c_f", [P, 2, NT])
        c_t = sb("c_t", [P, 2, NT])
        sp_t = sb("sp_t", [P, 4, NT])
        posi = sb("posi", [P, 2, NT], i32)
        gb = sb("gb", [P, NT, 2, 2 * H])
        nrm = sb("nrm", [P, 2, 2 * H])
        gbs = sb("gbs", [P, NCH, 2 * H])
        gs = sb("gs", [P, NCH, H])
        gam = sb("gam", [P, NCH, H])
        bet = sb("bet", [P, NCH, H])
        bdec = sb("bdec", [P, NCH, H])
        gtot = sb("gtot", [128, NCH, HH])
        state = sb("state", [128, HH, 2 * DH])
        ktile, qtile, vtile = rows[:, 0, 0:D], rows[:, 0, D:2 * D], rows[:, 0, 2 * D:3 * D]
        kdec = rows[:, 1, 0:D]
        zt = rows[:, 1, D:2 * D]
        ot = rows[:, 1, 2 * D:3 * D]
        sdec = sb("sdec", [128, HH, 2 * DH])

        def cmat(n, half, parts=P):
            at = (n * 2 + half) * CW
            return big[0:parts, at:at + CW].rearrange("p (h i) -> p h i", h=HH)

        RG, BM, DT, AT, PT, TT = range(6)
        BS, RES, T0 = 9, 10, 11
        UU = T0

        def cmat16(n, half):
            at = (12 + n // 2 * 2 + half) * CW + n % 2 * CW // 2
            return big[0:P, at:at + CW // 2].bitcast(f16).rearrange("p (h i) -> p h i", h=HH)

        T16, TT16, B16, AT16 = range(4)
        ident16 = big[0:P, 24 * CW:24 * CW + 64].bitcast(f16)[:, 0:P]
        kT2 = big[:, 16 * CW:17 * CW].rearrange("p (j n) -> p j n", j=HH)
        qT2 = big[:, 17 * CW:18 * CW].rearrange("p (j n) -> p j n", j=HH)

        bank = ctx.enter_context(nc.psum_tensor("bank", [128, 8, 512], f32))

        S = {n: sem(n) for n in (
            "x_loaded", "consts_loaded", "edges_loaded", "bias_loaded", "small_loaded",
            "eps_added", "rstd_done", "xn_done", "xT_psum", "xT_done",
            "proj_psum", "proj_sum", "proj_neg", "proj_exp", "proj_done", "kv_psum", "kv_done",
            "h_psum", "h_done", "att_psum", "att_done", "attT_psum", "attT_done",
            "mix_psum", "mix_done", "mix_added", "filled", "onehots_done", "cells_done", "sort_oh", "sort_used", "sorted", "rounds_done", "off_psum", "counts_ready", "round_step", "scalars", "tile_scalars", "at16_done", "bs_raw",
            "kT_psum", "kT_done", "qT_psum", "qT_done", "ks_psum", "y_ready", "og_done", "s_psum", "state_done",
            "onehots_used", "count_done", "loops_added", "deg_psum", "deg_done",
            "dinv_done", "hs_done", "agg_psum", "agg_sum", "agg_done",
            "logit_psum", "gate_step", "gate_exp", "pos_psum", "pos_ready",
            "f_psum", "f_act", "ss_done", "rn_done", "rows_done",
            "gb_loaded", "gb_ready", "decay_psum", "decay_exp", "scal_done", 
            "k_loaded", "q_loaded", "v_loaded", "kdec_done", "sdec_done",
            "o_stored", "mixed", "f_ms", "f_rs", "f_gated", "fT_psum",
            "fT_done", "y_psum", "y_done", "ln_table", "vec_step", "gb_scattered", "vec_order", "ks_dec", "db_raw", "kk_psum", "tt1_done")}
        W_loaded = [sem(f"W{i}_loaded") for i in range(5)]
        HS = {n: [sem(f"{n}{h}") for h in range(2)] for n in (
            "rg_built", "bm_built", "e_psum", "dt_done",
            "kq_psum", "at_raw", "at_done", "pt_done", "a_psum",
            "m_psum", "m_done", "t_psum", "tt_psum", "t_done", "tt_done",
            "z_psum", "z_done", "o_psum", "o_done")}
        scattered, gathered, out_stored = ([sem(f"{n}{b}") for b in range(2)] for n in ("scattered", "gathered", "out_stored"))
        block = ctx.enter_context(nc.Block())

        class Step:
            def __init__(self, eng, s, base=0):
                self.eng, self.s, self.n, self.base = eng, s, 0, base

            def __call__(self, ins):
                self.n += 1
                ins.then_inc(self.s, 1)
                self.eng.wait_ge(self.s, self.base + self.n)

        def tt3(ap):
            return ap.rearrange("p (h e) -> p h e", e=DH)

        def bc(ap, n):
            return ap.unsqueeze(2).broadcast_to([ap.shape[0], ap.shape[1], n])

        def bm(ap, n):
            return ap.unsqueeze(1).broadcast_to([ap.shape[0], n, ap.shape[1]])

        def chunk(ap, c, h):
            return ap[:, bass.ds(c, 1), :].rearrange("p a (j b) -> p b (a j)", b=2)[:, h, :]

        def half(ap, h):
            return ap.rearrange("p (j b e) -> p b j e", b=2, e=DH)[:, h]

        def diag(ap, h):
            q = slice(DH * h, DH * h + DH)
            return ap[q, :, q]

        def prior(eng, s, n):
            if not (isinstance(n, int) and n == 0):
                eng.wait_ge(s, n)

        def settled(eng):
            eng.wait_ge(S["filled"], FILLS)

        def norm_tile(pool, t):
            pool.wait_ge(S["f_ms"], t + 1)
            nc.gpsimd.tensor_tensor(nrm[:, t % 2, 0:H], nrm[:, t % 2, 0:H], phalf[:, 0:H], ALU.pow).then_inc(S["f_rs"], 1)

        def mix_out(dve, V, t):
            dve.wait_ge(S["mix_psum"], t + 1)
            V.tensor_tensor(x_all[:, t, :], bank[0:P, 6 + t % 2, :], x_all[:, t, :], ALU.add).then_inc(S["mix_done"], 1)
            dve.wait_ge(S["mix_done"], t + 1)
            V.tensor_tensor(x_all[:, t, :], x_all[:, t, :], b_o[:, :], ALU.add).then_inc(S["mix_added"], 1)

        def last_sum(dve, V, t):
            dve.wait_ge(S["y_psum"], t + 1)
            if t >= 2:
                dve.wait_ge(out_stored[t % 2], 16 * (t // 2))
            V.tensor_tensor(tC[0:P, t % 2, :], bank[0:P, 6 + t % 2, :], x_all[:, t, :], ALU.add).then_inc(S["y_done"], 1)

        @block.sync
        def _(sp):
            sp.dma_start(x_all[:, :, :], d["x"].rearrange("(t p) d -> p t d", p=P)).then_inc(S["x_loaded"], 16)
            sp.dma_start(ident[:, :], d["ident"]).then_inc(S["consts_loaded"], 16)
            sp.dma_start(tri[:, :], d["tri"]).then_inc(S["consts_loaded"], 16)
            sp.dma_start(iota[:, :], d["iota"]).then_inc(S["consts_loaded"], 16)
            for n, name in enumerate(("L0_mix_Wk", "L0_mix_Wv", "L0_mix_Wq", "L0_mix_Wo", "L0_gnn_W")):
                sp.dma_start(W[:, n], d[name].rearrange("(k p) n -> p k n", p=128)).then_inc(W_loaded[n], 16)
            for buf, name in ((b_k, "L0_mix_bk"), (b_v, "L0_mix_bv"), (b_o, "L0_mix_bo"), (b_g, "L0_gnn_b")):
                sp.dma_start(buf[:, :], d[name].partition_broadcast(P)).then_inc(S["bias_loaded"], 16)
            sp.dma_start(b_q[:, :], d["L0_mix_bq"]).then_inc(S["bias_loaded"], 16)
            for n, name in enumerate(("src", "dst")):
                sp.dma_start(ei[:, n, :], d[name].rearrange("(p j) -> p j", p=P)).then_inc(S["edges_loaded"], 16)
            sp.dma_start(onorm[:, :], d["L0_ffn_o_norm_weight"].partition_broadcast(P)).then_inc(S["small_loaded"], 16)
            sp.dma_start(alog[:, :], d["L0_ffn_A_log"].partition_broadcast(P)).then_inc(S["small_loaded"], 16)
            sp.dma_start(dtb[:, :], d["L0_ffn_dt_bias"].partition_broadcast(P)).then_inc(S["small_loaded"], 16)
            sp.dma_start(wsm[:, :, :], d["wsmall"].rearrange("(k p) n -> p k n", p=128)).then_inc(S["small_loaded"], 16)
            sp.wait_ge(S["counts_ready"], 1)
            for n, name in enumerate(("L0_ffn_Wq", "L0_ffn_Wk", "L0_ffn_Wv", "L0_ffn_Wg", "L0_ffn_Wo")):
                sp.dma_start(W[:, n], d[name].rearrange("(k p) n -> p k n", p=128)).then_inc(W_loaded[n], 16)
            sp.wait_ge(S["gb_scattered"], 16 * 2 * NT)
            sp.dma_start(gbs[:, :, :], gb_slots.rearrange("(c p) n -> p c n", p=P)).then_inc(S["gb_loaded"], 16)
            for b in range(2):
                sp.wait_ge(scattered[b], 16 * NT)
            sp.dma_start(ktile, qkv_slots[0:P, D:2 * D]).then_inc(S["k_loaded"], 16)
            sp.dma_start(qtile, qkv_slots[0:P, 0:D]).then_inc(S["q_loaded"], 16)
            sp.dma_start(vtile, qkv_slots[0:P, 2 * D:3 * D]).then_inc(S["v_loaded"], 16)
            with sp.Fori(1, NCH) as c:
                r0 = c * P
                prior(sp, S["kT_psum"], c)
                prior(sp, S["qT_psum"], c)
                prior(sp, S["kdec_done"], c)
                sp.dma_start(ktile, qkv_slots[bass.ds(r0, P), D:2 * D]).then_inc(S["k_loaded"], 16)
                sp.dma_start(qtile, qkv_slots[bass.ds(r0, P), 0:D]).then_inc(S["q_loaded"], 16)
                prior(sp, S["y_ready"], c)
                sp.dma_start(vtile, qkv_slots[bass.ds(r0, P), 2 * D:3 * D]).then_inc(S["v_loaded"], 16)
                for h in range(2):
                    prior(sp, HS["o_done"][h], c)
                sp.dma_start(o_slots[bass.ds(r0 - P, P), :], ot).then_inc(S["o_stored"], 16)
            for h in range(2):
                sp.wait_ge(HS["o_done"][h], NCH)
            sp.dma_start(o_slots[SLOTS - P:SLOTS, :], ot).then_inc(S["o_stored"], 16)
            for t in range(NT):
                sp.wait_ge(S["y_done"], t + 1)
                sp.dma_start(out[t * P:(t + 1) * P, :], tC[0:P, t % 2, :]).then_inc(out_stored[t % 2], 16)
            for b in range(2):
                sp.wait_ge(out_stored[b], 16 * NT // 2)
            sp.wait_ge(S["o_stored"], 16 * NCH)

        @block.tensor
        def _(pe):
            mm = nc.tensor.matmul
            pe.wait_ge(S["consts_loaded"], 48)
            pe.wait_ge(S["filled"], FILLS)

            def transpose_tiles(src, ready, base, psum_sem, done, banks, at=0):
                for t in range(NT):
                    pe.wait_ge(ready, base + t + 1)
                    if t >= 2 or at:
                        pe.wait_ge(done, at + t - 1)
                    for k in range(KC):
                        last = nc.tensor.transpose(bank[:, banks + t % 2, k * P:(k + 1) * P],
                                                   src(t)[:, k * 128:(k + 1) * 128], ident[0:P, 0:P])
                    last.then_inc(psum_sem, 1)

            def project(dst, t, w):
                for k in range(KC):
                    last = mm(dst, xT[:, k, t * P:(t + 1) * P], W[:, w, k, :], start=(k == 0), stop=(k == KC - 1))
                return last

            transpose_tiles(lambda t: xn[:, t % 2, :], S["xn_done"], 0, S["xT_psum"], S["xT_done"], 6)
            pe.wait_ge(S["xT_done"], NT)
            pe.wait_ge(W_loaded[0], 16)
            pe.wait_ge(W_loaded[1], 16)
            mm(bank[:, 4, :], zeros16[:, 0:128], zeros16[:, :], start=True, stop=True)
            mm(bank[:, 5, :], zeros16[:, 0:128], zeros16[:, :], start=True, stop=True)
            unit = 0

            def kv_sums(t):
                pe.wait_ge(S["proj_done"], t + 1)
                pe.wait_ge(S["vec_step"], t + 1)
                for c in range(KC):
                    mm(bank[:, 4, c * 128:(c + 1) * 128], tC[0:P, t % 2, c * 128:(c + 1) * 128],
                       xn[:, t % 2, c * 128:(c + 1) * 128], start=False, stop=True, skip_group_check=True)
                for c in range(KC):
                    last = mm(bank[:, 5, c:c + 1], tC[0:P, t % 2, c * 128:(c + 1) * 128], ones[0:P, 0:1],
                              start=False, stop=True, skip_group_check=True)
                last.then_inc(S["kv_psum"], 1)

            for t in range(NT):
                if unit >= 2:
                    pe.wait_ge(S["proj_sum"], unit - 1)
                project(bank[0:P, unit % 2, :], t, 0).then_inc(S["proj_psum"], 1)
                if t >= 2:
                    pe.wait_ge(S["vec_step"], t - 1)
                project(bank[0:P, 2 + t % 2, :], t, 1).then_inc(S["h_psum"], 1)
                unit += 1
                if t >= 1:
                    kv_sums(t - 1)
            kv_sums(NT - 1)
            pe.wait_ge(W_loaded[2], 16)
            for c in range(KC):
                for s0, n in QSEG:
                    pe.wait_ge(S["proj_sum"], unit - 1)
                    for k in range(KC):
                        last = mm(bank[:, unit % 2, 0:n], W[:, 2, k, c * 128:(c + 1) * 128], xT[:, k, s0:s0 + n],
                                  start=(k == 0), stop=(k == KC - 1))
                    last.then_inc(S["proj_psum"], 1)
                    unit += 1
            pe.wait_ge(W_loaded[4], 16)
            for t in range(NT):
                if t < 2:
                    pe.wait_ge(S["vec_step"], NT)
                else:
                    pe.wait_ge(S["h_done"], t - 1)
                project(bank[0:P, 2 + t % 2, :], t, 4).then_inc(S["h_psum"], 1)
            pe.wait_ge(S["kv_done"], 4)
            pe.wait_ge(S["proj_done"], unit)
            pe.wait_ge(W_loaded[3], 16)
            for t in range(NT):
                b = t % 2
                if t >= 2:
                    pe.wait_ge(S["att_done"], t - 1)
                for c in range(KC):
                    mm(bank[0:P, b, c * 128:(c + 1) * 128], qT[:, c, t * P:(t + 1) * P], kvbd[:, c, :], start=True, stop=True)
                if t == 0:
                    pe.wait_ge(S["h_done"], NT)
                for c in range(KC):
                    last = mm(bank[0:P, 2 + b, 2 * c:2 * c + 2], qT[:, c, t * P:(t + 1) * P], ksbd[:, c, :], start=True, stop=True)
                last.then_inc(S["att_psum"], 1)
                pe.wait_ge(S["att_done"], t + 1)
                if t >= 2:
                    pe.wait_ge(S["attT_done"], t - 1)
                for k in range(KC):
                    last = nc.tensor.transpose(bank[:, 4 + b, k * P:(k + 1) * P], tA[0:P, b, k * 128:(k + 1) * 128], ident[0:P, 0:P])
                last.then_inc(S["attT_psum"], 1)
                pe.wait_ge(S["attT_done"], t + 1)
                if t >= 2:
                    pe.wait_ge(S["mix_done"], t - 1)
                for k in range(KC):
                    last = mm(bank[0:P, 6 + b, :], tB[:, b, k * P:(k + 1) * P], W[:, 3, k, :], start=(k == 0), stop=(k == KC - 1))
                last.then_inc(S["mix_psum"], 1)
            pe.wait_ge(S["mix_done"], NT)
            pe.wait_ge(S["cells_done"], 1)
            mm(bank[0:P, 6, 0:NT], LT, cnt_pb, start=True, stop=True)
            mm(bank[0:P, 6, 64:64 + NT], onesq[:, :], cnt_pb, start=True, stop=True).then_inc(S["off_psum"], 1)

            def count_round(r):
                mm(bank[:, 5, :], zeros16[:, 0:128], zeros16[:, :], start=True, stop=True)
                with pe.Fori(0, EPP // UC) as i:
                    for u in range(UC):
                        pe.wait_ge(S["sort_oh"], i * UC + (r * EPP + u + 1))
                        mm(bank[:, 5, 0:2 * SW], oh_row[:, u % 2, :], oh_col[:, u % 2, :], start=False, stop=True,
                           skip_group_check=True).then_inc(S["sort_used"], 1)
                with pe.Fori(0, NT // 2) as i:
                    for p in range(2):
                        pe.wait_ge(S["count_done"], i * 2 + (r * NT + p + 1))
                        for j in range(SC):
                            pe.wait_ge(S["onehots_done"], i * (2 * SC) + (r * NT * SC + p * SC + j + 1))
                            for k, (t0, n) in enumerate(TCOLS):
                                last = mm(bank[0:P, 3 * p + k, 0:n], oh_src[:, j % WB, 0:P], oh_dst[:, j % WB, t0:t0 + n],
                                          start=(j == 0), stop=(j == SC - 1))
                            last.then_inc(S["onehots_used"], 1)

            for s, n in ((S["sort_used"], 2), (S["onehots_used"], WB), (S["count_done"], 2)):
                for _ in range(n):
                    mm(bank[:, 7, 0:128], zeros16[:, 0:128], zeros16[:, 0:128], start=True, stop=True).then_inc(s, 1)
            count_round(0)
            pe.wait_ge(S["rounds_done"], 1)
            n_rounds = pe.value_load(rounds[0:1, 0:1], min_val=1, max_val=MAXR)
            with pe.If(n_rounds > 1):
                with pe.Fori(1, n_rounds) as r:
                    pe.wait_ge(S["count_done"], r * NT + 2)
                    count_round(r)
            pe.wait_ge(S["loops_added"], NT)
            for t in range(NT):
                for s in range(NT):
                    last = mm(bank[0:P, 6, t:t + 1], cnt[:, s, t * P:(t + 1) * P], ones[0:P, 0:1], start=(s == 0), stop=(s == NT - 1))
            last.then_inc(S["deg_psum"], 1)
            pe.wait_ge(S["hs_done"], NT)
            for t in range(NT):
                if t >= 2:
                    pe.wait_ge(S["agg_sum"], t - 1)
                for s in range(NT):
                    last = mm(bank[0:P, t % 2, :], cnt[:, s, t * P:(t + 1) * P], hs[:, s, :], start=(s == 0), stop=(s == NT - 1))
                last.then_inc(S["agg_psum"], 1)
            transpose_tiles(lambda t: xn[:, t % 2, :], S["xn_done"], NT, S["xT_psum"], S["xT_done"], 6, at=NT)
            pe.wait_ge(S["xT_done"], 2 * NT)
            pe.wait_ge(S["small_loaded"], 64)
            pe.wait_ge(S["agg_sum"], NT)
            for t in range(NT):
                n = E + 2 * H
                for k in range(KC):
                    last = mm(bank[0:P, 0, t * n:(t + 1) * n], xT[:, k, t * P:(t + 1) * P], wsm[:, k, :],
                              start=(k == 0), stop=(k == KC - 1))
            last.then_inc(S["logit_psum"], 1)
            pe.wait_ge(S["gate_step"], 1)
            mm(bank[0:P, 1, 0:E * NT], LT, sel[:, :, :].rearrange("p e t -> p (e t)"), start=True, stop=True)
            mm(bank[0:P, 1, 64:64 + E * NT], onesq[:, :], sel[:, :, :].rearrange("p e t -> p (e t)"),
               start=True, stop=True).then_inc(S["pos_psum"], 1)
            for w in range(4):
                pe.wait_ge(W_loaded[w], 32)
            for t in range(NT):
                for w in range(4):
                    if t:
                        pe.wait_ge(S["f_act"], 4 * (t - 1) + w + 1)
                    project(bank[0:P, 2 + w, :], t, w).then_inc(S["f_psum"], 1)
            pe.wait_ge(S["gb_ready"], 1)
            g2 = gs[:, :, :].rearrange("p c h -> p (c h)")
            mm(bank[0:P, 6, 0:NCH * H], LE, g2, start=True, stop=True)
            mm(bank[0:P, 6, 160:160 + NCH * H], GT, g2, start=True, stop=True)
            mm(bank[:, 6, 320:320 + NCH * H], ones[0:P, :], g2, start=True, stop=True).then_inc(S["decay_psum"], 1)
            pe.wait_ge(S["decay_exp"], 1)
            pe.wait_ge(S["f_act"], 4 * NT)
            def exponents(n):
                for h in range(2):
                    pe.wait_ge(HS["rg_built"][h], n + 1)
                    mm(bank[0:P, h, 0:CW], GT, cmat(RG, h).rearrange("p h i -> p (h i)"), start=True, stop=True).then_inc(HS["e_psum"][h], 1)

            def feature_major(n):
                settled(pe)
                prior(pe, S["og_done"], n)
                prior(pe, S["y_ready"], n)
                pe.wait_ge(S["k_loaded"], n * 16 + 16)
                for j in range(HH):
                    last = nc.tensor.transpose(bank[:, 4, j * P:(j + 1) * P], ktile[:, j * 128:(j + 1) * 128], ident[0:P, 0:P])
                last.then_inc(S["kT_psum"], 1)
                settled(pe)
                pe.wait_ge(S["q_loaded"], n * 16 + 16)
                for j in range(HH):
                    last = nc.tensor.transpose(bank[:, 5, j * P:(j + 1) * P], qtile[:, j * 128:(j + 1) * 128], ident[0:P, 0:P])
                last.then_inc(S["qT_psum"], 1)

            def chunk_step(c, more=True):
                pe.wait_ge(S["kT_done"], c + 1)
                pe.wait_ge(S["qT_done"], c + 1)
                for h in range(2):
                    for j in range(HH):
                        kj = kT2[DH * h:DH * h + DH, j, :]
                        last = mm(bank[0:P, 4 + h, j * P:(j + 1) * P], kj, kj, start=True, stop=True)
                    last.then_inc(S["kk_psum"], 1)
                prior(pe, S["state_done"], c * 2)
                for h in range(2):
                    for j in range(HH):
                        last = mm(bank[0:P, 6 + h, j * P:(j + 1) * P], kT2[DH * h:DH * h + DH, j, :],
                                  qT2[DH * h:DH * h + DH, j, :], start=True, stop=True)
                    last.then_inc(HS["kq_psum"][h], 1)
                for h in range(2):
                    pe.wait_ge(S["at16_done"], c * 2 + (h + 1))
                    prior(pe, HS["o_done"][h], c)
                    for j in range(HH):
                        last = mm(bank[0:P, 2 + h, j * P:(j + 1) * P], cmat16(AT16, h)[:, j, :], ident16[:, :], start=True, stop=True)
                    last.then_inc(HS["a_psum"][h], 1)
                for lv in range(1, LEVELS):
                    for h in range(2):
                        if lv == 1:
                            pe.wait_ge(HS["m_done"][h], c * (LEVELS + 1) + 1)
                        else:
                            pe.wait_ge(HS["t_done"][h], c * (LEVELS - 1) + (lv - 1))
                        for j in range(HH):
                            last = mm(bank[0:P, 4 + h, j * P:(j + 1) * P], cmat16(AT16, h)[:, j, :], cmat16(T16, h)[:, j, :], start=True, stop=True)
                        last.then_inc(HS["m_psum"][h], 1)
                    for h in range(2):
                        pe.wait_ge(HS["m_done"][h], c * (LEVELS + 1) + (lv + 1))
                        if lv == 1:
                            pe.wait_ge(S["tt1_done"], c * 2 + (h + 1))
                        else:
                            pe.wait_ge(HS["tt_done"][h], c * (LEVELS + 1) + (lv - 1))
                        for j in range(HH):
                            last = mm(bank[0:P, h, j * P:(j + 1) * P], cmat16(TT16, h)[:, j, :], cmat16(B16, h)[:, j, :], start=True, stop=True)
                        last.then_inc(HS["t_psum"][h], 1)
                        for j in range(HH):
                            last = mm(bank[0:P, 2 + h, j * P:(j + 1) * P], cmat16(B16, h)[:, j, :], cmat16(TT16, h)[:, j, :], start=True, stop=True)
                        last.then_inc(HS["tt_psum"][h], 1)
                for h in range(2):
                    pe.wait_ge(HS["t_done"][h], c * (LEVELS - 1) + (LEVELS - 1))
                    pe.wait_ge(HS["at_done"][h], c + 1)
                    for j in range(HH):
                        last = mm(bank[0:P, 4 + h, j * P:(j + 1) * P], cmat(AT, h)[:, j, :], cmat(T0, h)[:, j, :], start=True, stop=True)
                    last.then_inc(HS["m_psum"][h], 1)
                for h in range(2):
                    pe.wait_ge(HS["m_done"][h], c * (LEVELS + 1) + (LEVELS + 1))
                    pe.wait_ge(HS["tt_done"][h], c * (LEVELS + 1) + (LEVELS - 1))
                    for j in range(HH):
                        last = mm(bank[0:P, 2 + h, j * P:(j + 1) * P], cmat(RES, h)[:, j, :], cmat(TT, h)[:, j, :], start=True, stop=True)
                    last.then_inc(HS["tt_psum"][h], 1)
                for j in range(HH):
                    mm(bank[0:P, 4, j * 128:(j + 1) * 128], kT2[:, j, :], state[:, j, :], start=True, stop=True)
                for j in range(HH):
                    last = mm(bank[0:P, 5, j * 128:(j + 1) * 128], qT2[:, j, :], state[:, j, :], start=True, stop=True)
                last.then_inc(S["ks_psum"], 1)
                if more:
                    exponents(c + 1)
                for h in range(2):
                    pe.wait_ge(HS["tt_done"][h], c * (LEVELS + 1) + LEVELS)
                    for j in range(HH):
                        last = mm(bank[0:P, 2 + h, j * P:(j + 1) * P], cmat(RES, h)[:, j, :], cmat(UU, h)[:, j, :], start=True, stop=True)
                    last.then_inc(HS["tt_psum"][h], 1)
                for h in range(2):
                    pe.wait_ge(HS["tt_done"][h], c * (LEVELS + 1) + (LEVELS + 1))
                    pe.wait_ge(S["y_ready"], c + 1)
                    pe.wait_ge(HS["pt_done"][h], c + 1)
                    for j in range(HH):
                        last = mm(bank[0:P, 6 + h, j * DH:(j + 1) * DH], cmat(TT, h)[:, j, :], half(tA[0:P, 0, :], h)[:, j, :], start=True, stop=True)
                    last.then_inc(HS["z_psum"][h], 1)
                if more:
                    feature_major(c + 1)
                pe.wait_ge(S["kdec_done"], c + 1)
                for h in range(2):
                    pe.wait_ge(HS["z_done"][h], c + 1)
                for j in range(HH):
                    q = slice(j * 128, (j + 1) * 128)
                    last = mm(bank[:, 6, q], kdec[:, q], zt[:, q], start=True, stop=True)
                last.then_inc(S["s_psum"], 1)
                for h in range(2):
                    for j in range(HH):
                        last = mm(bank[0:P, 2 + h, j * DH:(j + 1) * DH], cmat(PT, h)[:, j, :], half(zt, h)[:, j, :], start=True, stop=True)
                    last.then_inc(HS["o_psum"][h], 1)

            exponents(0)
            feature_major(0)
            chunk_step(0)
            with pe.Fori(1, NCH - 1) as c:
                chunk_step(c)
            chunk_step(NCH - 1, more=False)
            for h in range(2):
                pe.wait_ge(HS["o_done"][h], NCH)
            pe.wait_ge(S["state_done"], 2 * NCH)
            pe.wait_ge(S["og_done"], NCH)
            pe.wait_ge(W_loaded[4], 32)
            for t in range(NT):
                b = t % 2
                pe.wait_ge(S["f_gated"], t + 1)
                if t >= 2:
                    pe.wait_ge(S["fT_done"], t - 1)
                for k in range(KC):
                    last = nc.tensor.transpose(bank[:, 4 + b, k * P:(k + 1) * P], tA[0:P, b, k * 128:(k + 1) * 128], ident[0:P, 0:P])
                last.then_inc(S["fT_psum"], 1)
                pe.wait_ge(S["fT_done"], t + 1)
                if t >= 2:
                    pe.wait_ge(S["y_done"], t - 1)
                for k in range(KC):
                    last = mm(bank[0:P, 6 + b, :], qT[:, b, k * P:(k + 1) * P], W[:, 4, k, :], start=(k == 0), stop=(k == KC - 1))
                last.then_inc(S["y_psum"], 1)

        @block.scalar
        def _(act):
            A = nc.scalar.activation

            def copy_tiles(at, base):
                for t in range(NT):
                    act.wait_ge(S["xT_psum"], base + t + 1)
                    A(xT[:, :, t * P:(t + 1) * P], bank[:, 6 + t % 2, 0:KC * P].rearrange("p (k n) -> p k n", k=KC),
                      ACT.Copy).then_inc(S["xT_done"], 1)

            copy_tiles(0, 0)
            for u in range(NT):
                act.wait_ge(S["proj_neg"], u + 1)
                A(tB[0:P, u % 2, :], tB[0:P, u % 2, :], ACT.Exp).then_inc(S["proj_exp"], 1)
            for u in range(NT, NT + KC * len(QSEG)):
                n = QSEG[(u - NT) % 3][1]
                act.wait_ge(S["proj_neg"], u + 1)
                A(tB[:, u % 2, 0:n], tB[:, u % 2, 0:n], ACT.Exp).then_inc(S["proj_exp"], 1)
            for t in range(NT):
                act.wait_ge(S["h_psum"], NT + t + 1)
                A(hs[:, t, :], bank[0:P, 2 + t % 2, :], ACT.Copy).then_inc(S["h_done"], 1)
            for t in range(NT):
                act.wait_ge(S["attT_psum"], t + 1)
                if t >= 2:
                    act.wait_ge(S["mix_psum"], t - 1)
                A(tB[:, t % 2, 0:KC * P], bank[:, 4 + t % 2, 0:KC * P], ACT.Copy).then_inc(S["attT_done"], 1)
            for t in range(NT):
                act.wait_ge(S["onehots_used"], WB + (t + 1) * SC)
                for k, (t0, n) in enumerate(TCOLS):
                    last = A(cnt[:, t, t0:t0 + n], bank[0:P, 3 * (t % 2) + k, 0:n], ACT.Copy)
                last.then_inc(S["count_done"], 1)
            copy_tiles(NT, NT)
            act.wait_ge(S["gate_exp"], 1)
            A(rt[:, 0, :, 0:E], rt[:, 0, :, 0:E], ACT.Exp).then_inc(S["ln_table"], 1)
            A(rt[:, 1, :, :], rt[:, 1, :, :], ACT.Exp).then_inc(S["ln_table"], 1)
            A(rt[:, 2, :, :], rt[:, 2, :, :], ACT.Exp).then_inc(S["ln_table"], 1)
            A(rt[:, 9, 0, :], alog[:, :], ACT.Exp).then_inc(S["ln_table"], 1)
            act.wait_ge(S["gate_exp"], 2)
            A(rt[:, 4, :, :], rt[:, 3, :, :], ACT.Ln).then_inc(S["ln_table"], 1)
            for t in range(NT):
                for w in range(4):
                    act.wait_ge(S["f_psum"], 4 * t + w + 1)
                    if w == 0 and t >= 2:
                        act.wait_ge(scattered[t % 2], 32 * (t // 2))
                    dst = hs[:, t, :] if w == 3 else rows[:, t % 2, w * D:(w + 1) * D]
                    A(dst, bank[0:P, 2 + w, :], ACT.Silu).then_inc(S["f_act"], 1)
            act.wait_ge(S["decay_psum"], 1)
            g2 = lambda a: a[:, :, :].rearrange("p c h -> p (c h)")
            A(ident16[:, :], ident[0:P, 0:P], ACT.Copy)
            A(g2(gam), bank[0:P, 6, 0:NCH * H], ACT.Exp)
            A(g2(bdec), bank[0:P, 6, 160:160 + NCH * H], ACT.Exp)
            for h in range(2):
                q = slice(DH * h, DH * h + DH)
                last = A(gtot[q, :, :], bank[q, 6, 320:320 + NCH * H].rearrange("p (c j b) -> p b c j", b=2, j=HH)[:, h], ACT.Exp)
            last.then_inc(S["decay_exp"], 1)
            def decays(n):
                for h in range(2):
                    act.wait_ge(HS["e_psum"][h], n + 1)
                    prior(act, HS["pt_done"][h], n)
                    A(cmat(DT, h).rearrange("p h i -> p (h i)"), bank[0:P, h, 0:CW], ACT.Exp).then_inc(HS["dt_done"][h], 1)

            def feature_major(n):
                flat = lambda a: a.rearrange("p j n -> p (j n)")
                act.wait_ge(S["kT_psum"], n + 1)
                prior(act, S["ks_psum"], n)
                A(flat(kT2), bank[:, 4, 0:CW], ACT.Copy).then_inc(S["kT_done"], 1)
                act.wait_ge(S["qT_psum"], n + 1)
                A(flat(qT2), bank[:, 5, 0:CW], ACT.Copy).then_inc(S["qT_done"], 1)

            def chunk_step(c, more=True):
                for lv in range(1, LEVELS):
                    for h in range(2):
                        act.wait_ge(HS["t_psum"][h], c * (LEVELS - 1) + lv)
                        A(cmat(T0, h) if lv == LEVELS - 1 else cmat16(T16, h),
                          bank[0:P, h, 0:CW].rearrange("p (h i) -> p h i", h=HH), ACT.Copy).then_inc(HS["t_done"][h], 1)
                        act.wait_ge(HS["tt_psum"][h], c * (LEVELS + 1) + lv)
                        A(cmat(TT, h) if lv == LEVELS - 1 else cmat16(TT16, h),
                          bank[0:P, 2 + h, 0:CW].rearrange("p (h i) -> p h i", h=HH), ACT.Copy).then_inc(HS["tt_done"][h], 1)
                if more:
                    decays(c + 1)
                for h in range(2):
                    act.wait_ge(HS["z_psum"][h], c + 1)
                    prior(act, HS["o_psum"][h], c)
                    A(half(zt, h), tt3(bank[0:P, 6 + h, 0:HH * DH]), ACT.Copy).then_inc(HS["z_done"][h], 1)
                if more:
                    feature_major(c + 1)

            decays(0)
            feature_major(0)
            chunk_step(0)
            with act.Fori(1, NCH - 1) as c:
                chunk_step(c)
            chunk_step(NCH - 1, more=False)
            for t in range(NT):
                act.wait_ge(S["fT_psum"], t + 1)
                if t >= 2:
                    act.wait_ge(S["y_psum"], t - 1)
                A(qT[:, t % 2, 0:KC * P], bank[:, 4 + t % 2, 0:KC * P], ACT.Copy).then_inc(S["fT_done"], 1)

        @block.gpsimd
        def _(pool):
            G = nc.gpsimd
            for buf, value in ((ones, 1.0), (onesq, 1.0), (one40, 1.0), (zeros16, 0.0), (phalf, -0.5),
                               (kvbd, 0.0), (ksbd, 0.0), (state, 0.0)):
                G.memset(buf[tuple(slice(None) for _ in buf.shape)], value).then_inc(S["filled"], 1)
            pool.wait_ge(S["filled"], FILLS)

            def rstd_of(n):
                pool.wait_ge(S["eps_added"], n)
                G.tensor_tensor(rstd[:, :], mv[:, :, 1], phalf[:, 0:NT], ALU.pow).then_inc(S["rstd_done"], 1)

            rstd_of(1)
            for u in range(NT):
                pool.wait_ge(S["proj_sum"], u + 1)
                if u >= 2:
                    pool.wait_ge(S["proj_done"], u - 1)
                G.tensor_scalar(tB[0:P, u % 2, :], tA[0:P, u % 2, :], 0.0, None, ALU.min).then_inc(S["proj_neg"], 1)
            for u in range(NT, NT + KC * len(QSEG)):
                n = QSEG[(u - NT) % 3][1]
                pool.wait_ge(S["proj_sum"], u + 1)
                pool.wait_ge(S["proj_done"], u - 1)
                G.tensor_scalar(tB[:, u % 2, 0:n], tA[:, u % 2, 0:n], 0.0, None, ALU.min).then_inc(S["proj_neg"], 1)
            pool.wait_ge(S["counts_ready"], 1)
            for t in range(NT):
                v = cnt[:, t, t * P:(t + 1) * P]
                G.tensor_tensor(v, v, ident[0:P, 0:P], ALU.add).then_inc(S["loops_added"], 1)
            pool.wait_ge(S["deg_done"], 1)
            G.tensor_tensor(dinv[:, :], deg[:, :], phalf[:, 0:NT], ALU.pow).then_inc(S["dinv_done"], 1)
            rstd_of(2)
            pool.wait_ge(S["pos_ready"], 1)
            for t in range(NT):
                for c in range(2):
                    G.indirect_dma_start(gb_slots, bass.IndirectOffsetOnAxis(ap=posi[:, c, t:t + 1], axis=0),
                                         gb[:, t, c, :], None).then_inc(S["gb_scattered"], 16)
            for t in range(NT):
                pool.wait_ge(S["ss_done"], t + 1)
                G.tensor_tensor(nrm[:, t % 2, :], nrm[:, t % 2, :], phalf[:, 0:2 * H], ALU.pow).then_inc(S["rn_done"], 1)
                pool.wait_ge(S["rows_done"], t + 1)
                for c in range(2):
                    G.indirect_dma_start(qkv_slots, bass.IndirectOffsetOnAxis(ap=posi[:, c, t:t + 1], axis=0),
                                         rows[:, t % 2, :], None).then_inc(scattered[t % 2], 16)
            pool.wait_ge(S["scal_done"], 1)
            def chunk_step(c):
                for h in range(2):
                    prior(pool, HS["e_psum"][h], c)
                    G.tensor_tensor(cmat(RG, h), bc(chunk(gs, c, h), P), bm(LE, HH), ALU.mult).then_inc(HS["rg_built"][h], 1)
                for h in range(2):
                    prior(pool, HS["at_raw"][h], c)
                    G.tensor_tensor(cmat(BS, h), bc(chunk(bet, c, h), P), bm(LT, HH), ALU.mult).then_inc(HS["bm_built"][h], 1)
                for h in range(2):
                    settled(pool)
                    prior(pool, HS["pt_done"][h], c)
                    G.tensor_tensor(cmat(BM, h), bc(chunk(bet, c, h), P), bm(LE, HH), ALU.mult).then_inc(HS["bm_built"][h], 1)
                pool.wait_ge(S["k_loaded"], c * 16 + 16)
                prior(pool, S["s_psum"], c)
                G.tensor_tensor(tt3(kdec), tt3(ktile), bc(bdec[:, bass.ds(c, 1), :].rearrange("p a h -> p (a h)"), DH), ALU.mult).then_inc(S["kdec_done"], 1)
                settled(pool)
                prior(pool, S["state_done"], c * 2)
                gj = gtot[:, bass.ds(c, 1), :].rearrange("p a j -> p (a j)")
                G.tensor_tensor(sdec[:, :, :], state[:, :, :], bc(gj, 2 * DH), ALU.mult).then_inc(S["sdec_done"], 1)
                for h in range(2):
                    pool.wait_ge(S["at16_done"], c * 2 + (h + 1))
                    G.tensor_tensor(cmat16(TT16, h), cmat16(AT16, h), bm(mask1T, HH), ALU.mult).then_inc(S["tt1_done"], 1)
                for h in range(2):
                    G.tensor_tensor(cmat(AT, h), cmat(AT, h), bm(ident[0:P, 0:P], HH), ALU.add).then_inc(HS["at_done"][h], 1)

            chunk_step(0)
            with pool.Fori(1, NCH) as c:
                chunk_step(c)
            pool.wait_ge(S["o_stored"], 16 * NCH)
            for t in range(NT):
                if t >= 2:
                    pool.wait_ge(S["mixed"], t - 1)
                for c in range(2):
                    G.indirect_dma_start(rows[:, t % 2, c * D:(c + 1) * D], None, o_slots,
                                         bass.IndirectOffsetOnAxis(ap=posi[:, c, t:t + 1], axis=0)).then_inc(gathered[t % 2], 16)
                if t >= 1:
                    norm_tile(pool, t - 1)
            norm_tile(pool, NT - 1)

        @block.vector
        def _(dve):
            V = nc.vector
            step = Step(dve, S["vec_order"])

            def layer_norm(n, psum_base):
                for t in range(NT):
                    if n:
                        dve.wait_ge(S["agg_done"], t + 1)
                    step(V.bn_stats(stats[:, t, :], x_all[:, t, :]))
                for t in range(NT):
                    step(V.bn_aggr(mv[:, t, :], stats[:, t, :]))
                V.tensor_scalar(mv[:, :, 1], mv[:, :, 1], 1e-5, None, ALU.add).then_inc(S["eps_added"], 1)
                dve.wait_ge(S["rstd_done"], n + 1)
                for t in range(NT):
                    if t >= 2 or n:
                        dve.wait_ge(S["xT_psum"], n * NT + t - 1)
                    V.tensor_scalar(xn[:, t % 2, :], x_all[:, t, :], mv[:, t, 0:1], rstd[:, t:t + 1],
                                    ALU.subtract, ALU.mult).then_inc(S["xn_done"], 1)

            dve.wait_ge(S["x_loaded"], 16)
            layer_norm(0, 0)
            dve.wait_ge(S["bias_loaded"], 80)

            def finish(u, rowsn, n, dst):
                dve.wait_ge(S["proj_exp"], u + 1)
                V.scalar_tensor_tensor(dst, tA[0:rowsn, u % 2, 0:n], 0.0, tB[0:rowsn, u % 2, 0:n],
                                       ALU.max, ALU.add).then_inc(S["proj_done"], 1)

            for t in range(NT):
                dve.wait_ge(S["proj_psum"], t + 1)
                V.tensor_tensor(tA[0:P, t % 2, :], bank[0:P, t % 2, :], b_k[:, :], ALU.add).then_inc(S["proj_sum"], 1)
                dve.wait_ge(S["h_psum"], t + 1)
                if t >= 2:
                    dve.wait_ge(S["kv_psum"], t - 1)
                elif t == 0:
                    dve.wait_ge(S["xT_psum"], NT)
                V.tensor_tensor(xn[:, t % 2, :], bank[0:P, 2 + t % 2, :], b_v[:, :], ALU.add).then_inc(S["vec_step"], 1)
                finish(t, P, D, tC[0:P, t % 2, :])
            dve.wait_ge(S["kv_psum"], NT)
            dve.wait_ge(S["filled"], FILLS)
            for a in range(2):
                q = slice(64 * a, 64 * a + 64)
                V.tensor_copy(kvbd[q, :, q], bank[q, 4, :].rearrange("p (c n) -> p c n", c=KC)[:, :, q]).then_inc(S["kv_done"], 1)
                V.tensor_copy(ksbd[q, :, a:a + 1], bank[q, 5, 0:KC].unsqueeze(2)).then_inc(S["kv_done"], 1)
            u = NT
            for c in range(KC):
                for s0, n in QSEG:
                    dve.wait_ge(S["proj_psum"], u + 1)
                    dve.wait_ge(S["proj_done"], u - 1)
                    V.tensor_scalar(tA[:, u % 2, 0:n], bank[:, u % 2, 0:n], b_q[:, c:c + 1], None, ALU.add).then_inc(S["proj_sum"], 1)
                    if u > NT:
                        finish(u - 1, 128, prev[1], prev[0])
                    prev = (qT[:, c, s0:s0 + n], n)
                    u += 1
            finish(u - 1, 128, prev[1], prev[0])
            for t in range(NT):
                b = t % 2
                dve.wait_ge(S["att_psum"], t + 1)
                step(V.tensor_scalar(den[:, b, :], bank[0:P, 2 + b, 0:H], 1e-6, None, ALU.add))
                step(V.reciprocal(den[:, b, :], den[:, b, :]))
                if t >= 2:
                    dve.wait_ge(S["attT_psum"], t - 1)
                elif t == 0:
                    dve.wait_ge(S["proj_done"], u)
                V.tensor_tensor(tt3(tA[0:P, b, :]), tt3(bank[0:P, b, :]), bc(den[:, b, :], DH), ALU.mult).then_inc(S["att_done"], 1)
                if t >= 1:
                    mix_out(dve, V, t - 1)
            mix_out(dve, V, NT - 1)
            dve.wait_ge(S["edges_loaded"], 32)
            dve.wait_ge(S["attT_psum"], NT)
            dve.wait_ge(S["mix_psum"], NT)
            dve.wait_ge(S["h_psum"], 2 * NT)
            step(V.tensor_copy(ef[:, :, :], ei[:, :, :]))
            for b in range(NT + 1):
                step(V.tensor_scalar(over[:, b, :], ef[:, 0, :], float(P * b), None, ALU.is_ge))
            step(V.tensor_tensor(binm[:, :, :], over[:, 0:NT, :], over[:, 1:NT + 1, :], ALU.subtract))
            step(V.tensor_reduce(e_tile, over[:, 1:NT + 1, :].rearrange("p b j -> p j b"), AX, ALU.add))
            step(V.scalar_tensor_tensor(e_loc, e_tile, float(-P), ef[:, 0, :], ALU.mult, ALU.add))
            step(V.tensor_scalar(e_loc, e_loc, 1.0, None, ALU.add))
            step(V.tensor_copy(e_dst, ef[:, 1, :]))
            step(V.memset(over[:, 0:NT, :], 1.0))
            step(V.memset(over[:, 0:NT, 0:1], 0.0))
            flat = lambda a: a.rearrange("p b j -> p (b j)")
            step(V.tensor_tensor_scan(flat(seen), flat(over[:, 0:NT, :]), flat(binm), 0.0, ALU.mult, ALU.add))
            V.tensor_copy(cnt_pb, seen[:, :, EPP - 1]).then_inc(S["cells_done"], 1)
            dve.wait_ge(S["off_psum"], 1)
            step(V.tensor_copy(off_pb, bank[0:P, 6, 0:NT]))
            step(V.tensor_copy(tot_b, bank[0:P, 6, 64:64 + NT]))
            step(V.tensor_reduce(n_max, tot_b, AX, ALU.max))
            step(V.tensor_scalar(over_r, iota[0:P, 1:MAXR], float(PLACES), n_max, ALU.mult, ALU.is_lt))
            step(V.tensor_reduce(n_r, over_r, AX, ALU.add))
            V.tensor_scalar(rounds[:, :], n_r, 1.0, None, ALU.add).then_inc(S["rounds_done"], 1)
            step(V.tensor_tensor(seen[:, :, :], seen[:, :, :], bc(off_pb, EPP), ALU.add))
            step(V.tensor_tensor(seen[:, :, :], seen[:, :, :], binm[:, :, :], ALU.mult))
            step(V.tensor_reduce(e_rank, seen[:, :, :].rearrange("p b j -> p j b"), AX, ALU.add))
            step(V.tensor_scalar(e_rank, e_rank, -1.0, None, ALU.add))

            def count_round(r):
                s2 = Step(dve, S["round_step"], r * ROUND_STEPS)
                s2(V.tensor_copy(e_int, e_rank))
                s2(V.tensor_scalar(e_int, e_int, 7, None, ALU.arith_shift_right))
                s2(V.tensor_copy(e_q, e_int))
                s2(V.scalar_tensor_tensor(e_row, e_q, -128.0, e_rank, ALU.mult, ALU.add))
                s2(V.tensor_scalar(e_ok, e_rank, 0.0, None, ALU.is_ge))
                s2(V.scalar_tensor_tensor(e_ok, e_rank, float(PLACES), e_ok, ALU.is_lt, ALU.mult))
                s2(V.scalar_tensor_tensor(e_col, e_tile, float(SC), e_q, ALU.mult, ALU.add))
                s2(V.scalar_tensor_tensor(e_col, e_col, 1.0, e_ok, ALU.add, ALU.mult))
                s2(V.tensor_scalar(e_col, e_col, -1.0, None, ALU.add))
                V.tensor_scalar(e_rank, e_rank, float(-PLACES), None, ALU.add).then_inc(S["round_step"], 1)
                with dve.Fori(0, EPP // UC) as i:
                    settled(dve)
                    dve.wait_ge(S["round_step"], r * ROUND_STEPS + ROUND_STEPS)
                    dve.wait_ge(S["sort_used"], i * UC + (r * EPP + 2))
                    V.tensor_copy(s_cols[:, :, :], e_all[:, :, bass.ds(i * UC, UC)]).then_inc(S["scalars"], 1)
                    dve.wait_ge(S["scalars"], i + (r * (EPP // UC) + 1))
                    for u in range(UC):
                        w = u % 2
                        dve.wait_ge(S["sort_used"], i * UC + (r * EPP + u + 1))
                        V.tensor_scalar(oh_row[:, w, :], iota[0:P, 0:128], s_cols[:, 0, u:u + 1], None, ALU.is_equal)
                        for a in range(2):
                            last = V.tensor_scalar(oh_col[:, w, a * SW:(a + 1) * SW], iota[0:P, 0:SW], s_cols[:, 1, u:u + 1],
                                                   s_cols[:, 2 + a, u:u + 1], ALU.is_equal, ALU.mult)
                        last.then_inc(S["sort_oh"], 1)
                dve.wait_ge(S["sort_used"], r * EPP + (EPP + 2))
                V.tensor_scalar(srt[:, 0, :], bank[:, 5, 0:SW], -1.0, None, ALU.add).then_inc(S["sorted"], 1)
                V.tensor_copy(srt[:, 1, :], bank[:, 5, SW:2 * SW]).then_inc(S["sorted"], 1)
                with dve.Fori(0, NT // 2) as i:
                    for p in range(2):
                        settled(dve)
                        dve.wait_ge(S["sorted"], r * 2 + 2)
                        dve.wait_ge(S["onehots_used"], i * (2 * SC) + (r * NT * SC + p * SC + 1))
                        V.tensor_copy(s_tile[:, p], srt[:, :, bass.ds(i * (2 * SC) + p * SC, SC)]).then_inc(S["tile_scalars"], 1)
                        dve.wait_ge(S["tile_scalars"], i * 2 + (r * NT + p + 1))
                        for j in range(SC):
                            dve.wait_ge(S["onehots_used"], i * (2 * SC) + (r * NT * SC + p * SC + j + 1))
                            V.tensor_scalar(oh_src[:, j % WB, :], iota[:, 0:OW], s_tile[:, p, 0, j:j + 1], None, ALU.is_equal)
                            V.tensor_scalar(oh_dst[:, j % WB, :], iota[:, :], s_tile[:, p, 1, j:j + 1],
                                            None, ALU.is_equal).then_inc(S["onehots_done"], 1)
                        if not (isinstance(r, int) and r == 0):
                            settled(dve)
                            dve.wait_ge(S["onehots_used"], i * (2 * SC) + (r * NT * SC + (p + 1) * SC + WB))
                            for k, (t0, n) in enumerate(TCOLS):
                                cq = cnt[:, bass.ds(i * 2 + p, 1), t0:t0 + n].rearrange("p a n -> p (a n)")
                                last = V.tensor_tensor(cq, bank[0:P, 3 * p + k, 0:n], cq, ALU.add)
                            last.then_inc(S["count_done"], 1)

            count_round(0)
            dve.wait_ge(S["count_done"], NT + 2)
            dve.wait_ge(S["rounds_done"], 1)
            n_rounds = dve.value_load(rounds[0:1, 0:1], min_val=1, max_val=MAXR)
            with dve.If(n_rounds > 1):
                with dve.Fori(1, n_rounds) as r:
                    count_round(r)
            V.tensor_copy(n_r, n_max).then_inc(S["counts_ready"], 1)
            dve.wait_ge(S["deg_psum"], 1)
            V.tensor_copy(deg[:, :], bank[0:P, 6, 0:NT]).then_inc(S["deg_done"], 1)
            dve.wait_ge(S["dinv_done"], 1)
            for t in range(NT):
                if t == 0:
                    dve.wait_ge(S["h_done"], NT)
                V.tensor_scalar(hs[:, t, :], hs[:, t, :], dinv[:, t:t + 1], None, ALU.mult).then_inc(S["hs_done"], 1)
            for t in range(NT):
                b = t % 2
                dve.wait_ge(S["agg_psum"], t + 1)
                V.scalar_tensor_tensor(tA[0:P, b, :], bank[0:P, b, :], dinv[:, t:t + 1], b_g[:, :],
                                       ALU.mult, ALU.add).then_inc(S["agg_sum"], 1)
                dve.wait_ge(S["agg_sum"], t + 1)
                V.scalar_tensor_tensor(x_all[:, t, :], tA[0:P, b, :], 0.0, x_all[:, t, :],
                                       ALU.max, ALU.add).then_inc(S["agg_done"], 1)
            layer_norm(1, 0)
            dve.wait_ge(S["logit_psum"], 1)
            step(V.tensor_copy(lg[:, :, :], bank[0:P, 0, 0:NT * 20].rearrange("p (t n) -> p t n", t=NT)))
            step(V.tensor_reduce(sp_t[:, 0, :], lg[:, :, 0:E], AX, ALU.max))
            step(V.tensor_tensor(rt[:, 0, :, 0:E], lg[:, :, 0:E], bc(sp_t[:, 0, :], E), ALU.subtract))
            step(V.tensor_scalar(rt[:, 1, :, :], lg[:, :, E:E + H], -1.0, None, ALU.mult))
            step(V.tensor_tensor(rt[:, 5, :, :], lg[:, :, E + H:E + 2 * H], bm(dtb[:, :], NT), ALU.add))
            step(V.tensor_scalar(rt[:, 6, :, :], rt[:, 5, :, :], -1.0, None, ALU.mult))
            V.tensor_tensor(rt[:, 2, :, :], rt[:, 5, :, :], rt[:, 6, :, :], ALU.min).then_inc(S["gate_exp"], 1)
            dve.wait_ge(S["ln_table"], 4)
            V.tensor_scalar(rt[:, 3, :, :], rt[:, 2, :, :], 1.0, None, ALU.add).then_inc(S["gate_exp"], 1)
            dve.wait_ge(S["gate_exp"], 2)
            step(V.tensor_scalar(rt[:, 6, :, :], rt[:, 3, :, :], -1.0, None, ALU.add))
            step(V.tensor_tensor(rt[:, 6, :, :], rt[:, 2, :, :], rt[:, 6, :, :], ALU.subtract))
            step(V.reciprocal(rt[:, 7, :, :], rt[:, 3, :, :]))
            step(V.tensor_tensor(rt[:, 6, :, :], rt[:, 6, :, :], rt[:, 7, :, :], ALU.mult))
            dve.wait_ge(S["ln_table"], 5)
            step(V.tensor_tensor(rt[:, 6, :, :], rt[:, 6, :, :], rt[:, 4, :, :], ALU.add))
            step(V.scalar_tensor_tensor(rt[:, 6, :, :], rt[:, 5, :, :], 0.0, rt[:, 6, :, :], ALU.max, ALU.add))
            step(V.tensor_tensor(rt[:, 6, :, :], rt[:, 6, :, :], bm(rt[:, 9, 0, :], NT), ALU.mult))
            step(V.tensor_scalar(rt[:, 6, :, :], rt[:, 6, :, :], -1.0, G_FLOOR, ALU.mult, ALU.max))
            step(V.tensor_scalar(rt[:, 1, :, :], rt[:, 1, :, :], 1.0, None, ALU.add))
            step(V.reciprocal(rt[:, 8, :, :], rt[:, 1, :, :]))
            step(V.tensor_reduce(sp_t[:, 1, :], rt[:, 0, :, 0:E], AX, ALU.add))
            step(V.reciprocal(sp_t[:, 2, :], sp_t[:, 1, :]))
            step(V.tensor_tensor(sc[:, :, :], rt[:, 0, :, 0:E].rearrange("p t e -> p e t"), bm(sp_t[:, 2, :], E), ALU.mult))
            step(V.memset(rk[:, :, :], 0.0))
            for a in range(E):
                for b in range(a + 1, E):
                    step(V.tensor_tensor(t4[:, 0, 0, :], sc[:, a, :], sc[:, b, :], ALU.is_ge))
                    step(V.tensor_tensor(rk[:, b, :], rk[:, b, :], t4[:, 0, 0, :], ALU.add))
                    step(V.scalar_tensor_tensor(rk[:, a, :], rk[:, a, :], 1.0, t4[:, 0, 0, :], ALU.add, ALU.subtract))
            V.tensor_scalar(sel[:, :, :], rk[:, :, :], 1.5, None, ALU.is_lt).then_inc(S["gate_step"], 1)
            dve.wait_ge(S["gate_step"], 1)
            dve.wait_ge(S["pos_psum"], 1)
            step(V.tensor_copy(tots[:, :], bank[0:P, 1, 64:64 + E * NT]))
            step(V.tensor_tensor_scan(offs[:, :], one40[:, :], tots[:, :], 0.0, ALU.mult, ALU.add))
            step(V.tensor_tensor(offs[:, :], offs[:, :], tots[:, :], ALU.subtract))
            pf = pos[:, :, :].rearrange("p e t -> p (e t)")
            step(V.tensor_tensor(pf, bank[0:P, 1, 0:E * NT], offs[:, :], ALU.add))
            of = offs[:, :].rearrange("p (e t) -> p e t", e=E)[:, :, 0:1].broadcast_to([P, E, NT])
            step(V.tensor_tensor(fst[:, :, :], pos[:, :, :], of, ALU.is_equal))
            for c in range(2):
                step(V.tensor_scalar(t4[:, 0], rk[:, :, :], float(c), None, ALU.is_equal))
                for dst, src in ((c_pos, pos), (c_w, sc), (c_f, fst)):
                    step(V.tensor_tensor(t4[:, 1], t4[:, 0], src[:, :, :], ALU.mult))
                    step(V.tensor_reduce(dst[:, c, :], t4[:, 1].rearrange("p e t -> p t e"), AX, ALU.add))
            step(V.tensor_copy(posi[:, :, :], c_pos[:, :, :]))
            step(V.tensor_tensor(sp_t[:, 3, :], c_w[:, 0, :], c_w[:, 1, :], ALU.add))
            step(V.reciprocal(sp_t[:, 3, :], sp_t[:, 3, :]))
            step(V.tensor_tensor(c_w[:, :, :], c_w[:, :, :], bm(sp_t[:, 3, :], 2), ALU.mult))
            step(V.tensor_scalar(c_m[:, :, :], c_w[:, :, :], 0.0, None, ALU.is_gt))
            step(V.tensor_scalar(c_f[:, :, :], c_f[:, :, :], G_FLOOR, None, ALU.mult))
            for c in range(2):
                step(V.tensor_tensor(gb[:, :, c, 0:H], rt[:, 6, :, :], bc(c_m[:, c, :], H), ALU.mult))
                step(V.tensor_tensor(gb[:, :, c, 0:H], gb[:, :, c, 0:H], bc(c_f[:, c, :], H), ALU.add))
                step(V.tensor_tensor(gb[:, :, c, H:2 * H], rt[:, 8, :, :], bc(c_m[:, c, :], H), ALU.mult))
            V.tensor_copy(c_t[:, :, :], c_w[:, :, :]).then_inc(S["pos_ready"], 1)
            for t in range(NT):
                b = t % 2
                dve.wait_ge(S["f_act"], 4 * t + 2)
                qk = rows[:, b, 0:2 * D]
                sq = qT[0:P, 0:2, 0:D]
                if t >= 1:
                    dve.wait_ge(S["ss_done"], t)
                step(V.tensor_tensor(sq, qk.rearrange("p (a n) -> p a n", a=2), qk.rearrange("p (a n) -> p a n", a=2), ALU.mult))
                step(V.tensor_reduce(nrm[:, b, :].rearrange("p (a h) -> p a h", a=2), sq.rearrange("p a (h e) -> p a h e", e=DH), AX, ALU.add))
                V.tensor_scalar(nrm[:, b, :], nrm[:, b, :], 1e-6, None, ALU.add).then_inc(S["ss_done"], 1)
                dve.wait_ge(S["rn_done"], t + 1)
                V.scalar_tensor_tensor(tt3(qk[:, 0:D]), tt3(qk[:, 0:D]), DH ** -0.5, bc(nrm[:, b, 0:H], DH), ALU.mult, ALU.mult)
                dve.wait_ge(S["f_act"], 4 * t + 3)
                V.tensor_tensor(tt3(qk[:, D:2 * D]), tt3(qk[:, D:2 * D]), bc(nrm[:, b, H:2 * H], DH), ALU.mult).then_inc(S["rows_done"], 1)
            dve.wait_ge(S["gb_loaded"], 16)
            step(V.tensor_copy(gs[:, :, :], gbs[:, :, 0:H]))
            V.tensor_copy(bet[:, :, :], gbs[:, :, H:2 * H]).then_inc(S["gb_ready"], 1)
            dve.wait_ge(S["gb_ready"], 1)
            dve.wait_ge(S["decay_exp"], 1)
            V.tensor_tensor(bdec[:, :, :], bdec[:, :, :], bet[:, :, :], ALU.mult).then_inc(S["scal_done"], 1)
            pm = lambda n: bank[0:P, n, 0:CW].rearrange("p (h i) -> p h i", h=HH)

            def decay_beta(n):
                for h in range(2):
                    dve.wait_ge(HS["dt_done"][h], n + 1)
                    dve.wait_ge(HS["bm_built"][h], n * 2 + 1)
                    V.tensor_tensor(cmat(BS, h), cmat(DT, h), cmat(BS, h), ALU.mult).then_inc(S["bs_raw"], 1)
                for h in range(2):
                    dve.wait_ge(S["bs_raw"], n * 2 + (h + 1))
                    dve.wait_ge(HS["bm_built"][h], n * 2 + 2)
                    V.tensor_tensor(cmat(DT, h), cmat(DT, h), cmat(BM, h), ALU.mult).then_inc(S["db_raw"], 1)

            def chunk_step(c, more=True):
                for h in range(2):
                    dve.wait_ge(S["bs_raw"], c * 2 + (h + 1))
                    dve.wait_ge(S["kk_psum"], c * 2 + (h + 1))
                    V.tensor_tensor(cmat(AT, h), pm(4 + h), cmat(BS, h), ALU.mult).then_inc(HS["at_raw"][h], 1)
                for h in range(2):
                    dve.wait_ge(HS["at_raw"][h], c + 1)
                    V.tensor_tensor(cmat16(AT16, h), cmat(AT, h), bm(ident[0:P, 0:P], HH), ALU.add).then_inc(S["at16_done"], 1)
                for h in range(2):
                    dve.wait_ge(HS["a_psum"][h], c + 1)
                    V.tensor_tensor(cmat16(T16, h), pm(2 + h), bm(level_mask(0), HH), ALU.mult).then_inc(HS["m_done"][h], 1)
                for lv in range(1, LEVELS):
                    for h in range(2):
                        dve.wait_ge(HS["m_psum"][h], c * LEVELS + lv)
                        V.tensor_tensor(cmat16(B16, h), pm(4 + h), bm(level_mask(lv), HH), ALU.mult).then_inc(HS["m_done"][h], 1)
                    if lv <= 2:
                        h = lv - 1
                        dve.wait_ge(S["db_raw"], c * 2 + (h + 1))
                        dve.wait_ge(HS["kq_psum"][h], c + 1)
                        prior(dve, HS["o_psum"][h], c)
                        V.tensor_tensor(cmat(PT, h), pm(6 + h), cmat(DT, h), ALU.mult).then_inc(HS["pt_done"][h], 1)
                for h in range(2):
                    dve.wait_ge(HS["m_psum"][h], c * LEVELS + LEVELS)
                    V.tensor_tensor(cmat(RES, h), bm(ident[0:P, 0:P], HH), pm(4 + h), ALU.subtract).then_inc(HS["m_done"][h], 1)
                for h in range(2):
                    dve.wait_ge(HS["tt_psum"][h], c * (LEVELS + 1) + LEVELS)
                    V.tensor_tensor(cmat(UU, h), pm(2 + h), cmat(TT, h), ALU.add).then_inc(HS["tt_done"][h], 1)
                dve.wait_ge(S["v_loaded"], c * 16 + 16)
                gc = bc(gam[:, bass.ds(c, 1), :].rearrange("p a h -> p (a h)"), DH)
                dve.wait_ge(S["ks_psum"], c + 1)
                for h in range(2):
                    prior(dve, HS["z_psum"][h], c)
                y, og = tA[0:P, 0, :], tB[0:P, 0, :]
                V.tensor_tensor(tt3(y), tt3(bank[0:P, 4, :]), gc, ALU.mult).then_inc(S["ks_dec"], 1)
                V.tensor_tensor(tt3(og), tt3(bank[0:P, 5, :]), gc, ALU.mult).then_inc(S["og_done"], 1)
                dve.wait_ge(S["ks_dec"], c + 1)
                V.tensor_tensor(y, vtile, y, ALU.subtract).then_inc(S["y_ready"], 1)
                for h in range(2):
                    dve.wait_ge(HS["tt_psum"][h], c * (LEVELS + 1) + (LEVELS + 1))
                    V.tensor_tensor(cmat(TT, h), pm(2 + h), cmat(TT, h), ALU.add).then_inc(HS["tt_done"][h], 1)
                if more:
                    decay_beta(c + 1)
                dve.wait_ge(S["sdec_done"], c + 1)
                dve.wait_ge(S["s_psum"], c + 1)
                for h in range(2):
                    V.tensor_tensor(diag(state, h), diag(bank[:, 6, :].rearrange("p (j n) -> p j n", j=HH), h),
                                    diag(sdec, h), ALU.add).then_inc(S["state_done"], 1)
                dve.wait_ge(S["og_done"], c + 1)
                prior(dve, S["o_stored"], c * 16)
                for h in range(2):
                    dve.wait_ge(HS["o_psum"][h], c + 1)
                    V.tensor_tensor(half(ot, h), tt3(bank[0:P, 2 + h, 0:256]), half(tB[0:P, 0, :], h), ALU.add).then_inc(HS["o_done"][h], 1)

            decay_beta(0)
            chunk_step(0)
            with dve.Fori(1, NCH - 1) as c:
                chunk_step(c)
            chunk_step(NCH - 1, more=False)
            for t in range(NT):
                b = t % 2
                dve.wait_ge(gathered[t % 2], 32 * (t // 2 + 1))
                r0, r1 = rows[:, b, 0:D], rows[:, b, D:2 * D]
                step(V.tensor_scalar(r0, r0, c_t[:, 0, t:t + 1], None, ALU.mult))
                if t >= 2:
                    dve.wait_ge(S["fT_psum"], t - 1)
                V.scalar_tensor_tensor(tA[0:P, b, :], r1, c_t[:, 1, t:t + 1], r0, ALU.mult, ALU.add).then_inc(S["mixed"], 1)
                dve.wait_ge(S["mixed"], t + 1)
                step(V.tensor_tensor(tB[0:P, b, :], tA[0:P, b, :], tA[0:P, b, :], ALU.mult))
                step(V.tensor_reduce(nrm[:, b, 0:H], tt3(tB[0:P, b, :]), AX, ALU.add))
                V.tensor_scalar(nrm[:, b, 0:H], nrm[:, b, 0:H], 1.0 / DH, 1e-5, ALU.mult, ALU.add).then_inc(S["f_ms"], 1)
                step(V.tensor_tensor(tt3(hs[:, t, :]), tt3(hs[:, t, :]), bm(onorm[:, :], H), ALU.mult))
                dve.wait_ge(S["f_rs"], t + 1)
                step(V.tensor_tensor(tt3(tA[0:P, b, :]), tt3(tA[0:P, b, :]), bc(nrm[:, b, 0:H], DH), ALU.mult))
                V.tensor_tensor(tA[0:P, b, :], tA[0:P, b, :], hs[:, t, :], ALU.mult).then_inc(S["f_gated"], 1)
                if t >= 1:
                    last_sum(dve, V, t - 1)
            last_sum(dve, V, NT - 1)


_SHARED = ("x", "src", "dst")


def kernel(**inputs):
    import concourse.bacc as bacc
    from concourse.bass_utils import run_bass_kernel_spmd

    nc = bacc.Bacc("TRN2", target_bir_lowering=False, num_devices=1)
    a = {k: np.asarray(v) for k, v in inputs.items()}
    for name in ("L0_mix_Wq", "L0_mix_Wk", "L0_mix_Wv", "L0_mix_Wo"):
        a[name] = a[name].T
    a["L0_mix_bq"] = a["L0_mix_bq"].reshape(KC, 128).T
    a["wsmall"] = np.concatenate([a.pop("L0_ffn_Wgate"), a.pop("L0_ffn_Wb"), a.pop("L0_ffn_Wa")], axis=1)
    a.update(consts())
    arrays, d = {}, {}
    for name, v in a.items():
        v = np.ascontiguousarray(v)
        arrays["in_" + name] = v
        d[name] = nc.dram_tensor("in_" + name, v.shape, mybir.dt.from_np(v.dtype), kind="ExternalInput").ap()
    out = nc.dram_tensor("out_0", (N, D), mybir.dt.float32, kind="ExternalOutput").ap()
    gps_layer(nc, d, out)
    r = run_bass_kernel_spmd(nc, [arrays], core_ids=[0])
    return r.results[0]["out_0"]
```
